# Optimizing a Trainium2 kernel written in Bass

```python
import numpy as np
import jax
import jax.numpy as jnp

def _softmax(x, axis=-1):
    return jax.nn.softmax(x, axis=axis)

def _gelu(x):
    return jax.nn.gelu(x, approximate=True)

def _silu(x):
    return jax.nn.silu(x)

def _sigmoid(x):
    return jax.nn.sigmoid(x)

def _layernorm(x, axis=-1, eps=1e-05):
    m = jnp.mean(x, axis=axis, keepdims=True)
    v = jnp.var(x, axis=axis, keepdims=True)
    return (x - m) / jnp.sqrt(v + eps)

def _scatter_add(tgt, idx, src, axis=0):
    return tgt.at[idx].add(src)

def _segment_sum(src, seg, n):
    return jax.ops.segment_sum(src, seg, n)
kernel_name = 'mk_gnn_ffn_d2_gnn_r8_c04f3a'

def setup_inputs(seed: int=0):
    np.random.seed(seed)
    _w = jnp.asarray

    def _rec_inputs():
        import jax
        import jax.numpy as jnp
        _gk = jax.random.key(seed)
        x = -0.000364 + 1 * jax.random.normal(jax.random.fold_in(_gk, 1), (1250, 768), jnp.float32)
        src = jax.random.randint(jax.random.fold_in(_gk, 2), (20000,), 0, 1250, jnp.int32)
        dst = jax.random.randint(jax.random.fold_in(_gk, 3), (20000,), 0, 1250, jnp.int32)
        _o = jnp.argsort(dst, stable=True)
        src = src[_o]
        dst = dst[_o]
        return (x, src, dst)
    x, src, dst = _rec_inputs()

    def _L0_gnn_setup():
        import jax, jax.numpy as jnp
        import numpy as np
        N_NODES = 2500
        N_EDGES = 12500
        D_IN = 768
        NEG_SLOPE = 0.2

        def _gat_layer(x, W, attn_l, attn_r, bias, src, dst, num_heads, head_dim, use_elu):
            N = x.shape[0]
            z = (x @ W).reshape(N, num_heads, head_dim)
            el = jnp.sum(z * attn_l, axis=-1)
            er = jnp.sum(z * attn_r, axis=-1)
            e = jax.nn.leaky_relu(el[src] + er[dst], NEG_SLOPE)
            m = jax.ops.segment_max(e, dst, num_segments=N)
            ex = jnp.exp(e - m[dst])
            denom = jax.ops.segment_sum(ex, dst, num_segments=N)
            alpha = ex / denom[dst]
            msg = alpha[:, :, None] * z[src]
            out = jax.ops.segment_sum(msg, dst, num_segments=N)
            out = out + z
            out = out + bias.reshape(1, num_heads, head_dim)
            if use_elu:
                out = jax.nn.elu(out)
            return out.reshape(N, num_heads * head_dim)
        key = jax.random.key(seed)
        ks = jax.random.split(key, 16)
        node_features = jax.random.normal(ks[0], (N_NODES, D_IN), dtype=jnp.float32)
        src = jax.random.randint(ks[1], (N_EDGES,), 0, N_NODES)
        dst = jax.random.randint(ks[2], (N_EDGES,), 0, N_NODES)
        s = 1.0 / np.sqrt(D_IN)
        inp = {'node_features': node_features, 'src': src, 'dst': dst}
        heads = [(12, 64), (12, 64), (1, 768)]
        for i, (H, D) in enumerate(heads):
            inp[f'W{i}'] = jax.random.normal(ks[3 + 4 * i], (D_IN, H * D), dtype=jnp.float32) * s
            inp[f'al{i}'] = jax.random.normal(ks[4 + 4 * i], (H, D), dtype=jnp.float32) * s
            inp[f'ar{i}'] = jax.random.normal(ks[5 + 4 * i], (H, D), dtype=jnp.float32) * s
            inp[f'b{i}'] = jnp.zeros((H * D,), dtype=jnp.float32)
        return inp
    _L0_gnn_all = _L0_gnn_setup()
    _L0_gnn_in = {k: v for k, v in _L0_gnn_all.items() if k in ('W0', 'al0', 'ar0', 'b0', 'W1', 'al1', 'ar1', 'b1', 'W2', 'al2', 'ar2', 'b2')}
    del _L0_gnn_all

    def _L0_ffn_setup():
        import jax, jax.numpy as jnp
        import numpy as np
        DECAY = 0.9
        EPS = 0.01
        TOP_K = 2
        key = jax.random.key(seed)
        k1, k2, k3, k4 = jax.random.split(key, 4)
        B, S, H, I, E = (4, 256, 768, 256, 8)
        return {'hidden_states': jax.random.normal(k1, (B, S, H), jnp.float32), 'router_w': jax.random.normal(k2, (E, H), jnp.float32) * 0.02, 'w1': jax.random.normal(k3, (E, I, H), jnp.float32) * 0.02, 'w2': jax.random.normal(k4, (E, H, I), jnp.float32) * 0.02}
    _L0_ffn_all = _L0_ffn_setup()
    _L0_ffn_in = {k: v for k, v in _L0_ffn_all.items() if k in ('router_w', 'w1', 'w2')}
    del _L0_ffn_all

    def _L1_gnn_setup():
        import jax, jax.numpy as jnp
        import numpy as np
        N_NODES = 1250
        N_EDGES = 10000
        IN_DIM, HID, OUT_DIM, HEADS = (768, 512, 768, 4)
        NEG_SLOPE = 0.2

        def _gat_layer(x, src, dst, W, a_src, a_dst, b, heads, d_out, concat):
            N = x.shape[0]
            h = (x @ W).reshape(N, heads, d_out)
            as_n = jnp.einsum('nhd,hd->nh', h, a_src)
            ad_n = jnp.einsum('nhd,hd->nh', h, a_dst)
            e = jax.nn.leaky_relu(as_n[src] + ad_n[dst], NEG_SLOPE)
            e_max = jax.lax.stop_gradient(jax.ops.segment_max(e, dst, num_segments=N))
            ex = jnp.exp(e - e_max[dst])
            denom = jax.ops.segment_sum(ex, dst, num_segments=N)
            alpha = ex / (denom[dst] + 1e-16)
            msg = alpha[:, :, None] * h[src]
            out = jax.ops.segment_sum(msg, dst, num_segments=N)
            out = out.reshape(N, heads * d_out) if concat else out.mean(axis=1)
            return out + b
        key = jax.random.key(seed)
        ks = jax.random.split(key, 10)
        g = 0.05
        return {'x': jax.random.normal(ks[0], (N_NODES, IN_DIM), jnp.float32), 'edge_index': jax.random.randint(ks[1], (2, N_EDGES), 0, N_NODES, jnp.int64), 'W1': jax.random.normal(ks[2], (IN_DIM, HEADS * HID), jnp.float32) * g, 'a1_src': jax.random.normal(ks[3], (HEADS, HID), jnp.float32) * g, 'a1_dst': jax.random.normal(ks[4], (HEADS, HID), jnp.float32) * g, 'b1': jnp.zeros((HEADS * HID,), jnp.float32), 'W2': jax.random.normal(ks[5], (HEADS * HID, OUT_DIM), jnp.float32) * g, 'a2_src': jax.random.normal(ks[6], (1, OUT_DIM), jnp.float32) * g, 'a2_dst': jax.random.normal(ks[7], (1, OUT_DIM), jnp.float32) * g, 'b2': jnp.zeros((OUT_DIM,), jnp.float32)}
    _L1_gnn_all = _L1_gnn_setup()
    _L1_gnn_in = {k: v for k, v in _L1_gnn_all.items() if k in ('W1', 'a1_src', 'a1_dst', 'b1', 'W2', 'a2_src', 'a2_dst', 'b2')}
    del _L1_gnn_all

    def _L1_ffn_setup():
        import jax, jax.numpy as jnp
        import numpy as np
        TOP_K = 2
        key = jax.random.key(seed)
        ks = jax.random.split(key, 5)
        B, T, C, H, E = (4, 1024, 768, 384, 8)
        x = jax.random.normal(ks[0], (B, T, C), dtype=jnp.float32)
        Wg = jax.random.normal(ks[1], (C, E), dtype=jnp.float32) * 0.02
        W1 = jax.random.normal(ks[2], (E, C, H), dtype=jnp.float32) * (1.0 / np.sqrt(C))
        b1 = jnp.zeros((E, H), dtype=jnp.float32)
        W2 = jax.random.normal(ks[3], (E, H, C), dtype=jnp.float32) * (1.0 / np.sqrt(H))
        b2 = jnp.zeros((E, C), dtype=jnp.float32)
        return {'x': x, 'Wg': Wg, 'W1': W1, 'b1': b1, 'W2': W2, 'b2': b2}
    _L1_ffn_all = _L1_ffn_setup()
    _L1_ffn_in = {k: v for k, v in _L1_ffn_all.items() if k in ('Wg', 'W1', 'b1', 'W2', 'b2')}
    del _L1_ffn_all
    return {'x': x, 'src': src, 'dst': dst, 'L0_gnn_W0': _L0_gnn_in['W0'], 'L0_gnn_al0': _L0_gnn_in['al0'], 'L0_gnn_ar0': _L0_gnn_in['ar0'], 'L0_gnn_b0': _L0_gnn_in['b0'], 'L0_gnn_W1': _L0_gnn_in['W1'], 'L0_gnn_al1': _L0_gnn_in['al1'], 'L0_gnn_ar1': _L0_gnn_in['ar1'], 'L0_gnn_b1': _L0_gnn_in['b1'], 'L0_gnn_W2': _L0_gnn_in['W2'], 'L0_gnn_al2': _L0_gnn_in['al2'], 'L0_gnn_ar2': _L0_gnn_in['ar2'], 'L0_gnn_b2': _L0_gnn_in['b2'], 'L0_ffn_router_w': _L0_ffn_in['router_w'], 'L0_ffn_w1': _L0_ffn_in['w1'], 'L0_ffn_w2': _L0_ffn_in['w2'], 'L1_gnn_W1': _L1_gnn_in['W1'], 'L1_gnn_a1_src': _L1_gnn_in['a1_src'], 'L1_gnn_a1_dst': _L1_gnn_in['a1_dst'], 'L1_gnn_b1': _L1_gnn_in['b1'], 'L1_gnn_W2': _L1_gnn_in['W2'], 'L1_gnn_a2_src': _L1_gnn_in['a2_src'], 'L1_gnn_a2_dst': _L1_gnn_in['a2_dst'], 'L1_gnn_b2': _L1_gnn_in['b2'], 'L1_ffn_Wg': _L1_ffn_in['Wg'], 'L1_ffn_W1': _L1_ffn_in['W1'], 'L1_ffn_b1': _L1_ffn_in['b1'], 'L1_ffn_W2': _L1_ffn_in['W2'], 'L1_ffn_b2': _L1_ffn_in['b2']}

def reference(x, src, dst, L0_gnn_W0, L0_gnn_al0, L0_gnn_ar0, L0_gnn_b0, L0_gnn_W1, L0_gnn_al1, L0_gnn_ar1, L0_gnn_b1, L0_gnn_W2, L0_gnn_al2, L0_gnn_ar2, L0_gnn_b2, L0_ffn_router_w, L0_ffn_w1, L0_ffn_w2, L1_gnn_W1, L1_gnn_a1_src, L1_gnn_a1_dst, L1_gnn_b1, L1_gnn_W2, L1_gnn_a2_src, L1_gnn_a2_dst, L1_gnn_b2, L1_ffn_Wg, L1_ffn_W1, L1_ffn_b1, L1_ffn_W2, L1_ffn_b2):
    import jax
    import jax.numpy as jnp

    def _L0_gnn_ref(node_features, W0, al0, ar0, b0, W1, al1, ar1, b1, W2, al2, ar2, b2, src, dst):
        import jax, jax.numpy as jnp
        import numpy as np
        N_NODES = 2500
        N_EDGES = 12500
        D_IN = 768
        NEG_SLOPE = 0.2

        def _gat_layer(x, W, attn_l, attn_r, bias, src, dst, num_heads, head_dim, use_elu):
            N = x.shape[0]
            z = (x @ W).reshape(N, num_heads, head_dim)
            el = jnp.sum(z * attn_l, axis=-1)
            er = jnp.sum(z * attn_r, axis=-1)
            e = jax.nn.leaky_relu(el[src] + er[dst], NEG_SLOPE)
            m = jax.ops.segment_max(e, dst, num_segments=N)
            ex = jnp.exp(e - m[dst])
            denom = jax.ops.segment_sum(ex, dst, num_segments=N)
            alpha = ex / denom[dst]
            msg = alpha[:, :, None] * z[src]
            out = jax.ops.segment_sum(msg, dst, num_segments=N)
            out = out + z
            out = out + bias.reshape(1, num_heads, head_dim)
            if use_elu:
                out = jax.nn.elu(out)
            return out.reshape(N, num_heads * head_dim)
        x = _gat_layer(node_features, W0, al0, ar0, b0, src, dst, 12, 64, True)
        x = _gat_layer(x, W1, al1, ar1, b1, src, dst, 12, 64, True)
        x = _gat_layer(x, W2, al2, ar2, b2, src, dst, 1, 768, False)
        return x

    def _L0_ffn_ref(hidden_states, router_w, w1, w2):
        import jax, jax.numpy as jnp
        import numpy as np
        DECAY = 0.9
        EPS = 0.01
        TOP_K = 2
        B, S, H = hidden_states.shape
        E = router_w.shape[0]
        flat = hidden_states.reshape(B * S, H)
        logits = flat @ router_w.T
        probs = jax.nn.softmax(logits, axis=-1)
        topk_probs, topk_idx = jax.lax.top_k(probs, TOP_K)
        importance = jax.lax.stop_gradient(probs).sum(axis=0)
        running = jnp.ones((E,), dtype=flat.dtype)
        blended = running + (1.0 - DECAY) * (importance - running)
        running = blended + EPS
        balance = running[topk_idx]
        balanced = topk_probs / balance
        balanced = balanced / balanced.sum(axis=-1, keepdims=True)
        h = jnp.einsum('th,eih->tei', flat, w1)
        h = jax.nn.silu(h)
        outs = jnp.einsum('tei,ehi->teh', h, w2)
        sel = jnp.take_along_axis(outs, topk_idx[:, :, None], axis=1)
        combined = (sel * balanced[..., None]).sum(axis=1)
        return combined.reshape(B, S, H)

    def _L1_gnn_ref(x, edge_index, W1, a1_src, a1_dst, b1, W2, a2_src, a2_dst, b2):
        import jax, jax.numpy as jnp
        import numpy as np
        N_NODES = 1250
        N_EDGES = 10000
        IN_DIM, HID, OUT_DIM, HEADS = (768, 512, 768, 4)
        NEG_SLOPE = 0.2

        def _gat_layer(x, src, dst, W, a_src, a_dst, b, heads, d_out, concat):
            N = x.shape[0]
            h = (x @ W).reshape(N, heads, d_out)
            as_n = jnp.einsum('nhd,hd->nh', h, a_src)
            ad_n = jnp.einsum('nhd,hd->nh', h, a_dst)
            e = jax.nn.leaky_relu(as_n[src] + ad_n[dst], NEG_SLOPE)
            e_max = jax.lax.stop_gradient(jax.ops.segment_max(e, dst, num_segments=N))
            ex = jnp.exp(e - e_max[dst])
            denom = jax.ops.segment_sum(ex, dst, num_segments=N)
            alpha = ex / (denom[dst] + 1e-16)
            msg = alpha[:, :, None] * h[src]
            out = jax.ops.segment_sum(msg, dst, num_segments=N)
            out = out.reshape(N, heads * d_out) if concat else out.mean(axis=1)
            return out + b
        N = x.shape[0]
        loops = jnp.arange(N, dtype=edge_index.dtype)
        src = jnp.concatenate([edge_index[0], loops])
        dst = jnp.concatenate([edge_index[1], loops])
        h = _gat_layer(x, src, dst, W1, a1_src, a1_dst, b1, HEADS, HID, True)
        h = jax.nn.elu(h)
        out = _gat_layer(h, src, dst, W2, a2_src, a2_dst, b2, 1, OUT_DIM, False)
        return out

    def _L1_ffn_ref(x, Wg, W1, b1, W2, b2):
        import jax, jax.numpy as jnp
        import numpy as np
        TOP_K = 2
        E = Wg.shape[-1]
        logits = jnp.einsum('btc,ce->bte', x, Wg)
        probs = jax.nn.softmax(logits, axis=-1)
        top_vals, top_idx = jax.lax.top_k(probs, TOP_K)
        gates = (jax.nn.one_hot(top_idx, E, dtype=probs.dtype) * top_vals[..., None]).sum(-2)
        h = jax.nn.relu(jnp.einsum('btc,ech->bteh', x, W1) + b1)
        y = jnp.einsum('bteh,ehc->btec', h, W2) + b2
        out = jnp.einsum('bte,btec->btc', gates, y)
        return out
    edge_index = jnp.stack([src, dst])
    x = x + _L0_gnn_ref(_layernorm(x, axis=-1), L0_gnn_W0, L0_gnn_al0, L0_gnn_ar0, L0_gnn_b0, L0_gnn_W1, L0_gnn_al1, L0_gnn_ar1, L0_gnn_b1, L0_gnn_W2, L0_gnn_al2, L0_gnn_ar2, L0_gnn_b2, src, dst)
    x = x + _L0_ffn_ref(_layernorm(x, axis=-1)[None], L0_ffn_router_w, L0_ffn_w1, L0_ffn_w2)[0]
    x = x + _L1_gnn_ref(_layernorm(x, axis=-1), edge_index, L1_gnn_W1, L1_gnn_a1_src, L1_gnn_a1_dst, L1_gnn_b1, L1_gnn_W2, L1_gnn_a2_src, L1_gnn_a2_dst, L1_gnn_b2)
    x = x + _L1_ffn_ref(_layernorm(x, axis=-1)[None], L1_ffn_Wg, L1_ffn_W1, L1_ffn_b1, L1_ffn_W2, L1_ffn_b2)[0]
    return x

_drawn_inputs = setup_inputs


def setup_inputs(seed=0):
    import zlib

    import numpy as np

    out = dict(_drawn_inputs(seed))
    spreads = {'L0_gnn_b0': (0.0, 0.1),
     'L0_gnn_b1': (0.0, 0.1),
     'L0_gnn_b2': (0.0, 0.1),
     'L1_gnn_b1': (0.0, 0.1),
     'L1_gnn_b2': (0.0, 0.1),
     'L1_ffn_b1': (0.0, 0.717),
     'L1_ffn_b2': (0.0, 0.535)}
    factors = {'L0_gnn_ar0': 14.381, 'L0_gnn_ar1': 20.237, 'L1_gnn_a2_dst': 8.0}
    for name, (base, spread) in spreads.items():
        noise = np.random.default_rng([zlib.crc32(name.encode()), seed]).standard_normal(out[name].shape)
        drawn = base * np.exp(spread * noise) if base else spread * noise
        out[name] = jnp.asarray(drawn.astype(out[name].dtype))
    for name, factor in factors.items():
        out[name] = (out[name] * factor).astype(out[name].dtype)
    return out
```

```python
from contextlib import ExitStack

import numpy as np

import concourse.bass as bass
from concourse import mybir

F32 = mybir.dt.float32
BF16 = mybir.dt.bfloat16
I16 = mybir.dt.int16
I32 = mybir.dt.int32
ALU = mybir.AluOpType
ACT = mybir.ActivationFunctionType
AX = mybir.AxisListType

N = 1250
P = 125
T = N // P
HALF = N // 2
HT = T // 2
E = 20000
EP = 125
PAIRS = E // (2 * EP)
C = 768
CK = C // 128
EX = 8
NONE = -1.0e30
TINY = 1.0e-30
EPS = 1e-5
RING = 5
SLOPE = 0.2
DECAY_STEP = 1.0 - 0.9
BAL_EPS = 0.01


def split(total, parts):
    out, at = [], 0
    for n in range(parts):
        w = -(-(total - at) // (parts - n))
        w += w % 2 if at + w < total else 0
        out.append((at, w))
        at += w
    return out


class Step:

    def __init__(self, eng, sem):
        self.eng, self.sem, self.base, self.k = eng, sem, 0, 0

    def add(self, instruction):
        instruction.then_inc(self.sem, 1)
        self.k += 1

    def wait(self):
        self.eng.wait_ge(self.sem, self.base + self.k)

    def enter(self, i, per_round):
        self.kept = self.base + self.k
        self.base, self.k, self.per = self.kept + i * per_round, 0, per_round

    def leave(self, rounds):
        assert self.k == self.per, (self.k, self.per)
        self.base, self.k = self.kept + rounds * self.per, 0


class Gat:

    def __init__(self, name, heads, width, k_tiles, prep, spill, add_z, signals, before):
        self.name, self.H, self.D, self.KT = name, heads, width, k_tiles
        self.F = heads * width
        self.K = k_tiles * 128
        self.prep, self.spill, self.add_z = prep, spill, add_z
        self.batched = width == 64
        self.groups = [(g, min(4, k_tiles - g)) for g in range(0, k_tiles, 4)]
        if spill:
            self.chunks = [(h * width, width) for h in range(heads)] + [(self.F, 2 * heads)]
            self.ring = len(self.chunks)
        else:
            self.chunks = [(0, self.F // 2), (self.F // 2, self.F // 2 + 2 * heads)]
            self.ring = 4
        self.cols = [(0, width + 1)] if self.batched else [(0, width // 2), (width // 2, width // 2 + 1)]
        bias = prep == "elu"
        self.loads = 64 if bias else 48
        G, NC, of = len(self.groups), len(self.chunks), [(heads + 1) // 2, heads // 2]
        banks = 2 * heads if self.batched else T * heads
        self.totals = dict(
            w_in=self.loads, x_in=[16 * HT] * 2, x_free=T, half_prep=T, mid=T, prepped=T, tp_ready=G * T, xt_ready=G * T,
            zp_ready=NC * T, z_ready=NC * T, ones=1, spilled=[16 * HT * spill] * 2, elt_ready=3, elt_sb=3, el_out=16,
            elb_in=[16 * n for n in of], r_ready=heads, rt_ready=heads, rt_sb=heads, r_out=[16 * n for n in of],
            rb_in=[16 * n for n in of], z_in=[16 * n * spill for n in of], e_ready=2 * T * heads, e_free=2 * T * heads,
            p_ready=2 * T * heads, p_free=2 * heads, ag_ready=banks, out_done=banks, stored=[8 * banks] * 2)
        self.since = {k: [0, 0] if isinstance(v, list) else 0 for k, v in self.totals.items()}
        if before is not None:
            for k in self.totals:
                had, more = before.since[k], before.totals[k]
                self.since[k] = [x + y for x, y in zip(had, more)] if isinstance(had, list) else had + more
        self.w_in = signals["w_in"]
        self.x_in = signals["x_in"]
        self.x_free = signals["x_free"]
        self.half_prep = signals["half_prep"]
        self.mid = signals["mid"]
        self.prepped = signals["prepped"]
        self.tp_ready = signals["tp_ready"]
        self.xt_ready = signals["xt_ready"]
        self.zp_ready = signals["zp_ready"]
        self.z_ready = signals["z_ready"]
        self.ones = signals["ones"]
        self.spilled = signals["spilled"]
        self.elt_ready = signals["elt_ready"]
        self.elt_sb = signals["elt_sb"]
        self.el_out = signals["el_out"]
        self.elb_in = signals["elb_in"]
        self.r_ready = signals["r_ready"]
        self.rt_ready = signals["rt_ready"]
        self.rt_sb = signals["rt_sb"]
        self.r_out = signals["r_out"]
        self.rb_in = signals["rb_in"]
        self.z_in = signals["z_in"]
        self.e_ready = signals["e_ready"]
        self.e_free = signals["e_free"]
        self.p_ready = signals["p_ready"]
        self.p_free = signals["p_free"]
        self.ag_ready = signals["ag_ready"]
        self.out_done = signals["out_done"]
        self.stored = signals["stored"]


class Moe:

    def __init__(self, name, inner, balanced, bias, sem):
        self.name, self.I, self.IC, self.balanced, self.bias = name, inner, inner // 128, balanced, bias
        s = lambda what, n=1: sem(f"{name}_{what}") if n == 1 else [sem(f"{name}_{what}{i}") for i in range(n)]
        self.c_in = s("c_in")
        self.x_in = s("x_in", 2)
        self.raw_free = s("raw_free")
        self.half_prep = s("half_prep")
        self.mid = s("mid")
        self.prepped = s("prepped")
        self.tp_ready = s("tp_ready")
        self.xt_ready = s("xt_ready")
        self.lg_ready = s("lg_ready")
        self.exp_in = s("exp_in")
        self.exped = s("exped")
        self.probs = s("probs")
        self.imp_ready = s("imp_ready")
        self.gates = s("gates")
        self.gt_ready = s("gt_ready")
        self.gt_sb = s("gt_sb")
        self.gb_ready = s("gb_ready")
        self.gb_free = s("gb_free")
        self.w_in = s("w_in", 2)
        self.h_ready = s("h_ready")
        self.h_sb = s("h_sb")
        self.y_ready = s("y_ready")
        self.y_done = s("y_done")
        self.stored = s("stored")


def graph_transformer(nc, A, out):
    ctx = ExitStack()
    with ctx:
        sems = []

        def sem(name):
            s = ctx.enter_context(nc.semaphore(name))
            sems.append(s)
            return s

        def sb(name, shape, dt=F32):
            return ctx.enter_context(nc.sbuf_tensor(name, shape, dt))

        AT = sb("edge_counts", [P, T, N], I16)
        MB = sb("no_edge_bias", [P, T, N], BF16)
        ident = sb("ident", [128, 128])
        noti = sb("not_ident", [P, P], BF16)
        elr = sb("elr", [P, T * 24])
        el2 = sb("el2", [P, T * 12])
        small = sb("small", [128, 256])
        ARENA = 38400
        arena = sb("arena", [128, ARENA])

        def carve(at, parts, width):
            assert at + width <= ARENA, (at, width)
            return arena[0:parts, at:at + width]

        P_AT, P_W = 0, 12500
        Z_AT, Z_W = P_AT + P_W, 10260
        S_AT = Z_AT + Z_W
        Ph = [carve(P_AT + h * T * HALF, P, T * HALF).rearrange("p (s d) -> p s d", s=T) for h in range(2)]

        banks = [ctx.enter_context(nc.psum_tensor(f"bank{i}", [128, 512], F32)) for i in range(8)]

        def dram(name, shape, dt=F32):
            return nc.dram_tensor(name, shape, dt, kind="Internal").ap()

        el_rows = dram("el_rows", (12, N))
        r_rows = dram("r_rows", (12, 2 * T, P))
        z_heads = dram("z_heads", (4, N, 512))
        raw = [dram(f"raw{i}", (N, C)) for i in range(3)] + [dram("raw3", (N, 2048)), dram("raw4", (N, C))]
        x2 = dram("x2", (N, C))
        by_tile = lambda a: a.rearrange("(t p) f -> p t f", p=P)
        over = lambda row, parts=P: row.partition_broadcast(parts)

        signals = dict(
            w_in=sem("w_in"),
            x_in=[sem("x_in0"), sem("x_in1")],
            x_free=sem("x_free"),
            half_prep=sem("half_prep"),
            mid=sem("mid"),
            prepped=sem("prepped"),
            tp_ready=sem("tp_ready"),
            xt_ready=sem("xt_ready"),
            zp_ready=sem("zp_ready"),
            z_ready=sem("z_ready"),
            ones=sem("ones"),
            spilled=[sem("spilled0"), sem("spilled1")],
            elt_ready=sem("elt_ready"),
            elt_sb=sem("elt_sb"),
            el_out=sem("el_out"),
            elb_in=[sem("elb_in0"), sem("elb_in1")],
            r_ready=sem("r_ready"),
            rt_ready=sem("rt_ready"),
            rt_sb=sem("rt_sb"),
            r_out=[sem("r_out0"), sem("r_out1")],
            rb_in=[sem("rb_in0"), sem("rb_in1")],
            z_in=[sem("z_in0"), sem("z_in1")],
            e_ready=sem("e_ready"),
            e_free=sem("e_free"),
            p_ready=sem("p_ready"),
            p_free=sem("p_free"),
            ag_ready=sem("ag_ready"),
            out_done=sem("out_done"),
            stored=[sem("stored0"), sem("stored1")],
        )
        layers = []
        for args in [
            ("g0", 12, 64, CK, "ln", False, True),
            ("g1", 12, 64, CK, "elu", False, True),
            ("g2", 1, C, CK, "elu", False, True),
            ("g3", 4, 512, CK, "ln", True, False),
            ("g4", 1, C, 16, "elu", False, False),
        ]:
            layers.append(Gat(*args, signals, layers[-1] if layers else None))
        moes = [Moe("m0", 256, True, False, sem), Moe("m1", 384, False, True, sem)]
        for n, L in enumerate(layers):
            L.W, L.al, L.ar = [(A["L0_gnn_W0"], A["L0_gnn_al0"], A["L0_gnn_ar0"]),
                               (A["L0_gnn_W1"], A["L0_gnn_al1"], A["L0_gnn_ar1"]),
                               (A["L0_gnn_W2"], A["L0_gnn_al2"], A["L0_gnn_ar2"]),
                               (A["L1_gnn_W1"], A["L1_gnn_a1_src"], A["L1_gnn_a1_dst"]),
                               (A["L1_gnn_W2"], A["L1_gnn_a2_src"], A["L1_gnn_a2_dst"])][n]
            L.src = [A["x"], raw[0], raw[1], x2, raw[3]][n]
            L.src_bias = [None, A["L0_gnn_b0"], A["L0_gnn_b1"], None, A["L1_gnn_b1"]][n]
            L.dst = raw[n]
            WW = L.F + 2 * L.H
            L.w_sb = carve(P_AT, 128, L.KT * WW).rearrange("p (k f) -> p k f", k=L.KT)
            at = S_AT
            L.xin = [carve(at + u * L.K, P, L.K) for u in range(2)]
            at += 2 * L.K
            L.low = [carve(at + u * max(L.K, L.F), P, L.K) for u in range(2)]
            L.alb = [carve(at + u * max(L.K, L.F), 128, L.F) for u in range(2)]
            at += 2 * max(L.K, L.F)
            L.xbias = carve(at, P, L.K)
            at += L.K
            L.xt = [carve(at + u * L.KT * P, 128, L.KT * P).rearrange("p (k n) -> p k n", k=L.KT) for u in range(2)]
            L.prod = carve(at, 128, L.F)
            at = S_AT
            L.rb = [carve(at + u * 2 * N, P, 2 * N).rearrange("p (r d) -> p r d", r=2) for u in range(2)]
            at += 4 * N
            L.elb = [carve(at + u * N, P, N) for u in range(2)]
            at += 2 * N
            L.e = [[carve(at + (2 * u + r) * HALF, P, HALF) for r in range(2)] for u in range(2)]
            at += 4 * HALF
            L.m = [carve(at + u * HALF, P, HALF) for u in range(2)]
            at += 2 * HALF
            L.junk = carve(at, P, HALF).bitcast(BF16)
            at += HALF
            L.og = [carve(at + u * C, P, C) for u in range(2)]
            at += 2 * C
            L.elt = carve(at, 12, N)
            L.rt = [carve(at + u * P, 2 * T, P) for u in range(2)]
            at += N
            if L.batched:
                L.z = carve(Z_AT, P, T * L.H * 65).rearrange("p (t h f) -> p t h f", t=T, h=L.H)
                L.z_ones = L.z[:, :, :, 64:65]
            elif L.spill:
                L.zh = [carve(Z_AT + u * T * 513, P, T * 513).rearrange("p (t f) -> p t f", t=T) for u in range(2)]
                L.stage = [carve(Z_AT + u * L.F, P, L.F).rearrange("p (h f) -> p h f", h=L.H) for u in range(2)]
            else:
                L.z = carve(Z_AT, P, T * (C + 1)).rearrange("p (t f) -> p t f", t=T)
                L.z_ones = L.z[:, :, C:C + 1]
            L.elr = elr[:, 0:T * 2 * L.H].rearrange("p (t h) -> p t h", t=T)
            L.el2 = el2[:, 0:T * L.H].rearrange("p (t h) -> p t h", t=T)
        for n, M in enumerate(moes):
            M.res, M.raw, M.raw_bias = [(A["x"], raw[2], A["L0_gnn_b2"]), (x2, raw[4], A["L1_gnn_b2"])][n]
            M.dst = [x2, out][n]
            M.router = [A["L0_router"], A["L1_ffn_Wg"]][n]
            M.w1, M.w2 = [(A["L0_w1"], A["L0_w2"]), (A["L1_ffn_W1"], A["L1_ffn_W2"])][n]
            at = 0
            M.acc = carve(at, P, T * C).rearrange("p (t f) -> p t f", t=T)
            at += T * C
            M.xt = carve(at, 128, CK * N).rearrange("p (k n) -> p k n", k=CK)
            at += CK * N
            M.w1s = [carve(at + u * CK * M.I, 128, CK * M.I).rearrange("p (k i) -> p k i", k=CK) for u in range(2)]
            at += 2 * CK * M.I
            M.w2s = [carve(at + u * M.IC * C, 128, M.IC * C).rearrange("p (k f) -> p k f", k=M.IC) for u in range(2)]
            at += 2 * M.IC * C
            M.ht = [carve(at + u * M.IC * N, 128, M.IC * N).rearrange("p (k n) -> p k n", k=M.IC) for u in range(2)]
            M.rawt = [carve(at + u * C, P, C) for u in range(2)]
            M.xn = [carve(at + (2 + u) * C, P, C) for u in range(2)]
            M.rbias = carve(at + 4 * C, P, C)
            at += 2 * M.IC * N
            g = [carve(at + j * T * EX, P, T * EX) for j in range(8)]
            at += 8 * T * EX
            M.g = [a.rearrange("p (t e) -> p t e", t=T) for a in g]
            M.gflat = g
            M.col = [carve(at + j * T, P, T) for j in range(4)]
            at += 4 * T
            M.order = carve(at, P, EX)
            M.run = carve(at + EX, P, EX)
            at += 2 * EX
            M.wr = carve(at, 128, CK * EX).rearrange("p (k e) -> p k e", k=CK)
            at += CK * EX
            M.b1 = carve(at, 128, EX * M.IC).rearrange("p (e c) -> p e c", e=EX)
            at += EX * M.IC
            M.onesq = carve(at, P, P)
            at += P
            M.b2 = carve(at, EX, C)
            at += C
            M.gt = [carve(at + u * P, EX, P) for u in range(2)]

        g_at = 0
        iota = carve(0, P, N)
        e_nat = [carve(N + j * 256, PAIRS, 2 * EP).bitcast(I32) for j in range(2)]
        e_f = [carve(N + 512 + j * 256, PAIRS, 2 * EP) for j in range(2)]
        e_t = carve(N + 1024, EP, 4 * PAIRS).rearrange("p (w a j) -> p w a j", w=2, a=2)
        lim = carve(N + 1400, PAIRS, 2)
        ge = carve(N + 1402, PAIRS, T + 1)
        has = carve(N + 1414, PAIRS, T)
        rng = carve(N + 1424, PAIRS, 2 * T)
        red = carve(N + 1444, 2 * T, 1)
        row = carve(N + 1446, 1, 2 * T)
        tab_f = carve(N + 1470, 1, 4 * T)
        tab = carve(N + 1520, 1, 4 * T).bitcast(I32)
        gjunk = carve(N + 1560, PAIRS, 2 * EP)
        oh_s = [carve(4000 + u * 700, EP, N // 2).bitcast(BF16) for u in range(2)]
        oh_d = [carve(5400 + u * 64, EP, 63).bitcast(BF16)[:, 0:P] for u in range(2)]
        zero = carve(5600, EP, 300).bitcast(BF16)
        a_blk = [carve(6300 + u * N, P, N) for u in range(2)]
        cuts = split(N, 3)

        gs = {n: sem("graph_" + n) for n in (
            "in", "float", "et_ready", "et_sb", "rng", "rng_t", "red", "red_t", "tab", "zero",
            "oh0", "oh1", "used0", "used1", "blk_ready", "blk_sb", "bias", "at_ready", "at_sb", "loops")}
        v_step = sem("vector_step")

        block = ctx.enter_context(nc.Block())

        def apart(e):
            e.nop(nofuse=True)

        def graph_sync(e):
            e.dma_start(ident[:, :], A["ident"]).then_inc(gs["in"], 16)
            e.dma_start(iota, over(A["nodes"])).then_inc(gs["in"], 16)
            e.dma_start(lim, A["pair_limits"]).then_inc(gs["in"], 16)
            for j, name in enumerate(("dst", "src")):
                e.dma_start(e_nat[j], A[name].rearrange("(j e) -> j e", j=PAIRS)).then_inc(gs["in"], 16)

        def gat_sync(e, L):
            e.dma_start(L.w_sb[:, :, 0:L.F], L.W.rearrange("(k p) f -> p k f", p=128)).then_inc(L.w_in, 16)
            e.dma_start(L.alb[0], over(L.al.rearrange("h d -> (h d)"), 128)).then_inc(L.w_in, 16)
            e.dma_start(L.alb[1], over(L.ar.rearrange("h d -> (h d)"), 128)).then_inc(L.w_in, 16)
            if L.src_bias is not None:
                e.dma_start(L.xbias, over(L.src_bias)).then_inc(L.w_in, 16)
            with e.Fori(0, HT) as i:
                for u in range(2):
                    t = 2 * i + u
                    e.wait_ge(L.x_free, L.since["x_free"] + t + 1)
                    e.dma_start(L.xin[u], by_tile(L.src)[:, t, :]).then_inc(L.x_in[u], 16)
            e.wait_ge(L.elt_sb, L.since["elt_sb"] + 3)
            e.dma_start(el_rows[0:L.H, :], L.elt[0:L.H, :]).then_inc(L.el_out, 16)
            e.wait_ge(L.el_out, L.since["el_out"] + 16)

            def load_el(h, u):
                e.dma_start(L.elb[u], over(el_rows[h, :])).then_inc(L.elb_in[u], 16)

            def move_r(h, u, i):
                e.wait_ge(L.rt_sb, L.since["rt_sb"] + h + 1)
                e.dma_start(r_rows[h, :, :], L.rt[u]).then_inc(L.r_out[u], 16)
                e.wait_ge(L.r_out[u], L.since["r_out"][u] + 16 * (i + 1))
                apart(e)
                e.dma_start(L.rb[u], over(r_rows[h, :, :].rearrange("(r t) p -> r (t p)", r=2))).then_inc(L.rb_in[u], 16)

            def load_z(h, u):
                e.dma_start(L.zh[u][:, :, 0:L.D], by_tile(z_heads[h, :, :])).then_inc(L.z_in[u], 16)

            if L.spill:
                for u in range(2):
                    e.wait_ge(L.spilled[u], L.since["spilled"][u] + 16 * HT)
            if L.H == 1:
                load_el(0, 0)
                move_r(0, 0, 0)
                return
            load_el(0, 0)
            load_el(1, 1)
            if L.spill:
                e.wait_ge(L.ones, L.since["ones"] + 1)
                load_z(0, 0)
                load_z(1, 1)
            move_r(0, 0, 0)
            move_r(1, 1, 0)
            with e.Fori(1, L.H // 2) as i:
                for u in range(2):
                    h = 2 * i + u
                    e.wait_ge(L.r_ready, L.since["r_ready"] + h - 1)
                    load_el(h, u)
                    if L.spill:
                        e.wait_ge(L.p_free, L.since["p_free"] + 2 * h)
                        load_z(h, u)
                    e.wait_ge(L.e_ready, L.since["e_ready"] + 2 * T * (h - 1))
                    apart(e)
                    move_r(h, u, i)

        def moe_sync(e, M):
            e.dma_start(M.wr, M.router.rearrange("(k p) e -> p k e", p=128)).then_inc(M.c_in, 16)
            e.dma_start(M.rbias, over(M.raw_bias)).then_inc(M.c_in, 16)
            e.dma_start(M.order, over(A["order"])).then_inc(M.c_in, 16)
            if M.bias:
                e.dma_start(M.b1, A["L1_b1"]).then_inc(M.c_in, 16)
                e.dma_start(M.b2, A["L1_ffn_b2"]).then_inc(M.c_in, 16)
            with e.Fori(0, HT) as i:
                for u in range(2):
                    t = 2 * i + u
                    e.wait_ge(M.raw_free, t + 1)
                    e.dma_start(M.acc[:, t, :], by_tile(M.res)[:, t, :]).then_inc(M.x_in[u], 16)
                    e.dma_start(M.rawt[u], by_tile(M.raw)[:, t, :]).then_inc(M.x_in[u], 16)

            def load_w(x, u):
                e.dma_start(M.w1s[u], M.w1[x, :, :].rearrange("(k p) i -> p k i", p=128)).then_inc(M.w_in[u], 16)
                e.dma_start(M.w2s[u], M.w2[x, :, :].rearrange("(k p) f -> p k f", p=128)).then_inc(M.w_in[u], 16)

            load_w(0, 0)
            load_w(1, 1)
            with e.Fori(1, EX // 2) as i:
                for u in range(2):
                    e.wait_ge(M.y_ready, T * (2 * i + u - 1))
                    apart(e)
                    load_w(2 * i + u, u)
            with e.Fori(0, T) as t:
                e.wait_ge(M.y_done, 2 + T * (EX - 1) + t + 1)
                e.dma_start(by_tile(M.dst)[:, t, :], M.acc[:, t, :]).then_inc(M.stored, 16)
            e.wait_ge(M.stored, 16 * T)

        def previous_stored(e, L):
            for u in range(2):
                e.wait_ge(L.stored[u], L.since["stored"][u] + L.totals["stored"][u])

        @block.sync
        def _(e):
            graph_sync(e)
            e.wait_ge(gs["at_sb"], 3 * T)
            e.wait_ge(gs["bias"], T)
            for n in range(3):
                gat_sync(e, layers[n])
                previous_stored(e, layers[n])
            moe_sync(e, moes[0])
            for n in range(3, 5):
                gat_sync(e, layers[n])
                previous_stored(e, layers[n])
            moe_sync(e, moes[1])

        def gat_gpsimd(e, L):
            if L.spill:
                with e.Fori(0, HT) as i:
                    for u in range(2):
                        t = 2 * i + u
                        e.wait_ge(L.z_ready, L.since["z_ready"] + RING + len(L.chunks) * (t + 1))
                        e.dma_start(z_heads[:, :, :].rearrange("h (t p) f -> p t h f", p=P)[:, t, :, :],
                                    L.stage[u]).then_inc(L.spilled[u], 16)

            def store(h):
                for half in range(2):
                    if L.batched:
                        e.wait_ge(L.out_done, L.since["out_done"] + 2 + 2 * h + half + 1)
                        e.dma_start(by_tile(L.dst)[:, half * HT:(half + 1) * HT, bass.ds(h * 64, 64)],
                                    L.og[half][:, 0:HT * 64].rearrange("p (t f) -> p t f", t=HT)).then_inc(L.stored[half], 16)
                        continue
                    for d in range(HT):
                        j = half * HT + d
                        e.wait_ge(L.out_done, L.since["out_done"] + 2 + T * h + j + 1)
                        e.dma_start(by_tile(L.dst)[:, j, bass.ds(h * L.D, L.D)],
                                    L.og[j % 2][:, 0:L.D]).then_inc(L.stored[j % 2], 16)

            if L.H == 1:
                store(0)
            else:
                with e.Fori(0, L.H) as h:
                    store(h)

        def moe_gpsimd(e, M):
            e.sem_inc(M.raw_free, 2)
            e.sem_inc(M.y_done, 2)

        @block.gpsimd
        def _(e):
            for u in range(2):
                e.sem_inc(gs[f"oh{u}"], PAIRS)
                e.sem_inc(gs[f"used{u}"], PAIRS + 1)
            L = layers[0]
            e.sem_inc(L.x_free, 2)
            e.sem_inc(L.e_free, 2)
            e.sem_inc(L.p_free, 2)
            e.sem_inc(L.out_done, 2)
            for M in moes:
                moe_gpsimd(e, M)
            for L in layers:
                gat_gpsimd(e, L)

        def graph_tensor(e):
            e.wait_ge(gs["float"], 2)
            for w in range(2):
                for a in range(2):
                    ins = e.transpose(banks[7][0:EP, (2 * w + a) * PAIRS:(2 * w + a + 1) * PAIRS],
                                      e_f[w][:, a * EP:(a + 1) * EP], ident[0:PAIRS, 0:PAIRS])
            ins.then_inc(gs["et_ready"], 1)
            e.wait_ge(gs["rng"], 1)
            e.wait_ge(gs["et_sb"], 1)
            e.transpose(banks[7][0:2 * T, 0:PAIRS], rng, ident[0:PAIRS, 0:PAIRS]).then_inc(gs["rng_t"], 1)
            e.wait_ge(gs["red"], 1)
            e.transpose(banks[6][0:1, 0:2 * T], red, ident[0:2 * T, 0:2 * T]).then_inc(gs["red_t"], 1)
            e.wait_ge(gs["tab"], 1)
            e.wait_ge(gs["zero"], 1)
            for b in range(T):
                lo = e.value_load(tab[0:1, b:b + 1], min_val=0, max_val=PAIRS - 1)
                hi = e.value_load(tab[0:1, T + b:T + b + 1], min_val=1, max_val=PAIRS)
                before = e.value_load(tab[0:1, 2 * T + b:2 * T + b + 1], min_val=0, max_val=T * PAIRS)
                acc = [banks[3 * (b % 2) + c][0:P, 0:w] for c, (_, w) in enumerate(cuts)]
                if b >= 2:
                    e.wait_ge(gs["blk_sb"], b - 1)
                for c, (_, w) in enumerate(cuts):
                    e.matmul(acc[c], zero[:, 0:P], zero[:, P:P + w], start=True, stop=False)
                with e.Fori(lo, hi) as j:
                    for u in range(2):
                        e.wait_ge(gs[f"oh{u}"], before + j + 1)
                        for c, (at, w) in enumerate(cuts):
                            ins = e.matmul(acc[c], oh_d[u], oh_s[u][:, at:at + w], start=False, stop=False)
                        ins.then_inc(gs[f"used{u}"], 1)
                for c, (_, w) in enumerate(cuts):
                    ins = e.matmul(acc[c], zero[:, 0:P], zero[:, P:P + w], start=False, stop=True)
                ins.then_inc(gs["blk_ready"], 1)
                if b >= 1:
                    graph_turn(e, b - 1)
            graph_turn(e, T - 1)

        def graph_turn(e, b):
            e.wait_ge(gs["blk_sb"], b + 1)
            for g in range(3):
                if 3 * b + g >= 2:
                    e.wait_ge(gs["at_sb"], 3 * b + g - 1)
                bank = banks[6 + (3 * b + g) % 2]
                for s in range(4 * g, min(T, 4 * g + 4)):
                    ins = e.transpose(bank[0:P, (s % 4) * P:(s % 4 + 1) * P], a_blk[b % 2][:, s * P:(s + 1) * P],
                                      ident[0:P, 0:P])
                ins.then_inc(gs["at_ready"], 1)

        def two_ahead(e, body):
            with e.Fori(0, HT - 1) as i:
                for u in range(2):
                    body(2 * i + u, u, False)
            for t in (T - 2, T - 1):
                body(t, t % 2, True)

        def gat_tensor(e, L):
            G, NC = len(L.groups), len(L.chunks)

            def transposes(t, u):
                e.wait_ge(L.prepped, L.since["prepped"] + t + 1)
                for g, (k0, n) in enumerate(L.groups):
                    e.wait_ge(L.xt_ready, L.since["xt_ready"] + G * t + g + 1)
                    for k in range(n):
                        ins = e.transpose(banks[g % 2][:, k * P:(k + 1) * P],
                                          L.xin[u][:, (k0 + k) * 128:(k0 + k + 1) * 128], ident[0:P, 0:P])
                    ins.then_inc(L.tp_ready, 1)

            def project(t, u):
                e.wait_ge(L.xt_ready, L.since["xt_ready"] + 2 + G * (t + 1))
                for c, (at, w) in enumerate(L.chunks):
                    bank = banks[2 + (u * NC + c) % L.ring]
                    e.wait_ge(L.z_ready, L.since["z_ready"] + RING - L.ring + NC * t + c + 1)
                    for k in range(L.KT):
                        ins = e.matmul(bank[0:P, 0:w], L.xt[u][:, k, :], L.w_sb[:, k, at:at + w],
                                       start=(k == 0), stop=(k == L.KT - 1))
                        if c == 0 and k == 0:
                            ins.then_inc(L.x_free, 1)
                    ins.then_inc(L.zp_ready, 1)

            e.wait_ge(L.w_in, L.since["w_in"] + L.loads)
            transposes(0, 0)

            def both(t, u, last):
                if not (last and u == 1):
                    transposes(t + 1, 1 - u)
                project(t, u)
            two_ahead(e, both)

            for g in range(3):
                if g == 0:
                    e.wait_ge(L.z_ready, L.since["z_ready"] + RING + NC * T)
                if g == 2:
                    e.wait_ge(L.elt_sb, L.since["elt_sb"] + 1)
                for t in range(4 * g, min(T, 4 * g + 4)):
                    ins = e.transpose(banks[g % 2][0:L.H, (t % 4) * P:(t % 4 + 1) * P], L.elr[:, t, 0:L.H], ident[0:P, 0:P])
                ins.then_inc(L.elt_ready, 1)

            def turn_r(h, u):
                e.wait_ge(L.r_ready, L.since["r_ready"] + h + 1)
                if not isinstance(h, int) or h > 0:
                    e.wait_ge(L.rt_sb, L.since["rt_sb"] + h)
                e.transpose(banks[0][0:2 * T, 0:P], small[0:P, 64 + u * 2 * T:64 + (u + 1) * 2 * T], ident[0:P, 0:P]).then_inc(L.rt_ready, 1)

            def aggregate(h, u, i):
                if L.spill:
                    e.wait_ge(L.z_in[u], L.since["z_in"][u] + 16 * (i + 1))
                for half in range(2):
                    for d in range(HT):
                        j = half * HT + d
                        if not L.batched:
                            e.wait_ge(L.out_done, L.since["out_done"] + T * h + j + 1)
                        elif d == 0:
                            e.wait_ge(L.out_done, L.since["out_done"] + 2 * h + half + 1)
                        for c, (at, w) in enumerate(L.cols):
                            bank = banks[2 + half] if L.batched else banks[2 + 2 * (j % 2) + c]
                            o = bank[0:P, d * 65:(d + 1) * 65] if L.batched else bank[0:P, 0:w]
                            for s in range(T):
                                if d == 0 and c == 0:
                                    e.wait_ge(L.p_ready, L.since["p_ready"] + 2 * T * h + half * T + s + 1)
                                zz = L.z[:, s, h, :] if L.batched else (L.zh[u] if L.spill else L.z)[:, s, at:at + w]
                                ins = e.matmul(o, Ph[half][:, s, d * P:(d + 1) * P], zz, start=(s == 0), stop=(s == T - 1))
                        if not L.batched or d == HT - 1:
                            ins.then_inc(L.ag_ready, 1)
                    e.matmul(banks[6][0:1, 0:1], ident[:, 0:1], ident[:, 0:1], start=True, stop=True).then_inc(L.p_free, 1)

            turn_r(0, 0)
            if L.H == 1:
                aggregate(0, 0, 0)
                return
            with e.Fori(0, L.H // 2 - 1) as i:
                turn_r(2 * i + 1, 1)
                aggregate(2 * i, 0, i)
                turn_r(2 * i + 2, 0)
                aggregate(2 * i + 1, 1, i)
            turn_r(L.H - 1, 1)
            aggregate(L.H - 2, 0, L.H // 2 - 1)
            aggregate(L.H - 1, 1, L.H // 2 - 1)

        TOK = split(N, 3)

        def moe_tensor(e, M):
            e.wait_ge(M.c_in, 80 if M.bias else 48)

            def transposes(t, u, _):
                e.wait_ge(M.prepped, t + 1)
                for g in range(2):
                    e.wait_ge(M.xt_ready, 2 * t + g + 2)
                    for k in range(4 * g, min(CK, 4 * g + 4)):
                        ins = e.transpose(banks[g][:, (k % 4) * P:(k % 4 + 1) * P],
                                          M.xn[u][:, k * 128:(k + 1) * 128], ident[0:P, 0:P])
                    ins.then_inc(M.tp_ready, 1)
            two_ahead(e, transposes)
            for t in range(T):
                e.wait_ge(M.xt_ready, 3 + 2 * (t + 1))
                for k in range(CK):
                    ins = e.matmul(banks[2][0:P, t * EX:(t + 1) * EX], M.xt[:, k, t * P:(t + 1) * P], M.wr[:, k, :],
                                   start=(k == 0), stop=(k == CK - 1))
            ins.then_inc(M.lg_ready, 1)

            def hidden(x, u, i):
                e.wait_ge(M.w_in[u], 32 * (i + 1))
                for ci in range(M.IC):
                    for n, (at, w) in enumerate(TOK):
                        j = ci * 3 + n
                        e.wait_ge(M.h_sb, 3 * M.IC * x + j + 1)
                        bank = banks[(u * 3 * M.IC + j) % 2]
                        for k in range(CK):
                            ins = e.matmul(bank[:, 0:w], M.w1s[u][:, k, ci * 128:(ci + 1) * 128], M.xt[:, k, at:at + w],
                                           start=(k == 0), stop=(k == CK - 1))
                        ins.then_inc(M.h_ready, 1)

            def outputs(x, u):
                e.wait_ge(M.h_sb, 2 + 3 * M.IC * (x + 1))
                for t in range(T):
                    y = t % 2
                    e.wait_ge(M.y_done, T * x + t + 1)
                    for c in range(2):
                        for ci in range(M.IC):
                            ins = e.matmul(banks[2 + 2 * y + c][0:P, 0:C // 2], M.ht[u][:, ci, t * P:(t + 1) * P],
                                           M.w2s[u][:, ci, c * (C // 2):(c + 1) * (C // 2)],
                                           start=(ci == 0), stop=(ci == M.IC - 1))
                    ins.then_inc(M.y_ready, 1)

            if M.balanced:
                e.wait_ge(M.probs, 1)
                e.matmul(banks[3][0:P, 0:T * EX], M.onesq, M.gflat[1], start=True, stop=True).then_inc(M.imp_ready, 1)
            if M.bias:
                e.wait_ge(M.gates, 1)
                for t in range(T):
                    if t >= 2:
                        e.wait_ge(M.gt_sb, t - 1)
                    e.transpose(banks[t % 2][0:EX, 0:P], M.g[6][:, t, :], ident[0:P, 0:P]).then_inc(M.gt_ready, 1)
                    e.wait_ge(M.gt_sb, t + 1)
                    if t >= 2:
                        e.wait_ge(M.gb_free, t - 1)
                    for c in range(2):
                        ins = e.matmul(banks[4 + 2 * (t % 2) + c][0:P, 0:C // 2], M.gt[t % 2], M.b2[:, c * (C // 2):(c + 1) * (C // 2)],
                                       start=True, stop=True)
                    ins.then_inc(M.gb_ready, 1)
                e.wait_ge(M.gb_free, T)
            e.wait_ge(M.gates, 1)
            hidden(0, 0, 0)
            with e.Fori(0, EX // 2 - 1) as i:
                hidden(2 * i + 1, 1, i)
                outputs(2 * i, 0)
                hidden(2 * i + 2, 0, i + 1)
                outputs(2 * i + 1, 1)
            hidden(EX - 1, 1, EX // 2 - 1)
            outputs(EX - 2, 0)
            outputs(EX - 1, 1)

        @block.tensor
        def _(e):
            graph_tensor(e)
            for n in range(3):
                gat_tensor(e, layers[n])
            moe_tensor(e, moes[0])
            for n in range(3, 5):
                gat_tensor(e, layers[n])
            moe_tensor(e, moes[1])

        def graph_scalar(e):
            e.wait_ge(gs["et_ready"], 1)
            e.activation(e_t.rearrange("p w a j -> p (w a j)"), banks[7][0:EP, 0:4 * PAIRS], ACT.Copy).then_inc(gs["et_sb"], 1)

            def turned(b):
                for g in range(3):
                    e.wait_ge(gs["at_ready"], 3 * b + g + 1)
                    n = min(4, T - 4 * g)
                    e.activation(AT[:, 4 * g:4 * g + n, b * P:(b + 1) * P],
                                 banks[6 + (3 * b + g) % 2][0:P, 0:n * P].rearrange("p (s d) -> p s d", s=n),
                                 ACT.Copy).then_inc(gs["at_sb"], 1)
            for b in range(T):
                e.wait_ge(gs["blk_ready"], b + 1)
                if b >= 2:
                    e.wait_ge(gs["bias"], b - 1)
                for c, (at, w) in enumerate(cuts):
                    ins = e.activation(a_blk[b % 2][:, at:at + w], banks[3 * (b % 2) + c][0:P, 0:w], ACT.Copy)
                ins.then_inc(gs["blk_sb"], 1)
                if b >= 1:
                    turned(b - 1)
            turned(T - 1)

        def gat_scalar(e, L):
            G, NC = len(L.groups), len(L.chunks)
            if L is layers[0]:
                e.sem_inc(L.xt_ready, 2)
                e.sem_inc(L.z_ready, RING)

            def mid(t, u):
                e.wait_ge(L.half_prep, L.since["half_prep"] + t + 1)
                if L.prep == "ln":
                    e.activation(small[0:P, 16 + 4 * u + 1:16 + 4 * u + 2], small[0:P, 16 + 4 * u:16 + 4 * u + 1], ACT.Sqrt).then_inc(L.mid, 1)
                else:
                    e.activation(L.low[u], L.low[u], ACT.Exp).then_inc(L.mid, 1)

            def turned(t, u):
                for g, (k0, n) in enumerate(L.groups):
                    e.wait_ge(L.tp_ready, L.since["tp_ready"] + G * t + g + 1)
                    e.activation(L.xt[u][:, k0:k0 + n, :], banks[g % 2][:, 0:n * P].rearrange("p (k n) -> p k n", k=n),
                                 ACT.Copy).then_inc(L.xt_ready, 1)

            def keep(t, u, i):
                for c, (at, w) in enumerate(L.chunks):
                    bank = banks[2 + (u * NC + c) % L.ring]
                    e.wait_ge(L.zp_ready, L.since["zp_ready"] + NC * t + c + 1)
                    if L.spill and c == 0 and not (isinstance(i, int) and i == 0):
                        e.wait_ge(L.spilled[u], L.since["spilled"][u] + 16 * i)
                    apart(e)
                    zw = min(w, L.F - at)
                    if zw > 0:
                        if L.batched:
                            o = L.z[:, t, at // 64:(at + zw) // 64, 0:64]
                            s = bank[0:P, 0:zw].rearrange("p (h f) -> p h f", f=64)
                        elif L.spill:
                            o, s = L.stage[u][:, c, :], bank[0:P, 0:zw]
                        else:
                            o, s = L.z[:, t, at:at + zw], bank[0:P, 0:zw]
                        ins = e.activation(o, s, ACT.Copy)
                    if w > max(zw, 0):
                        ins = e.activation(L.elr[:, t, :], bank[0:P, max(zw, 0):w], ACT.Copy)
                    ins.then_inc(L.z_ready, 1)

            mid(0, 0)
            mid(1, 1)
            turned(0, 0)
            def around(i):
                for u in range(2):
                    t = 2 * i + u
                    turned(t + 1, 1 - u)
                    mid(t + 2, u)
                    keep(t, u, i)
            if L.spill:
                around(0)
            with e.Fori(1 if L.spill else 0, HT - 1) as i:
                around(i)
            turned(T - 1, 1)
            keep(T - 2, 0, HT - 1)
            keep(T - 1, 1, HT - 1)
            for g in range(3):
                n = min(4, T - 4 * g)
                e.wait_ge(L.elt_ready, L.since["elt_ready"] + g + 1)
                e.activation(L.elt[0:L.H, 4 * g * P:(4 * g + n) * P], banks[g % 2][0:L.H, 0:n * P], ACT.Copy).then_inc(L.elt_sb, 1)
            e.wait_ge(L.el_out, L.since["el_out"] + 16)

            def rows(h, u):
                e.wait_ge(L.rt_ready, L.since["rt_ready"] + h + 1)
                e.activation(L.rt[u], banks[0][0:2 * T, 0:P], ACT.Copy).then_inc(L.rt_sb, 1)

            def exps(h, u, i, js):
                for j in js:
                    half, s = j // T, j % T
                    if j == 0:
                        e.wait_ge(L.rb_in[u], L.since["rb_in"][u] + 16 * (i + 1))
                    e.wait_ge(L.e_free, L.since["e_free"] + 2 * T * h + j + 1)
                    apart(e)
                    cols = slice(half * HALF, (half + 1) * HALF)
                    e.activation(L.e[j % 2][0], L.rb[u][:, 0, cols], ACT.Exp, bias=L.elr[:, s, bass.ds(h, 1)])
                    e.activation(L.e[j % 2][1], L.rb[u][:, 1, cols], ACT.Exp, bias=L.el2[:, s, bass.ds(h, 1)]).then_inc(L.e_ready, 1)

            rows(0, 0)
            if L.H == 1:
                exps(0, 0, 0, range(2 * T))
                return
            with e.Fori(0, L.H // 2 - 1) as i:
                for u in range(2):
                    h = 2 * i + u
                    exps(h, u, i, range(ROWS_AT))
                    rows(h + 1, 1 - u)
                    exps(h, u, i, range(ROWS_AT, 2 * T))
            i = L.H // 2 - 1
            exps(L.H - 2, 0, i, range(ROWS_AT))
            rows(L.H - 1, 1)
            exps(L.H - 2, 0, i, range(ROWS_AT, 2 * T))
            exps(L.H - 1, 1, i, range(2 * T))

        MAX_STEPS = [0, 1, 3, 4, 6, 7, 9, 10, 12, 13]
        ROWS_AT = 15

        def moe_scalar(e, M):
            e.sem_inc(M.xt_ready, 3)
            e.sem_inc(M.h_sb, 2)

            def prep(t, u, _):
                e.wait_ge(M.half_prep, t + 1)
                e.activation(small[0:P, 16 + 4 * u + 1:16 + 4 * u + 2], small[0:P, 16 + 4 * u:16 + 4 * u + 1], ACT.Sqrt).then_inc(M.mid, 1)
                for g in range(2):
                    n = min(4, CK - 4 * g)
                    e.wait_ge(M.tp_ready, 2 * t + g + 1)
                    apart(e)
                    e.activation(M.xt[:, 4 * g:4 * g + n, bass.ds(t * P, P)],
                                 banks[g][:, 0:n * P].rearrange("p (k n) -> p k n", k=n), ACT.Copy).then_inc(M.xt_ready, 1)
            two_ahead(e, prep)
            e.wait_ge(M.exp_in, 1)
            e.activation(M.gflat[0], M.gflat[0], ACT.Exp).then_inc(M.exped, 1)
            if M.bias:
                for t in range(T):
                    e.wait_ge(M.gt_ready, t + 1)
                    if t >= 2:
                        e.wait_ge(M.gb_ready, t - 1)
                    e.activation(M.gt[t % 2], banks[t % 2][0:EX, 0:P], ACT.Copy).then_inc(M.gt_sb, 1)

            def hidden(x, u):
                for ci in range(M.IC):
                    for n, (at, w) in enumerate(TOK):
                        j = ci * 3 + n
                        e.wait_ge(M.h_ready, 3 * M.IC * x + j + 1)
                        apart(e)
                        bank = banks[(u * 3 * M.IC + j) % 2]
                        if M.bias:
                            ins = e.activation(M.ht[u][:, ci, at:at + w], bank[:, 0:w], ACT.Relu, bias=M.b1[:, bass.ds(x, 1), ci])
                        else:
                            ins = e.activation(M.ht[u][:, ci, at:at + w], bank[:, 0:w], ACT.Silu)
                        ins.then_inc(M.h_sb, 1)
            with e.Fori(0, EX // 2) as i:
                for u in range(2):
                    hidden(2 * i + u, u)

        @block.scalar
        def _(e):
            graph_scalar(e)
            for n in range(3):
                gat_scalar(e, layers[n])
            moe_scalar(e, moes[0])
            for n in range(3, 5):
                gat_scalar(e, layers[n])
            moe_scalar(e, moes[1])

        def graph_vector(e, st):
            e.wait_ge(gs["in"], 16 * 5)
            st.add(e.memset(zero, 0.0))
            for w in range(2):
                e.tensor_copy(e_f[w], e_nat[w]).then_inc(gs["float"], 1)
            e.wait_ge(gs["float"], 2)
            for b in range(T + 1):
                st.wait()
                st.add(e.tensor_scalar(gjunk, e_f[0], b * P - 0.5, None, ALU.is_ge, ALU.add, accum_out=ge[:, b:b + 1]))
            st.wait()
            st.add(e.tensor_tensor(has, ge[:, 0:T], ge[:, 1:T + 1], ALU.not_equal))
            st.wait()
            st.add(e.tensor_scalar(rng[:, 0:T], has, lim[:, 0:1], None, ALU.mult))
            e.tensor_scalar(rng[:, T:2 * T], has, lim[:, 1:2], None, ALU.mult).then_inc(gs["rng"], 1)
            e.wait_ge(gs["rng_t"], 1)
            e.tensor_reduce(red, banks[7][0:2 * T, 0:PAIRS], AX.X, ALU.max).then_inc(gs["red"], 1)
            e.wait_ge(gs["red_t"], 1)
            st.add(e.tensor_scalar(row[:, 0:T], banks[6][0:1, 0:T], -1.0, float(PAIRS), ALU.mult, ALU.add))
            st.wait()
            st.add(e.tensor_scalar(tab_f[:, 0:T], row[:, 0:T], float(PAIRS - 1), None, ALU.min))
            st.wait()
            st.add(e.tensor_scalar(row[:, T:2 * T], tab_f[:, 0:T], 1.0, None, ALU.add))
            st.wait()
            st.add(e.tensor_tensor(tab_f[:, T:2 * T], row[:, T:2 * T], banks[6][0:1, T:2 * T], ALU.max))
            st.wait()
            st.add(e.tensor_tensor(row[:, 0:T], tab_f[:, T:2 * T], tab_f[:, 0:T], ALU.subtract))
            st.add(e.memset(tab_f[:, 3 * T:4 * T], 0.0))
            st.wait()
            for b in range(1, T):
                st.add(e.tensor_tensor(tab_f[:, 3 * T + b:3 * T + b + 1], tab_f[:, 3 * T + b - 1:3 * T + b], row[:, b - 1:b], ALU.add))
                st.wait()
            st.add(e.tensor_tensor(row[:, 0:T], tab_f[:, 3 * T:4 * T], tab_f[:, 0:T], ALU.subtract))
            st.wait()
            st.add(e.tensor_scalar(tab_f[:, 2 * T:3 * T], row[:, 0:T], float(PAIRS), None, ALU.add))
            st.wait()
            e.tensor_copy(tab, tab_f).then_inc(gs["tab"], 1)
            st.add(e.tensor_scalar(noti[:, :], ident[0:P, 0:P], 0.0, None, ALU.is_equal))
            e.wait_ge(gs["et_sb"], 1)
            e.wait_ge(gs["tab"], 1)
            st.wait()
            e.engine_nop().then_inc(gs["zero"], 1)
            for b in range(T):
                lo = e.value_load(tab[0:1, b:b + 1], min_val=0, max_val=PAIRS - 1)
                hi = e.value_load(tab[0:1, T + b:T + b + 1], min_val=1, max_val=PAIRS)
                before = e.value_load(tab[0:1, 2 * T + b:2 * T + b + 1], min_val=0, max_val=T * PAIRS)
                with e.Fori(lo, hi) as j:
                    for u in range(2):
                        e.wait_ge(gs[f"used{u}"], before + j + 1)
                        e.tensor_scalar(oh_d[u], iota[:, b * P:(b + 1) * P], e_t[:, 0, u, bass.ds(j, 1)], None, ALU.is_equal)
                        e.tensor_scalar(oh_s[u], iota, e_t[:, 1, u, bass.ds(j, 1)], None, ALU.is_equal).then_inc(gs[f"oh{u}"], 1)
                if b >= 1:
                    graph_bias(e, b - 1)
            graph_bias(e, T - 1)

        def graph_bias(e, b):
            e.wait_ge(gs["blk_sb"], b + 1)
            e.wait_ge(gs["at_ready"], 3 * (b + 1))
            e.tensor_scalar(MB[:, b, :], a_blk[b % 2], 0.0, NONE, ALU.is_equal, ALU.mult).then_inc(gs["bias"], 1)

        def add_loops(e):
            for t in range(T):
                e.tensor_tensor(AT[:, t, t * P:(t + 1) * P], AT[:, t, t * P:(t + 1) * P], ident[0:P, 0:P], ALU.add)
                e.tensor_tensor(MB[:, t, t * P:(t + 1) * P], MB[:, t, t * P:(t + 1) * P], noti[:, :], ALU.mult).then_inc(gs["loops"], 1)

        def norm_a(e, st, x, u, done):
            apart(e)
            stats = small[0:P, 0:12].rearrange("p (a b) -> p a b", a=2)
            for a in range(2):
                st.add(e.bn_stats(stats[:, a, :], x[:, a * (C // 2):(a + 1) * (C // 2)]))
            st.wait()
            apart(e)
            st.add(e.bn_aggr(small[0:P, 12:14], stats))
            st.wait()
            e.tensor_scalar(small[0:P, 16 + 4 * u:16 + 4 * u + 1], small[0:P, 13:14], EPS, None, ALU.add).then_inc(done, 1)

        def norm_b(e, st, o, x, u, root, root_at, done):
            e.wait_ge(root, root_at)
            inv = small[0:P, 16 + 4 * u + 2:16 + 4 * u + 3]
            st.add(e.reciprocal(inv, small[0:P, 16 + 4 * u + 1:16 + 4 * u + 2]))
            st.wait()
            e.tensor_scalar(o, x, small[0:P, 12:13], inv, ALU.subtract, ALU.mult).then_inc(done, 1)

        def gat_vector(e, st, L):
            e.wait_ge(L.w_in, L.since["w_in"] + L.loads)
            for k in range(L.KT):
                for r in range(2):
                    if L.batched:
                        st.wait()
                        st.add(e.tensor_tensor(L.prod, L.w_sb[:, k, 0:L.F], L.alb[r], ALU.mult))
                        st.wait()
                        st.add(e.tensor_reduce(L.w_sb[:, k, L.F + r * L.H:L.F + (r + 1) * L.H],
                                               L.prod.rearrange("p (h d) -> p h d", h=L.H), AX.X, ALU.add))
                        continue
                    for h in range(L.H):
                        st.wait()
                        c = slice(h * L.D, (h + 1) * L.D)
                        st.add(e.tensor_tensor_reduce(L.prod[:, 0:L.D], L.w_sb[:, k, c], L.alb[r][:, c], 1.0, 0.0, ALU.mult,
                                                      ALU.add, L.w_sb[:, k, L.F + r * L.H + h:L.F + r * L.H + h + 1]))
            st.wait()
            if not L.spill:
                e.memset(L.z_ones, 1.0).then_inc(L.ones, 1)

            def prep(t, u, i):
                e.wait_ge(L.x_in[u], L.since["x_in"][u] + 16 * (i + 1))
                x = L.xin[u]
                if L.prep == "ln":
                    norm_a(e, st, x, u, L.half_prep)
                    norm_b(e, st, x, x, u, L.mid, L.since["mid"] + t + 1, L.prepped)
                    return
                st.add(e.tensor_tensor(x, x, L.xbias, ALU.add))
                st.wait()
                e.tensor_scalar(L.low[u], x, 0.0, None, ALU.min).then_inc(L.half_prep, 1)
                e.wait_ge(L.mid, L.since["mid"] + t + 1)
                e.scalar_tensor_tensor(out=x, in0=L.low[u], scalar=-1.0, in1=x, op0=ALU.add, op1=ALU.max).then_inc(L.prepped, 1)

            with e.Fori(0, HT) as i:
                st.enter(i, 8 if L.prep == "ln" else 2)
                for u in range(2):
                    prep(2 * i + u, u, i)
                st.leave(HT)

            e.wait_ge(L.z_ready, L.since["z_ready"] + RING + len(L.chunks) * T)
            st.add(e.tensor_scalar(L.el2, L.elr[:, :, 0:L.H], SLOPE, None, ALU.mult))
            st.wait()
            if L.spill:
                for u in range(2):
                    e.wait_ge(L.spilled[u], L.since["spilled"][u] + 16 * HT)
                for u in range(2):
                    st.add(e.memset(L.zh[u][:, :, L.D:L.D + 1], 1.0))
                st.wait()
                e.engine_nop().then_inc(L.ones, 1)
            mx = small[0:P, 32:32 + T]
            v = [small[0:P, 44:44 + T], small[0:P, 54:54 + T]]

            def max_tile(h, u, i, t):
                if t == 0:
                    e.wait_ge(L.elb_in[u], L.since["elb_in"][u] + 16 * (i + 1))
                st.wait()
                apart(e)
                st.add(e.tensor_tensor_reduce(L.junk, L.elb[u], MB[:, t, :], 1.0, -3.0e38, ALU.add, ALU.max, mx[:, t:t + 1]))

            def max_end(h, u):
                er = L.elr[:, :, bass.ds(L.H + h, 1)].rearrange("p t o -> p (t o)")
                r = small[0:P, 64 + u * 2 * T:64 + (u + 1) * 2 * T]
                st.wait()
                st.add(e.tensor_tensor(v[0], mx, er, ALU.add))
                st.wait()
                st.add(e.scalar_tensor_tensor(out=v[1], in0=v[0], scalar=SLOPE, in1=v[0], op0=ALU.mult, op1=ALU.max))
                st.wait()
                st.add(e.tensor_tensor(r[:, 0:T], er, v[1], ALU.subtract))
                e.scalar_tensor_tensor(out=r[:, T:2 * T], in0=er, scalar=SLOPE, in1=v[1], op0=ALU.mult, op1=ALU.subtract).then_inc(L.r_ready, 1)

            def weights(h, j):
                half, s = j // T, j % T
                if s == 0:
                    e.wait_ge(L.p_free, L.since["p_free"] + 2 * h + half + 1)
                e.wait_ge(L.e_ready, L.since["e_ready"] + 2 * T * h + j + 1)
                e.tensor_tensor(L.m[j % 2], L.e[j % 2][0], L.e[j % 2][1], ALU.max).then_inc(L.e_free, 1)
                e.wait_ge(L.e_free, L.since["e_free"] + 2 + 2 * T * h + j + 1)
                e.scalar_tensor_tensor(out=Ph[half][:, s, :], in0=L.m[j % 2], scalar=2.0,
                                       in1=AT[:, s, half * HALF:(half + 1) * HALF], op0=ALU.min, op1=ALU.mult).then_inc(L.p_ready, 1)

            rd = small[0:P, 110:110 + HT]

            def finish(h, half):
                if L.batched:
                    e.wait_ge(L.ag_ready, L.since["ag_ready"] + 2 * h + half + 1)
                    sums = banks[2 + half][0:P, 0:HT * 65].rearrange("p (t f) -> p t f", t=HT)
                    o = L.og[half][:, 0:HT * 64].rearrange("p (t f) -> p t f", t=HT)
                    st.add(e.tensor_scalar(rd.rearrange("p (t o) -> p t o", o=1), sums[:, :, 64:65], TINY, None, ALU.max))
                    st.wait()
                    st.add(e.reciprocal(rd, rd))
                    st.wait()
                    e.wait_ge(L.stored[half], L.since["stored"][half] + 16 * h)
                    st.add(e.tensor_tensor(o, sums[:, :, 0:64], rd.rearrange("p (t o) -> p t o", o=1).to_broadcast([P, HT, 64]), ALU.mult))
                    st.wait()
                    e.tensor_tensor(o, o, L.z[:, half * HT:(half + 1) * HT, h, 0:64], ALU.add).then_inc(L.out_done, 1)
                    return
                for d in range(HT):
                    j = half * HT + d
                    e.wait_ge(L.ag_ready, L.since["ag_ready"] + T * h + j + 1)
                    last = banks[2 + 2 * (j % 2) + 1][0:P, 0:L.cols[1][1]]
                    den = last[:, L.cols[1][1] - 1:L.cols[1][1]]
                    st.add(e.tensor_scalar(rd[:, 0:1], den, TINY if L.add_z else 1e-16, None, ALU.max if L.add_z else ALU.add))
                    st.wait()
                    st.add(e.reciprocal(rd[:, 1:2], rd[:, 0:1]))
                    st.wait()
                    e.wait_ge(L.stored[j % 2], L.since["stored"][j % 2] + 16 * (HT * h + j // 2))
                    for c, (at, w) in enumerate(L.cols):
                        w -= c
                        src = banks[2 + 2 * (j % 2) + c][0:P, 0:w]
                        o = L.og[j % 2][:, at:at + w]
                        if L.add_z:
                            ins = e.scalar_tensor_tensor(out=o, in0=src, scalar=rd[:, 1:2], in1=L.z[:, j, at:at + w], op0=ALU.mult, op1=ALU.add)
                        else:
                            ins = e.tensor_scalar(o, src, rd[:, 1:2], None, ALU.mult)
                    ins.then_inc(L.out_done, 1)

            FIN = 3 if L.batched else 2 * HT
            for t in range(T):
                max_tile(0, 0, 0, t)
            max_end(0, 0)

            def head(h, u, first, last, i):
                at = 0
                for j in range(2 * T):
                    if not last and j in MAX_STEPS:
                        max_tile(h + 1, 1 - u, i + u, at)
                        at += 1
                        if at == T:
                            max_end(h + 1, 1 - u)
                    weights(h, j)
                    if j == T - 1 and not first:
                        finish(h - 1, 1)
                finish(h, 0)

            if L.H == 1:
                head(0, 0, True, True, 0)
                finish(0, 1)
                return
            head(0, 0, True, False, 0)
            head(1, 1, False, L.H == 2, 0)
            if L.H > 4:
                with e.Fori(1, L.H // 2 - 1) as i:
                    st.enter(i - 1, 2 * (T + 3 + 2 * FIN))
                    head(2 * i, 0, False, False, i)
                    head(2 * i + 1, 1, False, False, i)
                    st.leave(L.H // 2 - 2)
            i = L.H // 2 - 1
            head(L.H - 2, 0, False, False, i)
            head(L.H - 1, 1, False, True, i)
            finish(L.H - 1, 1)

        def moe_vector(e, st, M):
            e.wait_ge(M.c_in, 80 if M.bias else 48)

            def prep(t, u, i):
                e.wait_ge(M.x_in[u], 32 * (i + 1))
                x = M.acc[:, t, :]
                st.add(e.tensor_tensor(x, x, M.rbias, ALU.add))
                st.wait()
                e.tensor_tensor(x, x, M.rawt[u], ALU.add).then_inc(M.raw_free, 1)
                e.wait_ge(M.raw_free, 2 + t + 1)
                norm_a(e, st, x, u, M.half_prep)
                e.wait_ge(M.xt_ready, 2 * t + 1)
                norm_b(e, st, M.xn[u], x, u, M.mid, t + 1, M.prepped)

            with e.Fori(0, HT) as i:
                st.enter(i, 10)
                for u in range(2):
                    prep(2 * i + u, u, i)
                st.leave(HT)
            g, flat, col = M.g, M.gflat, M.col
            wide = lambda c: c.rearrange("p (t o) -> p t o", o=1).to_broadcast([P, T, EX])
            order = M.order.rearrange("p (o e) -> p o e", o=1).to_broadcast([P, T, EX])

            def step(ins):
                st.add(ins)
                st.wait()
            step(e.memset(M.onesq, 1.0))
            e.wait_ge(M.lg_ready, 1)
            lg = banks[2][0:P, 0:T * EX].rearrange("p (t e) -> p t e", t=T)
            step(e.tensor_reduce(col[0], lg, AX.X, ALU.max))
            e.tensor_tensor(g[0], lg, wide(col[0]), ALU.subtract).then_inc(M.exp_in, 1)
            e.wait_ge(M.exped, 1)
            step(e.tensor_reduce(col[1], g[0], AX.X, ALU.add))
            step(e.reciprocal(col[2], col[1]))
            e.tensor_tensor(g[1], g[0], wide(col[2]), ALU.mult).then_inc(M.probs, 1)
            e.wait_ge(M.probs, 1)

            def pick(p, taken):
                step(e.tensor_reduce(col[0], p, AX.X, ALU.max))
                step(e.tensor_tensor(g[2], p, wide(col[0]), ALU.is_equal))
                step(e.tensor_tensor(g[2], g[2], order, ALU.mult))
                step(e.tensor_reduce(col[1], g[2], AX.X, ALU.max))
                step(e.tensor_tensor(taken, order, wide(col[1]), ALU.is_equal))
            pick(g[1], g[3])
            step(e.scalar_tensor_tensor(out=flat[4], in0=flat[3], scalar=-2.0, in1=flat[1], op0=ALU.mult, op1=ALU.add))
            pick(g[4], g[5])
            step(e.tensor_tensor(g[3], g[3], g[5], ALU.add))
            if M.balanced:
                step(e.tensor_tensor(g[4], g[3], g[1], ALU.mult))
                e.wait_ge(M.imp_ready, 1)
                step(e.tensor_reduce(M.run, banks[3][0:P, 0:T * EX].rearrange("p (t e) -> p e t", t=T), AX.X, ALU.add))
                step(e.tensor_scalar(M.run, M.run, -1.0, DECAY_STEP, ALU.add, ALU.mult))
                step(e.tensor_scalar(M.run, M.run, 1.0, BAL_EPS, ALU.add, ALU.add))
                step(e.reciprocal(M.run, M.run))
                step(e.tensor_tensor(g[5], g[4], M.run.rearrange("p (o e) -> p o e", o=1).to_broadcast([P, T, EX]), ALU.mult))
                step(e.tensor_reduce(col[0], g[5], AX.X, ALU.add))
                step(e.reciprocal(col[1], col[0]))
                e.tensor_tensor(g[6], g[5], wide(col[1]), ALU.mult).then_inc(M.gates, 1)
            else:
                e.tensor_tensor(g[6], g[3], g[1], ALU.mult).then_inc(M.gates, 1)
            e.wait_ge(M.gates, 1)
            if M.bias:
                for t in range(T):
                    e.wait_ge(M.gb_ready, t + 1)
                    for c in range(2):
                        a = M.acc[:, t, c * (C // 2):(c + 1) * (C // 2)]
                        ins = e.tensor_tensor(a, a, banks[4 + 2 * (t % 2) + c][0:P, 0:C // 2], ALU.add)
                    ins.then_inc(M.gb_free, 1)
                e.wait_ge(M.gb_free, T)

            with e.Fori(0, EX) as x:
                for t in range(T):
                    e.wait_ge(M.y_ready, T * x + t + 1)
                    e.wait_ge(M.y_done, T * x + t + 1)
                    for c in range(2):
                        a = M.acc[:, t, c * (C // 2):(c + 1) * (C // 2)]
                        ins = e.scalar_tensor_tensor(out=a, in0=banks[2 + 2 * (t % 2) + c][0:P, 0:C // 2],
                                                     scalar=g[6][:, t, bass.ds(x, 1)], in1=a, op0=ALU.mult, op1=ALU.add)
                    ins.then_inc(M.y_done, 1)

        @block.vector
        def _(e):
            st = Step(e, v_step)
            graph_vector(e, st)
            e.wait_ge(gs["at_sb"], 3 * T)
            e.wait_ge(gs["bias"], T)
            for n in range(3):
                gat_vector(e, st, layers[n])
            add_loops(e)
            moe_vector(e, st, moes[0])
            e.wait_ge(gs["loops"], T)
            for n in range(3, 5):
                gat_vector(e, st, layers[n])
            moe_vector(e, st, moes[1])


_KEEP = ["x", "src", "dst", "L0_gnn_W0", "L0_gnn_al0", "L0_gnn_ar0", "L0_gnn_b0", "L0_gnn_W1", "L0_gnn_al1",
         "L0_gnn_ar1", "L0_gnn_b1", "L0_gnn_W2", "L0_gnn_al2", "L0_gnn_ar2", "L0_gnn_b2", "L1_gnn_W1",
         "L1_gnn_a1_src", "L1_gnn_a1_dst", "L1_gnn_b1", "L1_gnn_W2", "L1_gnn_a2_src", "L1_gnn_a2_dst",
         "L1_gnn_b2", "L1_ffn_Wg", "L1_ffn_W1", "L1_ffn_W2", "L1_ffn_b2"]


def kernel(**inputs):
    import concourse.bacc as bacc
    from concourse.bass_utils import run_bass_kernel_spmd as run

    a = {n: np.ascontiguousarray(inputs[n]) for n in _KEEP}
    a["L0_router"] = np.ascontiguousarray(np.asarray(inputs["L0_ffn_router_w"]).T)
    a["L0_w1"] = np.ascontiguousarray(np.asarray(inputs["L0_ffn_w1"]).transpose(0, 2, 1))
    a["L0_w2"] = np.ascontiguousarray(np.asarray(inputs["L0_ffn_w2"]).transpose(0, 2, 1))
    a["L1_b1"] = np.ascontiguousarray(np.asarray(inputs["L1_ffn_b1"]).reshape(EX, -1, 128).transpose(2, 0, 1))
    a["ident"] = np.eye(128, dtype=np.float32)
    a["nodes"] = np.arange(N, dtype=np.float32)
    a["order"] = np.arange(EX, 0, -1).astype(np.float32)
    a["pair_limits"] = np.stack([PAIRS - np.arange(PAIRS), 1 + np.arange(PAIRS)], 1).astype(np.float32)

    nc = bacc.Bacc("TRN2", target_bir_lowering=False, num_devices=1)
    aps = {n: nc.dram_tensor(f"in_{n}", v.shape, mybir.dt.from_np(v.dtype), kind="ExternalInput").ap() for n, v in a.items()}
    out = nc.dram_tensor("out_x", (N, C), F32, kind="ExternalOutput").ap()
    graph_transformer(nc, aps, out)
    r = run(nc, [{f"in_{n}": v for n, v in a.items()}], core_ids=[0])
    return r.results[0]["out_x"]
```

```python
from contextlib import ExitStack

import numpy as np

import concourse.bass as bass
from concourse import mybir

F32 = mybir.dt.float32
BF16 = mybir.dt.bfloat16
I16 = mybir.dt.int16
I32 = mybir.dt.int32
ALU = mybir.AluOpType
ACT = mybir.ActivationFunctionType
AX = mybir.AxisListType

N = 1250
P = 125
T = N // P
HALF = N // 2
HT = T // 2
E = 20000
EP = 125
PAIRS = E // (2 * EP)
C = 768
CK = C // 128
EX = 8
NONE = -1.0e30
TINY = 1.0e-30
EPS = 1e-5
RING = 4
SLOPE = 0.2
ST = 128
MAX_TILES = (2 * N) // ST + EX
MIN_TILES = -(-2 * N // ST)
LIST = 32
DECAY_STEP = 1.0 - 0.9
BAL_EPS = 0.01


def split(total, parts):
    out, at = [], 0
    for n in range(parts):
        w = -(-(total - at) // (parts - n))
        w += w % 2 if at + w < total else 0
        out.append((at, w))
        at += w
    return out


class Step:

    def __init__(self, eng, sem):
        self.eng, self.sem, self.base, self.k = eng, sem, 0, 0

    def add(self, instruction):
        instruction.then_inc(self.sem, 1)
        self.k += 1

    def wait(self):
        self.eng.wait_ge(self.sem, self.base + self.k)

    def enter(self, i, per_round):
        self.kept = self.base + self.k
        self.base, self.k, self.per = self.kept + i * per_round, 0, per_round

    def leave(self, rounds):
        assert self.k == self.per, (self.k, self.per)
        self.base, self.k = self.kept + rounds * self.per, 0


class Gat:

    def __init__(self, name, heads, width, k_tiles, prep, spill, add_z, signals, before):
        self.name, self.H, self.D, self.KT = name, heads, width, k_tiles
        self.F = heads * width
        self.K = k_tiles * 128
        self.prep, self.spill, self.add_z = prep, spill, add_z
        self.batched = width == 64
        self.groups = [(g, min(4, k_tiles - g)) for g in range(0, k_tiles, 4)]
        if spill:
            self.chunks = [(h * width, width) for h in range(heads)]
            self.ring = 4
        else:
            self.chunks = [(0, self.F // 2), (self.F // 2, self.F // 2)]
            self.ring = 4
        self.cols = [(0, width + 1)] if self.batched else [(0, width // 2), (width // 2, width // 2 + 1)]
        bias = prep == "elu"
        self.vectors = 48 if bias else 32
        G, NC, of = len(self.groups), len(self.chunks), [(heads + 1) // 2, heads // 2]
        banks = 2 * heads if self.batched else T * heads
        self.totals = dict(
            w_in=[16] * 2, v_in=self.vectors, scored=T, x_in=[16 * HT] * 2, x_free=T, half_prep=T, mid=T, prepped=T, tp_ready=G * T, xt_ready=G * T,
            zp_ready=NC * T, z_ready=NC * T, ones=1, spilled=[16 * HT * spill] * 2, elt_ready=3, elt_sb=3, scaled=1, el_out=16,
            elb_in=[16 * n for n in of], r_ready=heads, rt_ready=heads, rt_sb=heads, r_out=[16 * n for n in of],
            rb_in=[16 * n * (not self.batched) for n in of], relued=2 * T * heads * self.batched, t_ready=2 * T * heads * self.batched,
            er_in=[16 * n * self.batched for n in of], r2_in=[48 * heads * self.batched] * 2, z_in=[16 * n * spill for n in of], e_ready=2 * T * heads, e_free=2 * T * heads * (not self.batched),
            p_ready=2 * T * heads, p_free=2 * heads, ag_ready=banks, out_done=banks, stored=[8 * banks] * 2)
        self.since = {k: [0, 0] if isinstance(v, list) else 0 for k, v in self.totals.items()}
        if before is not None:
            for k in self.totals:
                had, more = before.since[k], before.totals[k]
                self.since[k] = [x + y for x, y in zip(had, more)] if isinstance(had, list) else had + more
        self.w_in = signals["w_in"]
        self.v_in = signals["v_in"]
        self.scored = signals["scored"]
        self.scaled = signals["scaled"]
        self.relued = signals["relued"]
        self.t_ready = signals["t_ready"]
        self.er_in = signals["er_in"]
        self.r2_in = signals["r2_in"]
        self.x_in = signals["x_in"]
        self.x_free = signals["x_free"]
        self.half_prep = signals["half_prep"]
        self.mid = signals["mid"]
        self.prepped = signals["prepped"]
        self.tp_ready = signals["tp_ready"]
        self.xt_ready = signals["xt_ready"]
        self.zp_ready = signals["zp_ready"]
        self.z_ready = signals["z_ready"]
        self.ones = signals["ones"]
        self.spilled = signals["spilled"]
        self.elt_ready = signals["elt_ready"]
        self.elt_sb = signals["elt_sb"]
        self.el_out = signals["el_out"]
        self.elb_in = signals["elb_in"]
        self.r_ready = signals["r_ready"]
        self.rt_ready = signals["rt_ready"]
        self.rt_sb = signals["rt_sb"]
        self.r_out = signals["r_out"]
        self.rb_in = signals["rb_in"]
        self.z_in = signals["z_in"]
        self.e_ready = signals["e_ready"]
        self.e_free = signals["e_free"]
        self.p_ready = signals["p_ready"]
        self.p_free = signals["p_free"]
        self.ag_ready = signals["ag_ready"]
        self.out_done = signals["out_done"]
        self.stored = signals["stored"]


class Moe:

    def __init__(self, name, inner, balanced, bias, sem):
        self.name, self.I, self.IC, self.balanced, self.bias = name, inner, inner // 128, balanced, bias
        s = lambda what, n=1: sem(f"{name}_{what}") if n == 1 else [sem(f"{name}_{what}{i}") for i in range(n)]
        self.c_in = s("c_in")
        self.x_in = s("x_in", 2)
        self.raw_free = s("raw_free")
        self.half_prep = s("half_prep")
        self.mid = s("mid")
        self.prepped = s("prepped")
        self.tp_ready = s("tp_ready")
        self.xt_ready = s("xt_ready")
        self.lg_ready = s("lg_ready")
        self.exp_in = s("exp_in")
        self.exped = s("exped")
        self.probs = s("probs")
        self.imp_ready = s("imp_ready")
        self.picked = s("picked")
        self.counts = s("counts")
        self.placed = s("placed")
        self.gates = s("gates")
        self.xn_out = s("xn_out", 2)
        self.listed = s("listed")
        self.list_in = s("list_in")
        self.rows_ready = s("rows_ready")
        self.xg_in = s("xg_in")
        self.xg_ready = s("xg_ready")
        self.xg_sb = s("xg_sb")
        self.w_in = s("w_in", 2)
        self.w_free = s("w_free")
        self.h_ready = s("h_ready")
        self.h_sb = s("h_sb")
        self.y_ready = s("y_ready")
        self.y_sb = s("y_sb")
        self.y_out = s("y_out")
        self.yg_in = s("yg_in", 4)
        self.gt_ready = s("gt_ready")
        self.gt_sb = s("gt_sb")
        self.gb_ready = s("gb_ready")
        self.gb_free = s("gb_free")
        self.y_done = s("y_done")
        self.stored = s("stored")


def graph_transformer(nc, A, out):
    ctx = ExitStack()
    with ctx:
        sems = []

        def sem(name):
            s = ctx.enter_context(nc.semaphore(name))
            sems.append(s)
            return s

        def sb(name, shape, dt=F32):
            return ctx.enter_context(nc.sbuf_tensor(name, shape, dt))

        AT = sb("edge_counts", [P, T, N], I16)
        MB = sb("no_edge_bias", [P, T, N], BF16)
        ident = sb("ident", [128, 128])
        noti = sb("not_ident", [P, P], BF16)
        elr = sb("elr", [P, T * 24])
        el2 = sb("el2", [P, T * 12])
        el8 = sb("el8", [P, T * 12])
        spread = sb("spread", [P + 1, P])
        small = sb("small", [128, 256])
        ARENA = 38400
        arena = sb("arena", [128, ARENA])

        def carve(at, parts, width):
            assert at + width <= ARENA, (at, width)
            return arena[0:parts, at:at + width]

        P_AT, P_W = 0, 12500
        Z_AT, Z_W = P_AT + P_W, 10260
        S_AT = Z_AT + Z_W
        Ph = [carve(P_AT + h * T * HALF, P, T * HALF).rearrange("p (s d) -> p s d", s=T) for h in range(2)]

        psum = ctx.enter_context(nc.psum_tensor("psum", [128, 8 * 512], F32))
        banks = [psum[:, i * 512:(i + 1) * 512] for i in range(8)]

        def dram(name, shape, dt=F32):
            return nc.dram_tensor(name, shape, dt, kind="Internal").ap()

        el_rows = dram("el_rows", (24, N))
        r_rows = dram("r_rows", (12, 2 * T, P))
        z_heads = dram("z_heads", (4, N, 512))
        raw = [dram(f"raw{i}", (N, C)) for i in range(3)] + [dram("raw3", (N, 2048)), dram("raw4", (N, C))]
        x2 = dram("x2", (N, C))
        xn_rows = dram("xn_rows", (N, C))
        y_rows = dram("y_rows", (MAX_TILES * ST, C))
        by_tile = lambda a: a.rearrange("(t p) f -> p t f", p=P)
        over = lambda row, parts=P: row.partition_broadcast(parts)

        signals = dict(
            w_in=[sem("w_in0"), sem("w_in1")],
            v_in=sem("v_in"),
            scaled=sem("scaled"),
            scored=sem("scored"),
            relued=sem("relued"),
            t_ready=sem("t_ready"),
            er_in=[sem("er_in0"), sem("er_in1")],
            r2_in=[sem("r2_in0"), sem("r2_in1")],
            x_in=[sem("x_in0"), sem("x_in1")],
            x_free=sem("x_free"),
            half_prep=sem("half_prep"),
            mid=sem("mid"),
            prepped=sem("prepped"),
            tp_ready=sem("tp_ready"),
            xt_ready=sem("xt_ready"),
            zp_ready=sem("zp_ready"),
            z_ready=sem("z_ready"),
            ones=sem("ones"),
            spilled=[sem("spilled0"), sem("spilled1")],
            elt_ready=sem("elt_ready"),
            elt_sb=sem("elt_sb"),
            el_out=sem("el_out"),
            elb_in=[sem("elb_in0"), sem("elb_in1")],
            r_ready=sem("r_ready"),
            rt_ready=sem("rt_ready"),
            rt_sb=sem("rt_sb"),
            r_out=[sem("r_out0"), sem("r_out1")],
            rb_in=[sem("rb_in0"), sem("rb_in1")],
            z_in=[sem("z_in0"), sem("z_in1")],
            e_ready=sem("e_ready"),
            e_free=sem("e_free"),
            p_ready=sem("p_ready"),
            p_free=sem("p_free"),
            ag_ready=sem("ag_ready"),
            out_done=sem("out_done"),
            stored=[sem("stored0"), sem("stored1")],
        )
        layers = []
        for args in [
            ("g0", 12, 64, CK, "ln", False, True),
            ("g1", 12, 64, CK, "elu", False, True),
            ("g2", 1, C, CK, "elu", False, True),
            ("g3", 4, 512, CK, "ln", True, False),
            ("g4", 1, C, 16, "elu", False, False),
        ]:
            layers.append(Gat(*args, signals, layers[-1] if layers else None))
        moes = [Moe("m0", 256, True, False, sem), Moe("m1", 384, False, True, sem)]
        for n, L in enumerate(layers):
            L.W, L.al, L.ar = [(A["L0_gnn_W0"], A["L0_gnn_al0"], A["L0_gnn_ar0"]),
                               (A["L0_gnn_W1"], A["L0_gnn_al1"], A["L0_gnn_ar1"]),
                               (A["L0_gnn_W2"], A["L0_gnn_al2"], A["L0_gnn_ar2"]),
                               (A["L1_gnn_W1"], A["L1_gnn_a1_src"], A["L1_gnn_a1_dst"]),
                               (A["L1_gnn_W2"], A["L1_gnn_a2_src"], A["L1_gnn_a2_dst"])][n]
            L.src = [A["x"], raw[0], raw[1], x2, raw[3]][n]
            L.src_bias = [None, A["L0_gnn_b0"], A["L0_gnn_b1"], None, A["L1_gnn_b1"]][n]
            L.dst = raw[n]
            L.w_sb = carve(P_AT, 128, L.KT * L.F).rearrange("p (k f) -> p k f", k=L.KT)
            at = S_AT
            L.xin = [carve(at + u * L.K, P, L.K) for u in range(2)]
            at += 2 * L.K
            if L.prep == "elu":
                L.low = [carve(at + u * L.K, P, L.K) for u in range(2)]
                at += 2 * L.K
            L.xbias = carve(at, P, L.K)
            at += L.K
            L.xt = [carve(at + u * L.KT * P, 128, L.KT * P).rearrange("p (k n) -> p k n", k=L.KT) for u in range(2)]
            at += 2 * L.KT * P
            L.prod = carve(at, P, L.F).rearrange("p (h d) -> p h d", h=L.H)
            L.al_b = [carve(S_AT - (2 - u) * L.F, P, L.F).rearrange("p (h d) -> p h d", h=L.H) for u in range(2)]
            at = S_AT
            L.elb = [carve(at + u * N, P, N) for u in range(2)]
            at += 2 * N
            if L.batched:
                L.erb = [carve(at + u * N, P, N) for u in range(2)]
                at += 2 * N
                L.r2 = [carve(at + half * 3 * HALF, P + 1, 3 * HALF).rearrange("p (u d) -> p u d", u=3) for half in range(2)]
                at += 6 * HALF
                L.ex = [carve(at + u * HALF, P, HALF) for u in range(4)]
                at += 4 * HALF
            else:
                L.rb = [carve(at + u * 2 * N, P, 2 * N).rearrange("p (r d) -> p r d", r=2) for u in range(2)]
                at += 4 * N
                L.e = [[carve(at + (2 * u + r) * HALF, P, HALF) for r in range(2)] for u in range(2)]
                at += 4 * HALF
                L.m = [carve(at + u * HALF, P, HALF) for u in range(2)]
                at += 2 * HALF
            L.junk = carve(at, P, HALF).bitcast(BF16)
            at += HALF
            L.og = [carve(at + u * C, P, C) for u in range(2)]
            at += 2 * C
            L.elt = carve(at, 24, N)
            L.rt = [carve(at + u * P, 2 * T, P) for u in range(2)]
            at += N
            if L.batched:
                L.z = carve(Z_AT, P, T * L.H * 65).rearrange("p (t h f) -> p t h f", t=T, h=L.H)
                L.z_ones = L.z[:, :, :, 64:65]
            elif L.spill:
                L.zh = [carve(Z_AT + u * T * 513, P, T * 513).rearrange("p (t f) -> p t f", t=T) for u in range(2)]
                L.stage = [carve(Z_AT + u * L.F, P, L.F).rearrange("p (h f) -> p h f", h=L.H) for u in range(2)]
            else:
                L.z = carve(Z_AT, P, T * (C + 1)).rearrange("p (t f) -> p t f", t=T)
                L.z_ones = L.z[:, :, C:C + 1]
            L.elr = elr[:, 0:T * 2 * L.H].rearrange("p (t h) -> p t h", t=T)
            L.el2 = el2[:, 0:T * L.H].rearrange("p (t h) -> p t h", t=T)
            L.el8 = el8[:, 0:T * L.H].rearrange("p (t h) -> p t h", t=T)
        for n, M in enumerate(moes):
            M.res, M.raw, M.raw_bias = [(A["x"], raw[2], A["L0_gnn_b2"]), (x2, raw[4], A["L1_gnn_b2"])][n]
            M.dst = [x2, out][n]
            M.router = [A["L0_router"], A["L1_ffn_Wg"]][n]
            M.w1, M.w2 = [(A["L0_w1"], A["L0_w2"]), (A["L1_ffn_W1"], A["L1_ffn_W2"])][n]
            at = P_AT
            M.w1s = [carve(at + u * CK * M.I, 128, CK * M.I).rearrange("p (k i) -> p k i", k=CK) for u in range(2)]
            at += 2 * CK * M.I
            M.w2s = [carve(at + u * M.IC * C, 128, M.IC * C).rearrange("p (k f) -> p k f", k=M.IC) for u in range(2)]
            at += 2 * M.IC * C
            M.xg = carve(at, ST, C)
            M.xgt = carve(at + C, 128, CK * ST).rearrange("p (k n) -> p k n", k=CK)
            M.y = carve(at + 2 * C, ST, C)
            M.ht = carve(at + 3 * C, 128, M.IC * ST).rearrange("p (k n) -> p k n", k=M.IC)
            at += 3 * C + M.IC * ST
            assert at <= Z_AT
            at = Z_AT
            M.acc = carve(at, P, T * C).rearrange("p (t f) -> p t f", t=T)
            at += T * C
            M.xt = carve(at, 128, CK * N).rearrange("p (k n) -> p k n", k=CK)
            M.yg = [[carve(at + (2 * v + k) * C, P, C) for k in range(2)] for v in range(4)]
            at += CK * N
            M.rawt = [carve(at + u * C, P, C) for u in range(2)]
            M.xn = [carve(at + (2 + u) * C, P, C) for u in range(2)]
            M.rbias = carve(at + 4 * C, P, C)
            at += 5 * C
            g = [carve(at + j * T * EX, P, T * EX) for j in range(8)]
            at += 8 * T * EX
            M.g = [a.rearrange("p (t e) -> p t e", t=T) for a in g]
            M.gflat = g
            M.col = [carve(at + j * T, P, T) for j in range(4)]
            at += 4 * T
            M.order = carve(at, P, EX)
            M.run = carve(at + EX, P, EX)
            at += 2 * EX
            M.steps = carve(at, P, LIST)
            at += LIST
            M.above = carve(at, P, 2 * T * LIST)
            at += 2 * T * LIST
            M.per = [carve(at + j * EX, P, EX) for j in range(4)]
            at += 4 * EX
            M.slot, M.tile, M.place = [carve(at + j * 2 * T, P, 2 * T) for j in range(3)]
            M.slot_i, M.place_i = [carve(at + (3 + j) * 2 * T, P, 2 * T).bitcast(I32) for j in range(2)]
            M.node = carve(at + 10 * T, P, T).bitcast(I32)
            M.gate = [carve(at + (11 + k) * T, P, T) for k in range(2)]
            at += 13 * T
            M.span = carve(at, 1, 2 * EX).bitcast(I32)
            at += 2 * EX
            M.list = carve(at, ST, LIST).bitcast(I32)
            M.rows = carve(at + LIST, ST, 1).bitcast(I32)
            at += LIST + 1
            M.wr = carve(at, 128, CK * EX).rearrange("p (k e) -> p k e", k=CK)
            at += CK * EX
            M.b1 = carve(at, 128, EX * M.IC).rearrange("p (e c) -> p e c", e=EX)
            at += EX * M.IC
            M.onesq = carve(at, P, P)
            M.before = carve(at + P, P, P)
            at += 2 * P
            M.list_rows = dram(M.name + "_list", (ST * LIST, 1), I32)
            M.b2 = carve(at, EX, C)
            at += C
            M.gt = [carve(at + u * P, EX, P) for u in range(2)]

        G0 = S_AT
        iota = carve(G0, P, N // 2).bitcast(I16)
        e_nat = [carve(G0 + N + j * 256, PAIRS, 2 * EP).bitcast(I32) for j in range(2)]
        e_f = [carve(G0 + N + 512 + j * 256, PAIRS, 2 * EP) for j in range(2)]
        e_t = carve(G0 + N + 1024, EP, 4 * PAIRS).rearrange("p (w a j) -> p w a j", w=2, a=2)
        lim = carve(G0 + N + 1400, PAIRS, 2)
        ge = carve(G0 + N + 1402, PAIRS, T + 1)
        has = carve(G0 + N + 1414, PAIRS, T)
        rng = carve(G0 + N + 1424, PAIRS, 2 * T)
        red = carve(G0 + N + 1444, 2 * T, 1)
        row = carve(G0 + N + 1446, 1, 2 * T)
        tab_f = carve(G0 + N + 1470, 1, 4 * T)
        tab = carve(G0 + N + 1520, 1, 4 * T).bitcast(I32)
        gjunk = carve(G0 + N + 1560, PAIRS, 2 * EP)
        oh_s = [carve(G0 + 4000 + u * 700, EP, N // 2).bitcast(BF16) for u in range(2)]
        oh_d = [carve(G0 + 5400 + u * 64, EP, 63).bitcast(BF16)[:, 0:P] for u in range(2)]
        zero = carve(G0 + 5600, EP, 300).bitcast(BF16)
        a_blk = [carve(G0 + 6300 + u * N, P, N) for u in range(2)]
        cuts = split(N, 3)
        CUT = (HALF + 1) // 2

        gs = {n: sem("graph_" + n) for n in (
            "in", "float", "et_ready", "et_sb", "rng", "rng_t", "red", "red_t", "tab", "zero",
            "oh0", "oh1", "used0", "used1", "blk_ready", "blk_sb", "bias", "at_ready", "at_sb", "loops")}
        v_step = sem("vector_step")
        y_clear = sem("y_clear")

        block = ctx.enter_context(nc.Block())

        MAX_STEPS = [0, 1, 3, 4, 6, 7, 9, 10, 12, 13]
        ROWS_AT = 15
        TURN_EARLY, ROWS_EARLY = 11, 12

        def apart(e):
            e.nop(nofuse=True)

        def graph_sync(e):
            e.dma_start(ident[:, :], A["ident"]).then_inc(gs["in"], 16)
            e.dma_start(iota, over(A["nodes"])).then_inc(gs["in"], 16)
            e.dma_start(lim, A["pair_limits"]).then_inc(gs["in"], 16)
            e.dma_start(spread[:, :], A["spread"]).then_inc(gs["in"], 16)
            for j, name in enumerate(("dst", "src")):
                e.dma_start(e_nat[j], A[name].rearrange("(j e) -> j e", j=PAIRS)).then_inc(gs["in"], 16)

        def load_projection(e, L):
            w = L.W.rearrange("(k p) f -> p k f", p=128)
            cut = L.chunks[0][1]
            e.dma_start(L.w_sb[:, :, 0:cut], w[:, :, 0:cut]).then_inc(L.w_in[0], 16)
            e.dma_start(L.w_sb[:, :, cut:L.F], w[:, :, cut:L.F]).then_inc(L.w_in[1], 16)

        def gat_sync(e, L):
            for u, r in enumerate((L.al, L.ar)):
                e.dma_start(L.al_b[u].rearrange("p h d -> p (h d)"), over(r.rearrange("h d -> (h d)"))).then_inc(L.v_in, 16)
            if L.src_bias is not None:
                e.dma_start(L.xbias, over(L.src_bias)).then_inc(L.v_in, 16)
            with e.Fori(0, HT) as i:
                for u in range(2):
                    t = 2 * i + u
                    e.wait_ge(L.x_free, L.since["x_free"] + t + 1)
                    e.dma_start(L.xin[u], by_tile(L.src)[:, t, :]).then_inc(L.x_in[u], 16)
            e.wait_ge(L.elt_sb, L.since["elt_sb"] + 3)
            e.dma_start(el_rows[0:2 * L.H, :], L.elt[0:2 * L.H, :]).then_inc(L.el_out, 16)
            e.wait_ge(L.el_out, L.since["el_out"] + 16)

            def load_el(h, u):
                e.dma_start(L.elb[u], over(el_rows[h, :])).then_inc(L.elb_in[u], 16)

            def load_er(h, u):
                e.dma_start(L.erb[u], over(el_rows[h + L.H, :])).then_inc(L.er_in[u], 16)

            def lay_r2(h, u, i, first, more):
                e.wait_ge(L.rt_sb, L.since["rt_sb"] + h + 1)
                apart(e)
                e.dma_start(r_rows[h, T:2 * T, :], L.rt[u][T:2 * T, :]).then_inc(L.r_out[u], 16)
                e.wait_ge(L.r_out[u], L.since["r_out"][u] + 16 * (i + 1))
                apart(e)
                for half in range(2):
                    if not first:
                        e.wait_ge(L.t_ready, L.since["t_ready"] + 3 + 2 * T * (h - 1) + T * (half + 1))
                        apart(e)
                    for v in range(3):
                        e.dma_start(L.r2[half][P:P + 1, v, :],
                                    r_rows[h, T + half * HT:T + (half + 1) * HT, :].rearrange("(o t) p -> o (t p)", o=1)
                                    ).then_inc(L.r2_in[half], 16)
                    if half == 0 and more:
                        load_el(h + 2, u)

            def move_r(h, u, i):
                e.wait_ge(L.rt_sb, L.since["rt_sb"] + h + 1)
                e.dma_start(r_rows[h, :, :], L.rt[u]).then_inc(L.r_out[u], 16)
                e.wait_ge(L.r_out[u], L.since["r_out"][u] + 16 * (i + 1))
                apart(e)
                e.dma_start(L.rb[u], over(r_rows[h, :, :].rearrange("(r t) p -> r (t p)", r=2))).then_inc(L.rb_in[u], 16)

            def load_z(h, u):
                e.dma_start(L.zh[u][:, :, 0:L.D], by_tile(z_heads[h, :, :])).then_inc(L.z_in[u], 16)

            if L.spill:
                for u in range(2):
                    e.wait_ge(L.spilled[u], L.since["spilled"][u] + 16 * HT)
            if L.H == 1:
                load_el(0, 0)
                move_r(0, 0, 0)
                return
            load_el(0, 0)
            load_el(1, 1)
            if L.batched:
                load_er(0, 0)
                load_er(1, 1)
                lay_r2(0, 0, 0, True, True)
                lay_r2(1, 1, 0, False, True)

                def rows_of(h, u, i, more):
                    e.wait_ge(L.relued, L.since["relued"] + 2 * T * (h - 1))
                    apart(e)
                    load_er(h, u)
                    lay_r2(h, u, i, False, more)
                with e.Fori(1, L.H // 2 - 1) as i:
                    for u in range(2):
                        rows_of(2 * i + u, u, i, True)
                for u in range(2):
                    rows_of(L.H - 2 + u, u, L.H // 2 - 1, False)
                return
            if L.spill:
                e.wait_ge(L.ones, L.since["ones"] + 1)
                load_z(0, 0)
                load_z(1, 1)
            move_r(0, 0, 0)
            move_r(1, 1, 0)
            with e.Fori(1, L.H // 2) as i:
                for u in range(2):
                    h = 2 * i + u
                    e.wait_ge(L.r_ready, L.since["r_ready"] + h - 1)
                    load_el(h, u)
                    e.wait_ge(L.p_free, L.since["p_free"] + 2 * h)
                    load_z(h, u)
                    e.wait_ge(L.e_ready, L.since["e_ready"] + 2 + 2 * T * (h - 1))
                    apart(e)
                    move_r(h, u, i)

        def span(e, M, x):
            return (e.value_load(M.span[0:1, bass.ds(x, 1)], min_val=0, max_val=MAX_TILES),
                    e.value_load(M.span[0:1, bass.ds(x + EX, 1)], min_val=0, max_val=MAX_TILES))

        def all_tiles(e, M):
            return e.value_load(M.span[0:1, 2 * EX - 1:2 * EX], min_val=1, max_val=MAX_TILES)

        def moe_sync(e, M, before, following):
            def load_w(x, u):
                e.dma_start(M.w1s[u], M.w1[x, :, :].rearrange("(k p) i -> p k i", p=128)).then_inc(M.w_in[u], 16)
                e.dma_start(M.w2s[u], M.w2[x, :, :].rearrange("(k p) f -> p k f", p=128)).then_inc(M.w_in[u], 16)

            load_w(0, 0)
            load_w(1, 1)
            e.wait_ge(y_clear, 16 * (MAX_TILES - MIN_TILES))
            previous_stored(e, before)
            e.dma_start(M.list_rows, A["no_tokens"]).then_inc(M.c_in, 16)
            e.dma_start(M.wr, M.router.rearrange("(k p) e -> p k e", p=128)).then_inc(M.c_in, 16)
            e.dma_start(M.rbias, over(M.raw_bias)).then_inc(M.c_in, 16)
            e.dma_start(M.order, over(A["order"])).then_inc(M.c_in, 16)
            e.dma_start(M.steps, over(A["steps"])).then_inc(M.c_in, 16)
            e.dma_start(M.node, A["node_ids"]).then_inc(M.c_in, 16)
            e.dma_start(M.before, A["before"]).then_inc(M.c_in, 16)
            if M.bias:
                e.dma_start(M.b1, A["L1_b1"]).then_inc(M.c_in, 16)
                e.dma_start(M.b2, A["L1_ffn_b2"]).then_inc(M.c_in, 16)
            with e.Fori(0, HT) as i:
                for u in range(2):
                    t = 2 * i + u
                    e.wait_ge(M.raw_free, t + 1)
                    e.dma_start(M.acc[:, t, :], by_tile(M.res)[:, t, :]).then_inc(M.x_in[u], 16)
                    e.dma_start(M.rawt[u], by_tile(M.raw)[:, t, :]).then_inc(M.x_in[u], 16)

            e.wait_ge(M.listed, 32 * T)
            e.dma_start(M.list, M.list_rows.rearrange("(p g) o -> p (g o)", g=LIST)).then_inc(M.list_in, 16)

            def store_outputs(x):
                lo, hi = span(e, M, x)
                with e.Fori(lo, hi) as g:
                    e.wait_ge(M.y_sb, g + 2)
                    apart(e)
                    e.dma_start(y_rows.rearrange("(g p) f -> p g f", p=ST)[:, g, :], M.y).then_inc(M.y_out, 16)

            with e.Fori(0, EX // 2 - 1) as i:
                for u in range(2):
                    store_outputs(2 * i + u)
                    e.wait_ge(M.w_free, 2 * i + u + 1)
                    apart(e)
                    load_w(2 * i + u + 2, u)
            for u in range(2):
                store_outputs(EX - 2 + u)
            if following is not None:
                n = all_tiles(e, M)
                e.wait_ge(M.w_free, EX)
                e.wait_ge(M.y_out, 16 * n + 16)
                apart(e)
                e.wait_ge(M.xg_sb, n + 1)
                apart(e)
                load_projection(e, following)
            with e.Fori(0, T) as t:
                e.wait_ge(M.y_done, t + 1)
                e.dma_start(by_tile(M.dst)[:, t, :], M.acc[:, t, :]).then_inc(M.stored, 16)
            e.wait_ge(M.stored, 16 * T)

        def previous_stored(e, L):
            for u in range(2):
                e.wait_ge(L.stored[u], L.since["stored"][u] + L.totals["stored"][u])

        def p_is_free(e, L):
            e.wait_ge(L.p_free, L.since["p_free"] + 2 + 2 * L.H)

        def gat_to_gat(e, L, following):
            p_is_free(e, L)
            load_projection(e, following)
            previous_stored(e, L)
            gat_sync(e, following)

        @block.sync
        def _(e):
            graph_sync(e)
            load_projection(e, layers[0])
            e.wait_ge(gs["at_sb"], 3 * T)
            e.wait_ge(gs["bias"], T)
            gat_sync(e, layers[0])
            gat_to_gat(e, layers[0], layers[1])
            gat_to_gat(e, layers[1], layers[2])
            p_is_free(e, layers[2])
            moe_sync(e, moes[0], layers[2], layers[3])
            gat_sync(e, layers[3])
            gat_to_gat(e, layers[3], layers[4])
            p_is_free(e, layers[4])
            moe_sync(e, moes[1], layers[4], None)

        def gat_gpsimd(e, L):
            if L.spill:
                with e.Fori(0, HT) as i:
                    for u in range(2):
                        t = 2 * i + u
                        e.wait_ge(L.z_ready, L.since["z_ready"] + RING + len(L.chunks) * (t + 1))
                        e.dma_start(z_heads[:, :, :].rearrange("h (t p) f -> p t h f", p=P)[:, t, :, :],
                                    L.stage[u]).then_inc(L.spilled[u], 16)

            def store(h):
                for half in range(2):
                    if L.batched:
                        e.wait_ge(L.out_done, L.since["out_done"] + 2 + 2 * h + half + 1)
                        e.dma_start(by_tile(L.dst)[:, half * HT:(half + 1) * HT, bass.ds(h * 64, 64)],
                                    L.og[half][:, 0:HT * 64].rearrange("p (t f) -> p t f", t=HT)).then_inc(L.stored[half], 16)
                        continue
                    for d in range(HT):
                        j = half * HT + d
                        e.wait_ge(L.out_done, L.since["out_done"] + 2 + T * h + j + 1)
                        e.dma_start(by_tile(L.dst)[:, j, bass.ds(h * L.D, L.D)],
                                    L.og[j % 2][:, 0:L.D]).then_inc(L.stored[j % 2], 16)

            if L.H == 1:
                store(0)
            else:
                with e.Fori(0, L.H) as h:
                    store(h)

        def moe_gpsimd(e, M):
            e.wait_ge(y_clear, 16 * (MAX_TILES - MIN_TILES))
            e.wait_ge(M.c_in, 144 if M.bias else 112)
            e.wait_ge(M.placed, 1)
            for t in range(T):
                for k in range(2):
                    at = bass.IndirectOffsetOnAxis(ap=M.place_i[:, k * T + t:k * T + t + 1], axis=0)
                    e.indirect_dma_start(M.list_rows[:, :], at, M.node[:, t:t + 1], None).then_inc(M.listed, 16)
            for u in range(2):
                e.wait_ge(M.xn_out[u], 16 + 16 * HT)
            e.wait_ge(M.list_in, 16)

            def gather(g):
                e.tensor_copy(M.rows, M.list[:, bass.ds(g, 1)]).then_inc(M.rows_ready, 1)
                e.wait_ge(M.rows_ready, g + 1)
                apart(e)
                at = bass.IndirectOffsetOnAxis(ap=M.rows, axis=0)
                e.indirect_dma_start(M.xg[:, :], None, xn_rows[:, :], at).then_inc(M.xg_in, 16)
            gather(0)
            n = all_tiles(e, M)
            with e.Fori(0, n) as g:
                e.wait_ge(M.xg_ready, g + 1)
                apart(e)
                gather(g + 1)
            e.wait_ge(M.y_out, 16 * n + 16)
            apart(e)
            for t in range(T):
                if t >= 4:
                    e.wait_ge(M.y_done, t - 3)
                for k in range(2):
                    at = bass.IndirectOffsetOnAxis(ap=M.slot_i[:, k * T + t:k * T + t + 1], axis=0)
                    e.indirect_dma_start(M.yg[t % 4][k], None, y_rows[:, :], at).then_inc(M.yg_in[t % 4], 16)

        @block.gpsimd
        def _(e):
            for u in range(2):
                e.sem_inc(gs[f"oh{u}"], PAIRS)
                e.sem_inc(gs[f"used{u}"], PAIRS + 1)
            L = layers[0]
            e.sem_inc(L.x_free, 2)
            e.sem_inc(L.e_free, 2)
            e.sem_inc(L.p_free, 2)
            e.sem_inc(L.p_ready, 4)
            e.sem_inc(L.t_ready, 3)
            e.sem_inc(L.scored, 2)
            e.sem_inc(L.out_done, 2)
            with e.Fori(MIN_TILES, MAX_TILES) as g:
                e.dma_start(y_rows.rearrange("(g p) f -> p g f", p=ST)[:, g, :], A["no_outputs"]).then_inc(y_clear, 16)
            for M in moes:
                e.sem_inc(M.raw_free, 2)
                e.sem_inc(M.y_sb, 1)
                e.sem_inc(M.y_out, 16)
            for L in layers[0:3]:
                gat_gpsimd(e, L)
            moe_gpsimd(e, moes[0])
            for L in layers[3:5]:
                gat_gpsimd(e, L)
            moe_gpsimd(e, moes[1])

        def graph_tensor(e):
            e.wait_ge(gs["float"], 2)
            for w in range(2):
                for a in range(2):
                    ins = e.transpose(banks[7][0:EP, (2 * w + a) * PAIRS:(2 * w + a + 1) * PAIRS],
                                      e_f[w][:, a * EP:(a + 1) * EP], ident[0:PAIRS, 0:PAIRS])
            ins.then_inc(gs["et_ready"], 1)
            e.wait_ge(gs["rng"], 1)
            e.wait_ge(gs["et_sb"], 1)
            e.transpose(banks[7][0:2 * T, 0:PAIRS], rng, ident[0:PAIRS, 0:PAIRS]).then_inc(gs["rng_t"], 1)
            e.wait_ge(gs["red"], 1)
            e.transpose(banks[6][0:1, 0:2 * T], red, ident[0:2 * T, 0:2 * T]).then_inc(gs["red_t"], 1)
            e.wait_ge(gs["tab"], 1)
            e.wait_ge(gs["zero"], 1)
            for b in range(T):
                lo = e.value_load(tab[0:1, b:b + 1], min_val=0, max_val=PAIRS - 1)
                hi = e.value_load(tab[0:1, T + b:T + b + 1], min_val=1, max_val=PAIRS)
                before = e.value_load(tab[0:1, 2 * T + b:2 * T + b + 1], min_val=0, max_val=T * PAIRS)
                acc = [banks[3 * (b % 2) + c][0:P, 0:w] for c, (_, w) in enumerate(cuts)]
                if b >= 2:
                    e.wait_ge(gs["blk_sb"], b - 1)
                for c, (_, w) in enumerate(cuts):
                    e.matmul(acc[c], zero[:, 0:P], zero[:, P:P + w], start=True, stop=False)
                with e.Fori(lo, hi) as j:
                    for u in range(2):
                        e.wait_ge(gs[f"oh{u}"], before + j + 1)
                        for c, (at, w) in enumerate(cuts):
                            ins = e.matmul(acc[c], oh_d[u], oh_s[u][:, at:at + w], start=False, stop=False)
                        ins.then_inc(gs[f"used{u}"], 1)
                for c, (_, w) in enumerate(cuts):
                    ins = e.matmul(acc[c], zero[:, 0:P], zero[:, P:P + w], start=False, stop=True)
                ins.then_inc(gs["blk_ready"], 1)
                if b >= 1:
                    graph_turn(e, b - 1)
            graph_turn(e, T - 1)

        def graph_turn(e, b):
            e.wait_ge(gs["blk_sb"], b + 1)
            for g in range(3):
                if 3 * b + g >= 2:
                    e.wait_ge(gs["at_sb"], 3 * b + g - 1)
                bank = banks[6 + (3 * b + g) % 2]
                for s in range(4 * g, min(T, 4 * g + 4)):
                    ins = e.transpose(bank[0:P, (s % 4) * P:(s % 4 + 1) * P], a_blk[b % 2][:, s * P:(s + 1) * P],
                                      ident[0:P, 0:P])
                ins.then_inc(gs["at_ready"], 1)

        def two_ahead(e, body):
            with e.Fori(0, HT - 1) as i:
                for u in range(2):
                    body(2 * i + u, u, False)
            for t in (T - 2, T - 1):
                body(t, t % 2, True)

        def block_exponents(j):
            mid = (5 + 2 * (j % 2)) * 512
            return psum[0:P, mid - CUT:mid - CUT + HALF]

        def gat_tensor(e, L):
            G, NC = len(L.groups), len(L.chunks)

            def transposes(t, u):
                e.wait_ge(L.prepped, L.since["prepped"] + t + 1)
                for g, (k0, n) in enumerate(L.groups):
                    e.wait_ge(L.xt_ready, L.since["xt_ready"] + G * t + g + 1)
                    for k in range(n):
                        ins = e.transpose(banks[g % 2][:, k * P:(k + 1) * P],
                                          L.xin[u][:, (k0 + k) * 128:(k0 + k + 1) * 128], ident[0:P, 0:P])
                    ins.then_inc(L.tp_ready, 1)

            def project(t, u):
                e.wait_ge(L.xt_ready, L.since["xt_ready"] + 2 + G * (t + 1))
                for c, (at, w) in enumerate(L.chunks):
                    bank = banks[2 + (u * NC + c) % L.ring]
                    e.wait_ge(L.z_ready, L.since["z_ready"] + RING - L.ring + NC * t + c + 1)
                    for k in range(L.KT):
                        ins = e.matmul(bank[0:P, 0:w], L.xt[u][:, k, :], L.w_sb[:, k, at:at + w],
                                       start=(k == 0), stop=(k == L.KT - 1))
                        if c == 0 and k == 0:
                            ins.then_inc(L.x_free, 1)
                    ins.then_inc(L.zp_ready, 1)

            transposes(0, 0)
            for c in range(2):
                e.wait_ge(L.w_in[c], L.since["w_in"][c] + 16)

            def both(t, u, last):
                if not (last and u == 1):
                    transposes(t + 1, 1 - u)
                project(t, u)
            two_ahead(e, both)

            for g in range(3):
                if g == 0:
                    e.wait_ge(L.scored, L.since["scored"] + 2 + T)
                    e.wait_ge(L.z_ready, L.since["z_ready"] + RING + NC * T)
                if g == 2:
                    e.wait_ge(L.elt_sb, L.since["elt_sb"] + 1)
                for t in range(4 * g, min(T, 4 * g + 4)):
                    ins = e.transpose(banks[g % 2][0:2 * L.H, (t % 4) * P:(t % 4 + 1) * P], L.elr[:, t, :], ident[0:P, 0:P])
                ins.then_inc(L.elt_ready, 1)

            def turn_r(h, u):
                e.wait_ge(L.r_ready, L.since["r_ready"] + h + 1)
                if not isinstance(h, int) or h > 0:
                    e.wait_ge(L.rt_sb, L.since["rt_sb"] + h)
                e.transpose(banks[0][0:2 * T, 0:P], small[0:P, 64 + u * 2 * T:64 + (u + 1) * 2 * T], ident[0:P, 0:P]).then_inc(L.rt_ready, 1)

            def aggregate(h, u, i):
                if L.spill:
                    e.wait_ge(L.z_in[u], L.since["z_in"][u] + 16 * (i + 1))
                for half in range(2):
                    for d in range(HT):
                        j = half * HT + d
                        e.wait_ge(L.out_done, L.since["out_done"] + T * h + j + 1)
                        for c, (at, w) in enumerate(L.cols):
                            for s in range(T):
                                if d == 0 and c == 0:
                                    e.wait_ge(L.p_ready, L.since["p_ready"] + 4 + 2 * T * h + half * T + s + 1)
                                ins = e.matmul(banks[2 + 2 * (j % 2) + c][0:P, 0:w], Ph[half][:, s, d * P:(d + 1) * P],
                                               (L.zh[u] if L.spill else L.z)[:, s, at:at + w], start=(s == 0), stop=(s == T - 1))
                        ins.then_inc(L.ag_ready, 1)
                    e.matmul(banks[6][0:1, 0:1], ident[:, 0:1], ident[:, 0:1], start=True, stop=True).then_inc(L.p_free, 1)

            def exponents(h, j):
                half, s = j // T, j % T
                if s == 0:
                    e.wait_ge(L.r2_in[half], L.since["r2_in"][half] + 48 * (h + 1))
                e.wait_ge(L.relued, L.since["relued"] + 2 * T * h + j + 1)
                e.wait_ge(L.e_ready, L.since["e_ready"] + 2 * T * h + j + 1)
                o = block_exponents(j)
                for at, to in ((0, CUT), (CUT, HALF)):
                    ins = e.matmul(o[:, at:to], spread[:, :], L.r2[half][:, s % 3, at:to], start=True, stop=True)
                ins.then_inc(L.t_ready, 1)

            def sum_tile(h, half, d, part):
                if d == 0 and part == 0:
                    e.wait_ge(L.out_done, L.since["out_done"] + 2 * h + half + 1)
                if d == 0:
                    e.wait_ge(L.p_ready, L.since["p_ready"] + 4 + 2 * T * h + half * T + (part + 1) * HT)
                for s in range(part * HT, (part + 1) * HT):
                    ins = e.matmul(banks[2 + half][0:P, d * 65:(d + 1) * 65], Ph[half][:, s, d * P:(d + 1) * P], L.z[:, s, h, :],
                                   start=(s == 0), stop=(s == T - 1))
                if d == HT - 1 and part == 1:
                    ins.then_inc(L.ag_ready, 1)
                    e.matmul(banks[1][0:1, 0:1], ident[:, 0:1], ident[:, 0:1], start=True, stop=True).then_inc(L.p_free, 1)

            def batched_head(h, u, first, last):
                for j in range(2 * T):
                    half, s = j // T, j % T
                    exponents(h, j)
                    if not (first and half == 0):
                        sum_tile(h if half else h - 1, 1 - half, s // 2, s % 2)
                    if j == TURN_EARLY and not last:
                        turn_r(h + 1, 1 - u)

            turn_r(0, 0)
            if L.batched:
                batched_head(0, 0, True, False)
                batched_head(1, 1, False, False)
                with e.Fori(1, L.H // 2 - 1) as i:
                    for u in range(2):
                        batched_head(2 * i + u, u, False, False)
                batched_head(L.H - 2, 0, False, False)
                batched_head(L.H - 1, 1, False, True)
                for d in range(HT):
                    for part in range(2):
                        sum_tile(L.H - 1, 1, d, part)
                return
            if L.H == 1:
                aggregate(0, 0, 0)
                return
            with e.Fori(0, L.H // 2 - 1) as i:
                turn_r(2 * i + 1, 1)
                aggregate(2 * i, 0, i)
                turn_r(2 * i + 2, 0)
                aggregate(2 * i + 1, 1, i)
            turn_r(L.H - 1, 1)
            aggregate(L.H - 2, 0, L.H // 2 - 1)
            aggregate(L.H - 1, 1, L.H // 2 - 1)


        def moe_tensor(e, M):
            e.wait_ge(M.c_in, 144 if M.bias else 112)

            def transposes(t, u, _):
                e.wait_ge(M.prepped, t + 1)
                for g in range(2):
                    e.wait_ge(M.xt_ready, 2 * t + g + 2)
                    for k in range(4 * g, min(CK, 4 * g + 4)):
                        ins = e.transpose(banks[g][:, (k % 4) * P:(k % 4 + 1) * P],
                                          M.xn[u][:, k * 128:(k + 1) * 128], ident[0:P, 0:P])
                    ins.then_inc(M.tp_ready, 1)
            two_ahead(e, transposes)
            for t in range(T):
                e.wait_ge(M.xt_ready, 3 + 2 * (t + 1))
                for k in range(CK):
                    ins = e.matmul(banks[2][0:P, t * EX:(t + 1) * EX], M.xt[:, k, t * P:(t + 1) * P], M.wr[:, k, :],
                                   start=(k == 0), stop=(k == CK - 1))
            ins.then_inc(M.lg_ready, 1)

            if M.balanced:
                e.wait_ge(M.probs, 1)
                e.matmul(banks[3][0:P, 0:T * EX], M.onesq, M.gflat[1], start=True, stop=True).then_inc(M.imp_ready, 1)
            e.wait_ge(M.picked, 1)
            e.matmul(banks[4][0:P, 0:T * EX], M.before, M.gflat[7], start=True, stop=True)
            e.matmul(banks[4][0:P, T * EX:2 * T * EX], M.onesq, M.gflat[7], start=True, stop=True).then_inc(M.counts, 1)

            def transposes_of(g):
                e.wait_ge(M.xg_in, 16 * g + 16)
                apart(e)
                for k in range(CK):
                    ins = e.transpose(banks[k // 4][:, (k % 4) * ST:(k % 4 + 1) * ST], M.xg[:, k * 128:(k + 1) * 128], ident[:, :])
                ins.then_inc(M.xg_ready, 1)
            e.wait_ge(M.gates, 1)
            transposes_of(0)

            def expert(x, u, i):
                e.wait_ge(M.w_in[u], 32 * (i + 1))
                lo, hi = span(e, M, x)
                with e.Fori(lo, hi) as g:
                    e.wait_ge(M.xg_sb, g + 1)
                    apart(e)
                    for ci in range(M.IC):
                        for k in range(CK):
                            ins = e.matmul(banks[6][:, ci * ST:(ci + 1) * ST], M.w1s[u][:, k, ci * 128:(ci + 1) * 128], M.xgt[:, k, :],
                                           start=(k == 0), stop=(k == CK - 1))
                    ins.then_inc(M.h_ready, 1)
                    transposes_of(g + 1)
                    e.wait_ge(M.h_sb, g + 1)
                    e.wait_ge(M.y_sb, g + 1)
                    apart(e)
                    for c in range(2):
                        for ci in range(M.IC):
                            ins = e.matmul(banks[2 + c][:, 0:C // 2], M.ht[:, ci, :], M.w2s[u][:, ci, c * (C // 2):(c + 1) * (C // 2)],
                                           start=(ci == 0), stop=(ci == M.IC - 1))
                    ins.then_inc(M.y_ready, 1)
                e.matmul(banks[7][0:1, 0:1], ident[:, 0:1], ident[:, 0:1], start=True, stop=True).then_inc(M.w_free, 1)
            with e.Fori(0, EX // 2) as i:
                for u in range(2):
                    expert(2 * i + u, u, i)
            if M.bias:
                n = all_tiles(e, M)
                e.wait_ge(M.xg_sb, n + 1)
                apart(e)
                for t in range(T):
                    if t >= 2:
                        e.wait_ge(M.gt_sb, t - 1)
                    e.transpose(banks[t % 2][0:EX, 0:P], M.g[6][:, t, :], ident[0:P, 0:P]).then_inc(M.gt_ready, 1)
                    e.wait_ge(M.gt_sb, t + 1)
                    if t >= 2:
                        e.wait_ge(M.gb_free, t - 1)
                    for c in range(2):
                        ins = e.matmul(banks[4 + 2 * (t % 2) + c][0:P, 0:C // 2], M.gt[t % 2], M.b2[:, c * (C // 2):(c + 1) * (C // 2)],
                                       start=True, stop=True)
                    ins.then_inc(M.gb_ready, 1)

        @block.tensor
        def _(e):
            graph_tensor(e)
            for n in range(3):
                gat_tensor(e, layers[n])
            moe_tensor(e, moes[0])
            for n in range(3, 5):
                gat_tensor(e, layers[n])
            moe_tensor(e, moes[1])

        def graph_scalar(e):
            e.wait_ge(gs["et_ready"], 1)
            e.activation(e_t.rearrange("p w a j -> p (w a j)"), banks[7][0:EP, 0:4 * PAIRS], ACT.Copy).then_inc(gs["et_sb"], 1)

            def turned(b):
                for g in range(3):
                    e.wait_ge(gs["at_ready"], 3 * b + g + 1)
                    n = min(4, T - 4 * g)
                    e.activation(AT[:, 4 * g:4 * g + n, b * P:(b + 1) * P],
                                 banks[6 + (3 * b + g) % 2][0:P, 0:n * P].rearrange("p (s d) -> p s d", s=n),
                                 ACT.Copy).then_inc(gs["at_sb"], 1)
            for b in range(T):
                e.wait_ge(gs["blk_ready"], b + 1)
                if b >= 2:
                    e.wait_ge(gs["bias"], b - 1)
                for c, (at, w) in enumerate(cuts):
                    ins = e.activation(a_blk[b % 2][:, at:at + w], banks[3 * (b % 2) + c][0:P, 0:w], ACT.Copy)
                ins.then_inc(gs["blk_sb"], 1)
                if b >= 1:
                    turned(b - 1)
            turned(T - 1)

        def gat_scalar(e, L):
            G, NC = len(L.groups), len(L.chunks)
            if L is layers[0]:
                e.sem_inc(L.xt_ready, 2)
                e.sem_inc(L.z_ready, RING)
                e.sem_inc(L.e_ready, 2)

            def mid(t, u):
                e.wait_ge(L.half_prep, L.since["half_prep"] + t + 1)
                if L.prep == "ln":
                    e.activation(small[0:P, 16 + 4 * u + 1:16 + 4 * u + 2], small[0:P, 16 + 4 * u:16 + 4 * u + 1], ACT.Sqrt).then_inc(L.mid, 1)
                else:
                    e.activation(L.low[u], L.low[u], ACT.Exp).then_inc(L.mid, 1)

            def turned(t, u):
                for g, (k0, n) in enumerate(L.groups):
                    e.wait_ge(L.tp_ready, L.since["tp_ready"] + G * t + g + 1)
                    e.activation(L.xt[u][:, k0:k0 + n, :], banks[g % 2][:, 0:n * P].rearrange("p (k n) -> p k n", k=n),
                                 ACT.Copy).then_inc(L.xt_ready, 1)

            def keep(t, u, i):
                for c, (at, w) in enumerate(L.chunks):
                    bank = banks[2 + (u * NC + c) % L.ring]
                    e.wait_ge(L.zp_ready, L.since["zp_ready"] + NC * t + c + 1)
                    if L.spill and c == 0:
                        e.wait_ge(L.scored, L.since["scored"] + t + 1)
                    if L.spill and c == 0 and not (isinstance(i, int) and i == 0):
                        e.wait_ge(L.spilled[u], L.since["spilled"][u] + 16 * i)
                    apart(e)
                    if L.batched:
                        o = L.z[:, t, at // 64:(at + w) // 64, 0:64]
                        s = bank[0:P, 0:w].rearrange("p (h f) -> p h f", f=64)
                    elif L.spill:
                        o, s = L.stage[u][:, c, :], bank[0:P, 0:w]
                    else:
                        o, s = L.z[:, t, at:at + w], bank[0:P, 0:w]
                    ins = e.activation(o, s, ACT.Copy)
                    ins.then_inc(L.z_ready, 1)

            mid(0, 0)
            mid(1, 1)
            turned(0, 0)
            def around(i):
                for u in range(2):
                    t = 2 * i + u
                    turned(t + 1, 1 - u)
                    mid(t + 2, u)
                    keep(t, u, i)
            if L.spill:
                around(0)
            with e.Fori(1 if L.spill else 0, HT - 1) as i:
                around(i)
            turned(T - 1, 1)
            keep(T - 2, 0, HT - 1)
            keep(T - 1, 1, HT - 1)
            for g in range(3):
                n = min(4, T - 4 * g)
                e.wait_ge(L.elt_ready, L.since["elt_ready"] + g + 1)
                e.activation(L.elt[0:2 * L.H, 4 * g * P:(4 * g + n) * P], banks[g % 2][0:2 * L.H, 0:n * P], ACT.Copy).then_inc(L.elt_sb, 1)
            e.wait_ge(L.el_out, L.since["el_out"] + 16)
            e.wait_ge(L.scaled, L.since["scaled"] + 1)

            def rows(h, u):
                e.wait_ge(L.rt_ready, L.since["rt_ready"] + h + 1)
                e.activation(L.rt[u], banks[0][0:2 * T, 0:P], ACT.Copy).then_inc(L.rt_sb, 1)

            def exps(h, u, i, js):
                for j in js:
                    half, s = j // T, j % T
                    if j == 0:
                        e.wait_ge(L.rb_in[u], L.since["rb_in"][u] + 16 * (i + 1))
                    e.wait_ge(L.e_free, L.since["e_free"] + 2 * T * h + j + 1)
                    apart(e)
                    cols = slice(half * HALF, (half + 1) * HALF)
                    e.activation(L.e[j % 2][0], L.rb[u][:, 0, cols], ACT.Exp, bias=L.elr[:, s, bass.ds(h, 1)])
                    e.activation(L.e[j % 2][1], L.rb[u][:, 1, cols], ACT.Exp, bias=L.el2[:, s, bass.ds(h, 1)]).then_inc(L.e_ready, 1)

            def relu(h, u, i, j):
                half, s = j // T, j % T
                if j == 0:
                    e.wait_ge(L.er_in[u], L.since["er_in"][u] + 16 * (i + 1))
                e.wait_ge(L.t_ready, L.since["t_ready"] + 2 * T * h + j + 1)
                apart(e)
                e.activation(L.r2[half][0:P, s % 3, :], L.erb[u][:, half * HALF:(half + 1) * HALF], ACT.Relu,
                             bias=L.el8[:, s, bass.ds(h, 1)], scale=1.0 - SLOPE).then_inc(L.relued, 1)

            def exponentials(h, j):
                e.wait_ge(L.t_ready, L.since["t_ready"] + 3 + 2 * T * h + j + 1)
                e.wait_ge(L.p_ready, L.since["p_ready"] + 2 * T * h + j + 1)
                apart(e)
                e.activation(L.ex[j % 4], block_exponents(j), ACT.Exp, bias=L.el2[:, j % T, bass.ds(h, 1)]).then_inc(L.e_ready, 1)

            def batched_head(h, u, i, last):
                for j in range(2 * T):
                    exponentials(h, j)
                    if j == ROWS_EARLY and not last:
                        rows(h + 1, 1 - u)
                    if j + 3 < 2 * T:
                        relu(h, u, i, j + 3)
                    elif not last:
                        relu(h + 1, 1 - u, i + u, j + 3 - 2 * T)

            if L.batched:
                relu(0, 0, 0, 0)
                relu(0, 0, 0, 1)
                relu(0, 0, 0, 2)
            rows(0, 0)
            if L.batched:
                with e.Fori(0, L.H // 2 - 1) as i:
                    for u in range(2):
                        batched_head(2 * i + u, u, i, False)
                batched_head(L.H - 2, 0, L.H // 2 - 1, False)
                batched_head(L.H - 1, 1, L.H // 2 - 1, True)
                return
            if L.H == 1:
                exps(0, 0, 0, range(2 * T))
                return
            with e.Fori(0, L.H // 2 - 1) as i:
                for u in range(2):
                    h = 2 * i + u
                    exps(h, u, i, range(ROWS_AT))
                    rows(h + 1, 1 - u)
                    exps(h, u, i, range(ROWS_AT, 2 * T))
            i = L.H // 2 - 1
            exps(L.H - 2, 0, i, range(ROWS_AT))
            rows(L.H - 1, 1)
            exps(L.H - 2, 0, i, range(ROWS_AT, 2 * T))
            exps(L.H - 1, 1, i, range(2 * T))

        def moe_scalar(e, M):
            e.sem_inc(M.xt_ready, 3)
            for u in range(2):
                e.sem_inc(M.xn_out[u], 16)

            def prep(t, u, _):
                e.wait_ge(M.half_prep, t + 1)
                e.activation(small[0:P, 16 + 4 * u + 1:16 + 4 * u + 2], small[0:P, 16 + 4 * u:16 + 4 * u + 1], ACT.Sqrt).then_inc(M.mid, 1)
                for g in range(2):
                    n = min(4, CK - 4 * g)
                    e.wait_ge(M.tp_ready, 2 * t + g + 1)
                    apart(e)
                    e.activation(M.xt[:, 4 * g:4 * g + n, bass.ds(t * P, P)],
                                 banks[g][:, 0:n * P].rearrange("p (k n) -> p k n", k=n), ACT.Copy).then_inc(M.xt_ready, 1)
                e.dma_start(by_tile(xn_rows)[:, t, :], M.xn[u]).then_inc(M.xn_out[u], 16)
            two_ahead(e, prep)
            e.wait_ge(M.exp_in, 1)
            e.activation(M.gflat[0], M.gflat[0], ACT.Exp).then_inc(M.exped, 1)

            def keep_rows(g):
                e.wait_ge(M.xg_ready, g + 1)
                apart(e)
                e.activation(M.xgt[:, 0:4, :], banks[0][:, 0:4 * ST].rearrange("p (k n) -> p k n", k=4), ACT.Copy)
                e.activation(M.xgt[:, 4:CK, :], banks[1][:, 0:(CK - 4) * ST].rearrange("p (k n) -> p k n", k=CK - 4),
                             ACT.Copy).then_inc(M.xg_sb, 1)
            e.wait_ge(M.placed, 1)
            keep_rows(0)

            def expert(x):
                lo, hi = span(e, M, x)
                with e.Fori(lo, hi) as g:
                    e.wait_ge(M.h_ready, g + 1)
                    apart(e)
                    for ci in range(M.IC):
                        src = banks[6][:, ci * ST:(ci + 1) * ST]
                        if M.bias:
                            ins = e.activation(M.ht[:, ci, :], src, ACT.Relu, bias=M.b1[:, bass.ds(x, 1), ci])
                        else:
                            ins = e.activation(M.ht[:, ci, :], src, ACT.Silu)
                    ins.then_inc(M.h_sb, 1)
                    keep_rows(g + 1)
            with e.Fori(0, EX) as x:
                expert(x)
            if M.bias:
                for t in range(T):
                    e.wait_ge(M.gt_ready, t + 1)
                    if t >= 2:
                        e.wait_ge(M.gb_ready, t - 1)
                    e.activation(M.gt[t % 2], banks[t % 2][0:EX, 0:P], ACT.Copy).then_inc(M.gt_sb, 1)

        @block.scalar
        def _(e):
            graph_scalar(e)
            for n in range(3):
                gat_scalar(e, layers[n])
            moe_scalar(e, moes[0])
            for n in range(3, 5):
                gat_scalar(e, layers[n])
            moe_scalar(e, moes[1])

        def graph_vector(e, st):
            e.wait_ge(gs["in"], 16 * 6)
            st.add(e.memset(zero, 0.0))
            for w in range(2):
                e.tensor_copy(e_f[w], e_nat[w]).then_inc(gs["float"], 1)
            e.wait_ge(gs["float"], 2)
            for b in range(T + 1):
                st.wait()
                st.add(e.tensor_scalar(gjunk, e_f[0], b * P - 0.5, None, ALU.is_ge, ALU.add, accum_out=ge[:, b:b + 1]))
            st.wait()
            st.add(e.tensor_tensor(has, ge[:, 0:T], ge[:, 1:T + 1], ALU.not_equal))
            st.wait()
            st.add(e.tensor_scalar(rng[:, 0:T], has, lim[:, 0:1], None, ALU.mult))
            e.tensor_scalar(rng[:, T:2 * T], has, lim[:, 1:2], None, ALU.mult).then_inc(gs["rng"], 1)
            e.wait_ge(gs["rng_t"], 1)
            e.tensor_reduce(red, banks[7][0:2 * T, 0:PAIRS], AX.X, ALU.max).then_inc(gs["red"], 1)
            e.wait_ge(gs["red_t"], 1)
            st.add(e.tensor_scalar(row[:, 0:T], banks[6][0:1, 0:T], -1.0, float(PAIRS), ALU.mult, ALU.add))
            st.wait()
            st.add(e.tensor_scalar(tab_f[:, 0:T], row[:, 0:T], float(PAIRS - 1), None, ALU.min))
            st.wait()
            st.add(e.tensor_scalar(row[:, T:2 * T], tab_f[:, 0:T], 1.0, None, ALU.add))
            st.wait()
            st.add(e.tensor_tensor(tab_f[:, T:2 * T], row[:, T:2 * T], banks[6][0:1, T:2 * T], ALU.max))
            st.wait()
            st.add(e.tensor_tensor(row[:, 0:T], tab_f[:, T:2 * T], tab_f[:, 0:T], ALU.subtract))
            st.add(e.memset(tab_f[:, 3 * T:4 * T], 0.0))
            st.wait()
            for b in range(1, T):
                st.add(e.tensor_tensor(tab_f[:, 3 * T + b:3 * T + b + 1], tab_f[:, 3 * T + b - 1:3 * T + b], row[:, b - 1:b], ALU.add))
                st.wait()
            st.add(e.tensor_tensor(row[:, 0:T], tab_f[:, 3 * T:4 * T], tab_f[:, 0:T], ALU.subtract))
            st.wait()
            st.add(e.tensor_scalar(tab_f[:, 2 * T:3 * T], row[:, 0:T], float(PAIRS), None, ALU.add))
            st.wait()
            e.tensor_copy(tab, tab_f).then_inc(gs["tab"], 1)
            st.add(e.tensor_scalar(noti[:, :], ident[0:P, 0:P], 0.0, None, ALU.is_equal))
            e.wait_ge(gs["et_sb"], 1)
            e.wait_ge(gs["tab"], 1)
            st.wait()
            e.engine_nop().then_inc(gs["zero"], 1)
            for b in range(T):
                lo = e.value_load(tab[0:1, b:b + 1], min_val=0, max_val=PAIRS - 1)
                hi = e.value_load(tab[0:1, T + b:T + b + 1], min_val=1, max_val=PAIRS)
                before = e.value_load(tab[0:1, 2 * T + b:2 * T + b + 1], min_val=0, max_val=T * PAIRS)
                with e.Fori(lo, hi) as j:
                    for u in range(2):
                        e.wait_ge(gs[f"used{u}"], before + j + 1)
                        e.tensor_scalar(oh_d[u], iota[:, b * P:(b + 1) * P], e_t[:, 0, u, bass.ds(j, 1)], None, ALU.is_equal)
                        e.tensor_scalar(oh_s[u], iota, e_t[:, 1, u, bass.ds(j, 1)], None, ALU.is_equal).then_inc(gs[f"oh{u}"], 1)
                if b >= 1:
                    graph_bias(e, b - 1)
            graph_bias(e, T - 1)

        def graph_bias(e, b):
            e.wait_ge(gs["blk_sb"], b + 1)
            e.wait_ge(gs["at_ready"], 3 * (b + 1))
            e.tensor_scalar(MB[:, b, :], a_blk[b % 2], 0.0, NONE, ALU.is_equal, ALU.mult).then_inc(gs["bias"], 1)

        def add_loops(e):
            for t in range(T):
                e.tensor_tensor(AT[:, t, t * P:(t + 1) * P], AT[:, t, t * P:(t + 1) * P], ident[0:P, 0:P], ALU.add)
                e.tensor_tensor(MB[:, t, t * P:(t + 1) * P], MB[:, t, t * P:(t + 1) * P], noti[:, :], ALU.mult).then_inc(gs["loops"], 1)

        def norm_a(e, st, x, u, done):
            apart(e)
            stats = small[0:P, 0:12].rearrange("p (a b) -> p a b", a=2)
            for a in range(2):
                st.add(e.bn_stats(stats[:, a, :], x[:, a * (C // 2):(a + 1) * (C // 2)]))
            st.wait()
            apart(e)
            st.add(e.bn_aggr(small[0:P, 12:14], stats))
            st.wait()
            e.tensor_scalar(small[0:P, 16 + 4 * u:16 + 4 * u + 1], small[0:P, 13:14], EPS, None, ALU.add).then_inc(done, 1)

        def norm_b(e, st, o, x, u, root, root_at, done):
            e.wait_ge(root, root_at)
            inv = small[0:P, 16 + 4 * u + 2:16 + 4 * u + 3]
            st.add(e.reciprocal(inv, small[0:P, 16 + 4 * u + 1:16 + 4 * u + 2]))
            st.wait()
            e.tensor_scalar(o, x, small[0:P, 12:13], inv, ALU.subtract, ALU.mult).then_inc(done, 1)

        def gat_vector(e, st, L):
            e.wait_ge(L.v_in, L.since["v_in"] + L.vectors)
            if not L.spill:
                e.memset(L.z_ones, 1.0).then_inc(L.ones, 1)

            def prep(t, u, i):
                e.wait_ge(L.x_in[u], L.since["x_in"][u] + 16 * (i + 1))
                x = L.xin[u]
                if L.prep == "ln":
                    norm_a(e, st, x, u, L.half_prep)
                    norm_b(e, st, x, x, u, L.mid, L.since["mid"] + t + 1, L.prepped)
                    return
                st.add(e.tensor_tensor(x, x, L.xbias, ALU.add))
                st.wait()
                e.tensor_scalar(L.low[u], x, 0.0, None, ALU.min).then_inc(L.half_prep, 1)
                e.wait_ge(L.mid, L.since["mid"] + t + 1)
                e.scalar_tensor_tensor(out=x, in0=L.low[u], scalar=-1.0, in1=x, op0=ALU.add, op1=ALU.max).then_inc(L.prepped, 1)

            def score(t, u):
                e.wait_ge(L.z_ready, L.since["z_ready"] + RING + len(L.chunks) * (t + 1))
                zt = L.z[:, t, :, 0:64] if L.batched else L.stage[u] if L.spill else L.z[:, t, 0:C].rearrange("p (h d) -> p h d", h=1)
                for r in range(2):
                    st.wait()
                    st.add(e.tensor_tensor(L.prod, zt, L.al_b[r], ALU.mult))
                    st.wait()
                    ins = e.tensor_reduce(L.elr[:, t, r * L.H:(r + 1) * L.H], L.prod, AX.X, ALU.add)
                    if r == 0:
                        st.add(ins)
                ins.then_inc(L.scored, 1)
                e.wait_ge(L.scored, L.since["scored"] + 2 + t + 1)

            prep(0, 0, 0)
            prep(1, 1, 0)
            with e.Fori(0, HT - 1) as i:
                st.enter(i, 6 + (8 if L.prep == "ln" else 2))
                for u in range(2):
                    prep(2 * i + 2 + u, u, i + 1)
                    score(2 * i + u, u)
                st.leave(HT - 1)
            score(T - 2, 0)
            score(T - 1, 1)

            st.add(e.tensor_scalar(L.el2, L.elr[:, :, 0:L.H], SLOPE, None, ALU.mult))
            e.tensor_scalar(L.el8, L.elr[:, :, 0:L.H], 1.0 - SLOPE, None, ALU.mult).then_inc(L.scaled, 1)
            e.wait_ge(L.scaled, L.since["scaled"] + 1)
            if L.spill:
                for u in range(2):
                    e.wait_ge(L.spilled[u], L.since["spilled"][u] + 16 * HT)
                for u in range(2):
                    st.add(e.memset(L.zh[u][:, :, L.D:L.D + 1], 1.0))
                st.wait()
                e.engine_nop().then_inc(L.ones, 1)
            mx = small[0:P, 32:32 + T]
            v = [small[0:P, 44:44 + T], small[0:P, 54:54 + T]]

            def max_tile(h, u, i, t):
                if t == 0:
                    e.wait_ge(L.elb_in[u], L.since["elb_in"][u] + 16 * (i + 1))
                st.wait()
                apart(e)
                st.add(e.tensor_tensor_reduce(L.junk, L.elb[u], MB[:, t, :], 1.0, -3.0e38, ALU.add, ALU.max, mx[:, t:t + 1]))

            def max_end(h, u):
                er = L.elr[:, :, bass.ds(L.H + h, 1)].rearrange("p t o -> p (t o)")
                r = small[0:P, 64 + u * 2 * T:64 + (u + 1) * 2 * T]
                st.wait()
                st.add(e.tensor_tensor(v[0], mx, er, ALU.add))
                st.wait()
                st.add(e.scalar_tensor_tensor(out=v[1], in0=v[0], scalar=SLOPE, in1=v[0], op0=ALU.mult, op1=ALU.max))
                st.wait()
                st.add(e.tensor_tensor(r[:, 0:T], er, v[1], ALU.subtract))
                e.scalar_tensor_tensor(out=r[:, T:2 * T], in0=er, scalar=SLOPE, in1=v[1], op0=ALU.mult, op1=ALU.subtract).then_inc(L.r_ready, 1)

            def weights(h, j):
                half, s = j // T, j % T
                if s == 0:
                    e.wait_ge(L.p_free, L.since["p_free"] + 2 * h + half + 1)
                e.wait_ge(L.e_ready, L.since["e_ready"] + 2 + 2 * T * h + j + 1)
                counts = AT[:, s, half * HALF:(half + 1) * HALF]
                if L.batched:
                    e.scalar_tensor_tensor(out=Ph[half][:, s, :], in0=L.ex[j % 4], scalar=2.0, in1=counts,
                                           op0=ALU.min, op1=ALU.mult).then_inc(L.p_ready, 1)
                    return
                e.tensor_tensor(L.m[j % 2], L.e[j % 2][0], L.e[j % 2][1], ALU.max).then_inc(L.e_free, 1)
                e.wait_ge(L.e_free, L.since["e_free"] + 2 + 2 * T * h + j + 1)
                e.scalar_tensor_tensor(out=Ph[half][:, s, :], in0=L.m[j % 2], scalar=2.0,
                                       in1=counts, op0=ALU.min, op1=ALU.mult).then_inc(L.p_ready, 1)

            rd = small[0:P, 110:110 + HT]

            def finish(h, half):
                if L.batched:
                    e.wait_ge(L.ag_ready, L.since["ag_ready"] + 2 * h + half + 1)
                    sums = banks[2 + half][0:P, 0:HT * 65].rearrange("p (t f) -> p t f", t=HT)
                    o = L.og[half][:, 0:HT * 64].rearrange("p (t f) -> p t f", t=HT)
                    st.add(e.tensor_scalar(rd.rearrange("p (t o) -> p t o", o=1), sums[:, :, 64:65], TINY, None, ALU.max))
                    st.wait()
                    st.add(e.reciprocal(rd, rd))
                    st.wait()
                    e.wait_ge(L.stored[half], L.since["stored"][half] + 16 * h)
                    st.add(e.tensor_tensor(o, sums[:, :, 0:64], rd.rearrange("p (t o) -> p t o", o=1).to_broadcast([P, HT, 64]), ALU.mult))
                    st.wait()
                    e.tensor_tensor(o, o, L.z[:, half * HT:(half + 1) * HT, h, 0:64], ALU.add).then_inc(L.out_done, 1)
                    return
                for d in range(HT):
                    j = half * HT + d
                    e.wait_ge(L.ag_ready, L.since["ag_ready"] + T * h + j + 1)
                    last = banks[2 + 2 * (j % 2) + 1][0:P, 0:L.cols[1][1]]
                    den = last[:, L.cols[1][1] - 1:L.cols[1][1]]
                    st.add(e.tensor_scalar(rd[:, 0:1], den, TINY if L.add_z else 1e-16, None, ALU.max if L.add_z else ALU.add))
                    st.wait()
                    st.add(e.reciprocal(rd[:, 1:2], rd[:, 0:1]))
                    st.wait()
                    e.wait_ge(L.stored[j % 2], L.since["stored"][j % 2] + 16 * (HT * h + j // 2))
                    for c, (at, w) in enumerate(L.cols):
                        w -= c
                        src = banks[2 + 2 * (j % 2) + c][0:P, 0:w]
                        o = L.og[j % 2][:, at:at + w]
                        if L.add_z:
                            ins = e.scalar_tensor_tensor(out=o, in0=src, scalar=rd[:, 1:2], in1=L.z[:, j, at:at + w], op0=ALU.mult, op1=ALU.add)
                        else:
                            ins = e.tensor_scalar(o, src, rd[:, 1:2], None, ALU.mult)
                    ins.then_inc(L.out_done, 1)

            def batched_head(h, u, i, first, more):
                at = 0
                for j in range(2 * T):
                    if first:
                        if j < T:
                            max_tile(1, 1, 0, j)
                            if j == T - 1:
                                max_end(1, 1)
                        else:
                            max_tile(2, 0, 1, j - T)
                    elif more and j % 2 == 0:
                        max_tile(h + 2, u, i + 1, j // 2)
                    if more and j == 2 * T - 1:
                        max_end(h + 2, u)
                    weights(h, j)
                    if not first and j in (1, T + 1):
                        finish(h - 1, j // T)

            FIN = 3 if L.batched else 2 * HT
            for t in range(T):
                max_tile(0, 0, 0, t)
            max_end(0, 0)

            def head(h, u, first, last, i):
                at = 0
                for j in range(2 * T):
                    if not last and j in MAX_STEPS:
                        max_tile(h + 1, 1 - u, i + u, at)
                        at += 1
                        if at == T:
                            max_end(h + 1, 1 - u)
                    weights(h, j)
                    if j == T - 1 and not first:
                        finish(h - 1, 1)
                finish(h, 0)

            if L.batched:
                batched_head(0, 0, 0, True, True)
                batched_head(1, 1, 0, False, True)
                with e.Fori(1, L.H // 2 - 1) as i:
                    st.enter(i - 1, 2 * (T + 3 + 2 * FIN))
                    for u in range(2):
                        batched_head(2 * i + u, u, i, False, True)
                    st.leave(L.H // 2 - 2)
                for u in range(2):
                    batched_head(L.H - 2 + u, u, L.H // 2 - 1, False, False)
                finish(L.H - 1, 0)
                finish(L.H - 1, 1)
                return
            if L.H == 1:
                head(0, 0, True, True, 0)
                finish(0, 1)
                return
            head(0, 0, True, False, 0)
            head(1, 1, False, L.H == 2, 0)
            i = L.H // 2 - 1
            head(L.H - 2, 0, False, False, i)
            head(L.H - 1, 1, False, True, i)
            finish(L.H - 1, 1)

        def moe_vector(e, st, M):
            e.wait_ge(M.c_in, 144 if M.bias else 112)

            def prep(t, u, i):
                e.wait_ge(M.x_in[u], 32 * (i + 1))
                x = M.acc[:, t, :]
                st.add(e.tensor_tensor(x, x, M.rbias, ALU.add))
                st.wait()
                e.tensor_tensor(x, x, M.rawt[u], ALU.add).then_inc(M.raw_free, 1)
                e.wait_ge(M.raw_free, 2 + t + 1)
                norm_a(e, st, x, u, M.half_prep)
                e.wait_ge(M.xt_ready, 2 * t + 1)
                e.wait_ge(M.xn_out[u], 16 * (i + 1))
                norm_b(e, st, M.xn[u], x, u, M.mid, t + 1, M.prepped)

            with e.Fori(0, HT) as i:
                st.enter(i, 10)
                for u in range(2):
                    prep(2 * i + u, u, i)
                st.leave(HT)
            g, flat, col = M.g, M.gflat, M.col
            wide = lambda c: c.rearrange("p (t o) -> p t o", o=1).to_broadcast([P, T, EX])
            order = M.order.rearrange("p (o e) -> p o e", o=1).to_broadcast([P, T, EX])

            def step(ins):
                st.add(ins)
                st.wait()
            step(e.memset(M.onesq, 1.0))
            e.wait_ge(M.lg_ready, 1)
            lg = banks[2][0:P, 0:T * EX].rearrange("p (t e) -> p t e", t=T)
            step(e.tensor_reduce(col[0], lg, AX.X, ALU.max))
            e.tensor_tensor(g[0], lg, wide(col[0]), ALU.subtract).then_inc(M.exp_in, 1)
            e.wait_ge(M.exped, 1)
            step(e.tensor_reduce(col[1], g[0], AX.X, ALU.add))
            step(e.reciprocal(col[2], col[1]))
            e.tensor_tensor(g[1], g[0], wide(col[2]), ALU.mult).then_inc(M.probs, 1)
            e.wait_ge(M.probs, 1)

            def pick(p, taken):
                step(e.tensor_reduce(col[0], p, AX.X, ALU.max))
                step(e.tensor_tensor(g[2], p, wide(col[0]), ALU.is_equal))
                step(e.tensor_tensor(g[2], g[2], order, ALU.mult))
                step(e.tensor_reduce(col[1], g[2], AX.X, ALU.max))
                step(e.tensor_tensor(taken, order, wide(col[1]), ALU.is_equal))
            pick(g[1], g[3])
            step(e.scalar_tensor_tensor(out=flat[4], in0=flat[3], scalar=-2.0, in1=flat[1], op0=ALU.mult, op1=ALU.add))
            pick(g[4], g[5])
            e.tensor_tensor(g[7], g[3], g[5], ALU.add).then_inc(M.picked, 1)

            e.wait_ge(M.counts, 1)
            inside, tiles = [banks[4][0:P, j * T * EX:(j + 1) * T * EX].rearrange("p (t e) -> p t e", t=T) for j in range(2)]
            n, tile_n, end, first = M.per
            step(e.memset(g[2][:, 0, :], 0.0))
            for t in range(1, T):
                step(e.tensor_tensor(g[2][:, t, :], g[2][:, t - 1, :], tiles[:, t - 1, :], ALU.add))
            step(e.tensor_tensor(n, g[2][:, T - 1, :], tiles[:, T - 1, :], ALU.add))
            step(e.tensor_tensor(g[2], g[2], inside, ALU.add))
            most = -(-N // ST)
            above = M.above[:, 0:EX * most].rearrange("p (e k) -> p e k", e=EX)
            step(e.tensor_tensor(above, n.rearrange("p (e o) -> p e o", o=1).to_broadcast([P, EX, most]),
                                 M.steps[:, 0:most].rearrange("p (o k) -> p o k", o=1).to_broadcast([P, EX, most]), ALU.is_gt))
            step(e.tensor_reduce(tile_n, above, AX.X, ALU.add))
            step(e.tensor_copy(end[:, 0:1], tile_n[:, 0:1]))
            for x in range(1, EX):
                step(e.tensor_tensor(end[:, x:x + 1], end[:, x - 1:x], tile_n[:, x:x + 1], ALU.add))
            step(e.tensor_tensor(first, end, tile_n, ALU.subtract))
            step(e.tensor_copy(M.span[0:1, 0:EX], first[0:1, :]))
            step(e.tensor_copy(M.span[0:1, EX:2 * EX], end[0:1, :]))
            step(e.tensor_scalar(first, first, float(ST), None, ALU.mult))
            step(e.tensor_tensor(g[2], g[2], first.rearrange("p (o e) -> p o e", o=1).to_broadcast([P, T, EX]), ALU.add))
            for k, taken in enumerate((g[3], g[5])):
                step(e.tensor_tensor(g[4], g[2], taken, ALU.mult))
                step(e.tensor_reduce(M.slot[:, k * T:(k + 1) * T], g[4], AX.X, ALU.add))
            above = M.above[:, 0:2 * T * MAX_TILES].rearrange("p (s k) -> p s k", s=2 * T)
            wide_s = M.slot.rearrange("p (s o) -> p s o", o=1).to_broadcast([P, 2 * T, MAX_TILES])
            wide_k = M.steps[:, 1:1 + MAX_TILES].rearrange("p (o k) -> p o k", o=1).to_broadcast([P, 2 * T, MAX_TILES])
            step(e.tensor_tensor(above, wide_s, wide_k, ALU.is_ge))
            step(e.tensor_reduce(M.tile, above, AX.X, ALU.add))
            step(e.tensor_scalar(M.tile, M.tile, 1.0 - ST * LIST, None, ALU.mult))
            step(e.scalar_tensor_tensor(out=M.place, in0=M.slot, scalar=float(LIST), in1=M.tile, op0=ALU.mult, op1=ALU.add))
            step(e.tensor_copy(M.slot_i, M.slot))
            e.tensor_copy(M.place_i, M.place).then_inc(M.placed, 1)

            if M.balanced:
                step(e.tensor_tensor(g[4], g[7], g[1], ALU.mult))
                e.wait_ge(M.imp_ready, 1)
                step(e.tensor_reduce(M.run, banks[3][0:P, 0:T * EX].rearrange("p (t e) -> p e t", t=T), AX.X, ALU.add))
                step(e.tensor_scalar(M.run, M.run, -1.0, DECAY_STEP, ALU.add, ALU.mult))
                step(e.tensor_scalar(M.run, M.run, 1.0, BAL_EPS, ALU.add, ALU.add))
                step(e.reciprocal(M.run, M.run))
                step(e.tensor_tensor(g[0], g[4], M.run.rearrange("p (o e) -> p o e", o=1).to_broadcast([P, T, EX]), ALU.mult))
                step(e.tensor_reduce(col[0], g[0], AX.X, ALU.add))
                step(e.reciprocal(col[1], col[0]))
                e.tensor_tensor(g[6], g[0], wide(col[1]), ALU.mult).then_inc(M.gates, 1)
            else:
                e.tensor_tensor(g[6], g[7], g[1], ALU.mult).then_inc(M.gates, 1)
            e.wait_ge(M.gates, 1)
            for k, taken in enumerate((g[3], g[5])):
                step(e.tensor_tensor(g[4], g[6], taken, ALU.mult))
                step(e.tensor_reduce(M.gate[k], g[4], AX.X, ALU.add))

            e.wait_ge(M.placed, 1)
            with e.Fori(0, all_tiles(e, M)) as i:
                e.wait_ge(M.y_ready, i + 1)
                e.wait_ge(M.y_out, 16 * i + 16)
                apart(e)
                e.tensor_copy(M.y[:, 0:C // 2], banks[2][:, 0:C // 2])
                e.tensor_copy(M.y[:, C // 2:C], banks[3][:, 0:C // 2]).then_inc(M.y_sb, 1)
            if M.bias:
                for t in range(T):
                    e.wait_ge(M.gb_ready, t + 1)
                    for c in range(2):
                        a = M.acc[:, t, c * (C // 2):(c + 1) * (C // 2)]
                        ins = e.tensor_tensor(a, a, banks[4 + 2 * (t % 2) + c][0:P, 0:C // 2], ALU.add)
                    ins.then_inc(M.gb_free, 1)
                e.wait_ge(M.gb_free, T)
            for t in range(T):
                e.wait_ge(M.yg_in[t % 4], 32 * (t // 4 + 1))
                a = M.acc[:, t, :]
                for k in range(2):
                    ins = e.scalar_tensor_tensor(out=a, in0=M.yg[t % 4][k], scalar=M.gate[k][:, t:t + 1], in1=a, op0=ALU.mult, op1=ALU.add)
                    if k == 0:
                        step(ins)
                ins.then_inc(M.y_done, 1)

        @block.vector
        def _(e):
            st = Step(e, v_step)
            graph_vector(e, st)
            e.wait_ge(gs["at_sb"], 3 * T)
            e.wait_ge(gs["bias"], T)
            for n in range(3):
                gat_vector(e, st, layers[n])
            add_loops(e)
            moe_vector(e, st, moes[0])
            e.wait_ge(gs["loops"], T)
            for n in range(3, 5):
                gat_vector(e, st, layers[n])
            moe_vector(e, st, moes[1])


_KEEP = ["x", "src", "dst", "L0_gnn_W0", "L0_gnn_al0", "L0_gnn_ar0", "L0_gnn_b0", "L0_gnn_W1", "L0_gnn_al1",
         "L0_gnn_ar1", "L0_gnn_b1", "L0_gnn_W2", "L0_gnn_al2", "L0_gnn_ar2", "L0_gnn_b2", "L1_gnn_W1",
         "L1_gnn_a1_src", "L1_gnn_a1_dst", "L1_gnn_b1", "L1_gnn_W2", "L1_gnn_a2_src", "L1_gnn_a2_dst",
         "L1_gnn_b2", "L1_ffn_Wg", "L1_ffn_W1", "L1_ffn_W2", "L1_ffn_b2"]


def kernel(**inputs):
    import concourse.bacc as bacc
    from concourse.bass_utils import run_bass_kernel_spmd as run

    a = {n: np.ascontiguousarray(inputs[n]) for n in _KEEP}
    a["L0_router"] = np.ascontiguousarray(np.asarray(inputs["L0_ffn_router_w"]).T)
    a["L0_w1"] = np.ascontiguousarray(np.asarray(inputs["L0_ffn_w1"]).transpose(0, 2, 1))
    a["L0_w2"] = np.ascontiguousarray(np.asarray(inputs["L0_ffn_w2"]).transpose(0, 2, 1))
    a["L1_b1"] = np.ascontiguousarray(np.asarray(inputs["L1_ffn_b1"]).reshape(EX, -1, 128).transpose(2, 0, 1))
    a["ident"] = np.eye(128, dtype=np.float32)
    a["spread"] = np.concatenate([np.eye(P), np.ones((1, P))]).astype(np.float32)
    a["nodes"] = np.arange(N, dtype=np.int16)
    a["order"] = np.arange(EX, 0, -1).astype(np.float32)
    a["no_tokens"] = np.zeros((ST * LIST, 1), np.int32)
    a["no_outputs"] = np.zeros((ST, C), np.float32)
    a["steps"] = (ST * np.arange(LIST)).astype(np.float32)
    a["node_ids"] = np.ascontiguousarray(np.arange(N, dtype=np.int32).reshape(T, P).T)
    a["before"] = np.triu(np.ones((P, P), np.float32), 1)
    a["pair_limits"] = np.stack([PAIRS - np.arange(PAIRS), 1 + np.arange(PAIRS)], 1).astype(np.float32)

    nc = bacc.Bacc("TRN2", target_bir_lowering=False, num_devices=1)
    aps = {n: nc.dram_tensor(f"in_{n}", v.shape, mybir.dt.from_np(v.dtype), kind="ExternalInput").ap() for n, v in a.items()}
    out = nc.dram_tensor("out_x", (N, C), F32, kind="ExternalOutput").ap()
    graph_transformer(nc, aps, out)
    r = run(nc, [{f"in_{n}": v for n, v in a.items()}], core_ids=[0])
    return r.results[0]["out_x"]
```

```python
from contextlib import ExitStack

import numpy as np

import concourse.bass as bass
from concourse import mybir

F32 = mybir.dt.float32
BF16 = mybir.dt.bfloat16
I16 = mybir.dt.int16
I32 = mybir.dt.int32
ALU = mybir.AluOpType
ACT = mybir.ActivationFunctionType
AX = mybir.AxisListType

N = 1250
P = 125
T = N // P
HALF = N // 2
HT = T // 2
E = 20000
EP = 125
PER = 4
GROUPS = E // (PER * EP)
C = 768
CK = C // 128
EX = 8
NONE = -1.0e30
TINY = 1.0e-30
EPS = 1e-5
RING = 4
SLOPE = 0.2
ST = 128
MAX_TILES = (2 * N) // ST + EX
MIN_TILES = -(-2 * N // ST)
LIST = 32
DECAY_STEP = 1.0 - 0.9
BAL_EPS = 0.01


ADD_AT = [3, 7, 9]
ADDS, TURNS = 2 * len(ADD_AT), 2 * (T - len(ADD_AT))


def of_vector(j):
    return sum(v % T in ADD_AT for v in range(j))


def split(total, parts):
    out, at = [], 0
    for n in range(parts):
        w = -(-(total - at) // (parts - n))
        w += w % 2 if at + w < total else 0
        out.append((at, w))
        at += w
    return out


class Step:

    def __init__(self, eng, sem):
        self.eng, self.sem, self.base, self.k = eng, sem, 0, 0

    def add(self, instruction):
        instruction.then_inc(self.sem, 1)
        self.k += 1

    def wait(self):
        self.eng.wait_ge(self.sem, self.base + self.k)

    def enter(self, i, per_round):
        self.kept = self.base + self.k
        self.base, self.k, self.per = self.kept + i * per_round, 0, per_round

    def leave(self, rounds):
        assert self.k == self.per, (self.k, self.per)
        self.base, self.k = self.kept + rounds * self.per, 0


class Gat:

    def __init__(self, name, heads, width, k_tiles, prep, spill, add_z, signals, before):
        self.name, self.H, self.D, self.KT = name, heads, width, k_tiles
        self.F = heads * width
        self.K = k_tiles * 128
        self.prep, self.spill, self.add_z = prep, spill, add_z
        self.batched = width == 64
        self.groups = [(g, min(4, k_tiles - g)) for g in range(0, k_tiles, 4)]
        if spill:
            self.chunks = [(h * width, width) for h in range(heads)]
            self.ring = 4
        else:
            self.chunks = [(0, self.F // 2), (self.F // 2, self.F // 2)]
            self.ring = 4
        self.cols = [(0, width + 1)] if self.batched else [(0, width // 2), (width // 2, width // 2 + 1)]
        bias = prep == "elu"
        self.vectors = 48 if bias else 32
        G, NC, of = len(self.groups), len(self.chunks), [(heads + 1) // 2, heads // 2]
        banks = 2 * heads if self.batched else T * heads
        self.totals = dict(
            w_in=[16] * 2, v_in=self.vectors, scored=T, x_in=[16 * HT] * 2, x_free=T, half_prep=T, mid=T, prepped=T, tp_ready=G * T, xt_ready=G * T,
            zp_ready=NC * T, z_ready=NC * T, ones=1, spilled=[16 * HT * spill] * 2, elt_ready=3, elt_sb=3, scaled=1, el_out=16,
            elb_in=[16 * n for n in of], r_ready=heads, rt_ready=heads, rt_sb=heads, r_out=[16 * n for n in of],
            rb_in=[16 * n * (not self.batched) for n in of], relued=2 * T * heads * self.batched, t_ready=TURNS * heads * self.batched,
            added=ADDS * heads * self.batched, rb2_in=[16 * n * self.batched for n in of],
            er_in=[16 * n * self.batched for n in of], r2_in=[48 * heads * self.batched] * 2, z_in=[16 * n * spill for n in of], e_ready=2 * T * heads, e_free=2 * T * heads * (not self.batched),
            p_ready=2 * T * heads, p_free=2 * heads, ag_ready=banks, out_done=banks, stored=[8 * banks] * 2)
        self.since = {k: [0, 0] if isinstance(v, list) else 0 for k, v in self.totals.items()}
        if before is not None:
            for k in self.totals:
                had, more = before.since[k], before.totals[k]
                self.since[k] = [x + y for x, y in zip(had, more)] if isinstance(had, list) else had + more
        self.w_in = signals["w_in"]
        self.v_in = signals["v_in"]
        self.scored = signals["scored"]
        self.scaled = signals["scaled"]
        self.relued = signals["relued"]
        self.t_ready = signals["t_ready"]
        self.added = signals["added"]
        self.rb2_in = signals["rb2_in"]
        self.er_in = signals["er_in"]
        self.r2_in = signals["r2_in"]
        self.x_in = signals["x_in"]
        self.x_free = signals["x_free"]
        self.half_prep = signals["half_prep"]
        self.mid = signals["mid"]
        self.prepped = signals["prepped"]
        self.tp_ready = signals["tp_ready"]
        self.xt_ready = signals["xt_ready"]
        self.zp_ready = signals["zp_ready"]
        self.z_ready = signals["z_ready"]
        self.ones = signals["ones"]
        self.spilled = signals["spilled"]
        self.elt_ready = signals["elt_ready"]
        self.elt_sb = signals["elt_sb"]
        self.el_out = signals["el_out"]
        self.elb_in = signals["elb_in"]
        self.r_ready = signals["r_ready"]
        self.rt_ready = signals["rt_ready"]
        self.rt_sb = signals["rt_sb"]
        self.r_out = signals["r_out"]
        self.rb_in = signals["rb_in"]
        self.z_in = signals["z_in"]
        self.e_ready = signals["e_ready"]
        self.e_free = signals["e_free"]
        self.p_ready = signals["p_ready"]
        self.p_free = signals["p_free"]
        self.ag_ready = signals["ag_ready"]
        self.out_done = signals["out_done"]
        self.stored = signals["stored"]


class Moe:

    def __init__(self, name, inner, balanced, bias, sem):
        self.name, self.I, self.IC, self.balanced, self.bias = name, inner, inner // 128, balanced, bias
        s = lambda what, n=1: sem(f"{name}_{what}") if n == 1 else [sem(f"{name}_{what}{i}") for i in range(n)]
        self.c_in = s("c_in")
        self.x_in = s("x_in", 2)
        self.raw_free = s("raw_free")
        self.half_prep = s("half_prep")
        self.mid = s("mid")
        self.prepped = s("prepped")
        self.tp_ready = s("tp_ready")
        self.xt_ready = s("xt_ready")
        self.lg_ready = s("lg_ready")
        self.exp_in = s("exp_in")
        self.exped = s("exped")
        self.probs = s("probs")
        self.imp_ready = s("imp_ready")
        self.picked = s("picked")
        self.counts = s("counts")
        self.placed = s("placed")
        self.gates = s("gates")
        self.xn_out = s("xn_out", 2)
        self.list_ready = s("list_ready")
        self.listed = s("listed")
        self.rows_ready = s("rows_ready")
        self.xg_in = s("xg_in")
        self.xg_ready = s("xg_ready")
        self.xg_sb = s("xg_sb")
        self.w_in = s("w_in", 2)
        self.w_free = s("w_free")
        self.h_ready = s("h_ready")
        self.h_sb = s("h_sb")
        self.y_ready = s("y_ready")
        self.y_sb = s("y_sb")
        self.y_out = s("y_out")
        self.yg_in = s("yg_in", 4)
        if bias:
            self.gt_ready = s("gt_ready")
            self.gt_sb = s("gt_sb")
            self.gb_ready = s("gb_ready")
            self.gb_free = s("gb_free")
        self.y_done = s("y_done")
        self.stored = s("stored")


def graph_transformer(nc, A, out):
    ctx = ExitStack()
    with ctx:
        sems = []

        def sem(name):
            s = ctx.enter_context(nc.semaphore(name))
            sems.append(s)
            return s

        def sb(name, shape, dt=F32):
            return ctx.enter_context(nc.sbuf_tensor(name, shape, dt))

        AT = sb("edge_counts", [P, T, N], I16)
        MB = sb("no_edge_bias", [P, T, N], BF16)
        ident = sb("ident", [128, 128])
        noti = sb("not_ident", [P, P], BF16)
        elr = sb("elr", [P, T * 24])
        el2 = sb("el2", [P, T * 12])
        el8 = sb("el8", [P, T * 12])
        spread = sb("spread", [P + 1, P])
        small = sb("small", [128, 256])
        ARENA = 38400
        arena = sb("arena", [128, ARENA])

        def carve(at, parts, width):
            assert at + width <= ARENA, (at, width)
            return arena[0:parts, at:at + width]

        P_AT, P_W = 0, 12500
        Z_AT, Z_W = P_AT + P_W, 10260
        S_AT = Z_AT + Z_W
        Ph = [carve(P_AT + h * T * HALF, P, T * HALF).rearrange("p (s d) -> p s d", s=T) for h in range(2)]

        psum = ctx.enter_context(nc.psum_tensor("psum", [128, 8 * 512], F32))
        banks = [psum[:, i * 512:(i + 1) * 512] for i in range(8)]

        def dram(name, shape, dt=F32):
            return nc.dram_tensor(name, shape, dt, kind="Internal").ap()

        el_rows = dram("el_rows", (24, N))
        r_rows = dram("r_rows", (12, 2 * T, P))
        z_heads = dram("z_heads", (4, N, 512))
        raw = [dram(f"raw{i}", (N, C)) for i in range(3)] + [dram("raw3", (N, 2048)), dram("raw4", (N, C))]
        x2 = dram("x2", (N, C))
        xn_rows = dram("xn_rows", (N, C))
        y_rows = dram("y_rows", (MAX_TILES * ST, C))
        by_tile = lambda a: a.rearrange("(t p) f -> p t f", p=P)
        over = lambda row, parts=P: row.partition_broadcast(parts)

        signals = dict(
            w_in=[sem("w_in0"), sem("w_in1")],
            v_in=sem("v_in"),
            scaled=sem("scaled"),
            scored=sem("scored"),
            relued=sem("relued"),
            t_ready=sem("t_ready"),
            added=sem("added"),
            rb2_in=[sem("rb2_in0"), sem("rb2_in1")],
            er_in=[sem("er_in0"), sem("er_in1")],
            r2_in=[sem("r2_in0"), sem("r2_in1")],
            x_in=[sem("x_in0"), sem("x_in1")],
            x_free=sem("x_free"),
            half_prep=sem("half_prep"),
            mid=sem("mid"),
            prepped=sem("prepped"),
            tp_ready=sem("tp_ready"),
            xt_ready=sem("xt_ready"),
            zp_ready=sem("zp_ready"),
            z_ready=sem("z_ready"),
            ones=sem("ones"),
            spilled=[sem("spilled0"), sem("spilled1")],
            elt_ready=sem("elt_ready"),
            elt_sb=sem("elt_sb"),
            el_out=sem("el_out"),
            elb_in=[sem("elb_in0"), sem("elb_in1")],
            r_ready=sem("r_ready"),
            rt_ready=sem("rt_ready"),
            rt_sb=sem("rt_sb"),
            r_out=[sem("r_out0"), sem("r_out1")],
            rb_in=[sem("rb_in0"), sem("rb_in1")],
            z_in=[sem("z_in0"), sem("z_in1")],
            e_ready=sem("e_ready"),
            e_free=sem("e_free"),
            p_ready=sem("p_ready"),
            p_free=sem("p_free"),
            ag_ready=sem("ag_ready"),
            out_done=sem("out_done"),
            stored=[sem("stored0"), sem("stored1")],
        )
        layers = []
        for args in [
            ("g0", 12, 64, CK, "ln", False, True),
            ("g1", 12, 64, CK, "elu", False, True),
            ("g2", 1, C, CK, "elu", False, True),
            ("g3", 4, 512, CK, "ln", True, False),
            ("g4", 1, C, 16, "elu", False, False),
        ]:
            layers.append(Gat(*args, signals, layers[-1] if layers else None))
        moes = [Moe("m0", 256, True, False, sem), Moe("m1", 384, False, True, sem)]
        for n, L in enumerate(layers):
            L.W, L.al, L.ar = [(A["L0_gnn_W0"], A["L0_gnn_al0"], A["L0_gnn_ar0"]),
                               (A["L0_gnn_W1"], A["L0_gnn_al1"], A["L0_gnn_ar1"]),
                               (A["L0_gnn_W2"], A["L0_gnn_al2"], A["L0_gnn_ar2"]),
                               (A["L1_gnn_W1"], A["L1_gnn_a1_src"], A["L1_gnn_a1_dst"]),
                               (A["L1_gnn_W2"], A["L1_gnn_a2_src"], A["L1_gnn_a2_dst"])][n]
            L.src = [A["x"], raw[0], raw[1], x2, raw[3]][n]
            L.src_bias = [None, A["L0_gnn_b0"], A["L0_gnn_b1"], None, A["L1_gnn_b1"]][n]
            L.dst = raw[n]
            L.w_sb = carve(P_AT, 128, L.KT * L.F).rearrange("p (k f) -> p k f", k=L.KT)
            at = S_AT
            L.xin = [carve(at + u * L.K, P, L.K) for u in range(2)]
            at += 2 * L.K
            if L.prep == "elu":
                L.low = [carve(at + u * L.K, P, L.K) for u in range(2)]
                at += 2 * L.K
            L.xbias = carve(at, P, L.K)
            at += L.K
            L.xt = [carve(at + u * L.KT * P, 128, L.KT * P).rearrange("p (k n) -> p k n", k=L.KT) for u in range(2)]
            at += 2 * L.KT * P
            L.prod = carve(at, P, L.F).rearrange("p (h d) -> p h d", h=L.H)
            L.al_b = [carve(S_AT - (2 - u) * L.F, P, L.F).rearrange("p (h d) -> p h d", h=L.H) for u in range(2)]
            at = S_AT
            L.elb = [carve(at + u * N, P, N) for u in range(2)]
            at += 2 * N
            if L.batched:
                L.erb = [carve(at + u * N, P, N) for u in range(2)]
                at += 2 * N
                L.r2 = [carve(at + half * 3 * HALF, P + 1, 3 * HALF).rearrange("p (u d) -> p u d", u=3) for half in range(2)]
                at += 6 * HALF
                L.ex = [carve(at + u * HALF, P, HALF) for u in range(4)]
                L.elt = carve(at, 24, N)
                at += 4 * HALF
                L.rb2 = [carve(at + u * N, P, N) for u in range(2)]
                at += 2 * N
            else:
                L.rb = [carve(at + u * 2 * N, P, 2 * N).rearrange("p (r d) -> p r d", r=2) for u in range(2)]
                at += 4 * N
                L.e = [[carve(at + (2 * u + r) * HALF, P, HALF) for r in range(2)] for u in range(2)]
                at += 4 * HALF
                L.m = [carve(at + u * HALF, P, HALF) for u in range(2)]
                at += 2 * HALF
            L.junk = carve(at, P, HALF).bitcast(BF16)
            at += HALF
            width = HT * 64 if L.batched else C
            L.og = [carve(at + u * width, P, width) for u in range(2)]
            at += 2 * width
            if not L.batched:
                L.elt = carve(at, 24, N)
            L.rt = [carve(at + u * P, 2 * T, P) for u in range(2)]
            if L.batched:
                L.z = carve(Z_AT, P, T * L.H * 65).rearrange("p (t h f) -> p t h f", t=T, h=L.H)
                L.z_ones = L.z[:, :, :, 64:65]
            elif L.spill:
                L.zh = [carve(Z_AT + u * T * 513, P, T * 513).rearrange("p (t f) -> p t f", t=T) for u in range(2)]
                L.stage = [carve(Z_AT + u * L.F, P, L.F).rearrange("p (h f) -> p h f", h=L.H) for u in range(2)]
            else:
                L.z = carve(Z_AT, P, T * (C + 1)).rearrange("p (t f) -> p t f", t=T)
                L.z_ones = L.z[:, :, C:C + 1]
            L.elr = elr[:, 0:T * 2 * L.H].rearrange("p (t h) -> p t h", t=T)
            L.el2 = el2[:, 0:T * L.H].rearrange("p (t h) -> p t h", t=T)
            L.el8 = el8[:, 0:T * L.H].rearrange("p (t h) -> p t h", t=T)
        for n, M in enumerate(moes):
            M.res, M.raw, M.raw_bias = [(A["x"], raw[2], A["L0_gnn_b2"]), (x2, raw[4], A["L1_gnn_b2"])][n]
            M.dst = [x2, out][n]
            M.router = [A["L0_router"], A["L1_ffn_Wg"]][n]
            M.w1, M.w2 = [(A["L0_w1"], A["L0_w2"]), (A["L1_ffn_W1"], A["L1_ffn_W2"])][n]
            at = P_AT
            M.w1s = [carve(at + u * CK * M.I, 128, CK * M.I).rearrange("p (k i) -> p k i", k=CK) for u in range(2)]
            at += 2 * CK * M.I
            M.w2s = [carve(at + u * M.IC * C, 128, M.IC * C).rearrange("p (k f) -> p k f", k=M.IC) for u in range(2)]
            at += 2 * M.IC * C
            M.xg = carve(at, ST, C)
            M.xgt = carve(at + C, 128, CK * ST).rearrange("p (k n) -> p k n", k=CK)
            M.y = carve(at + 2 * C, ST, C)
            M.ht = carve(at + 3 * C, 128, M.IC * ST).rearrange("p (k n) -> p k n", k=M.IC)
            at += 3 * C + M.IC * ST
            assert at <= Z_AT
            at = Z_AT
            M.acc = carve(at, P, T * C).rearrange("p (t f) -> p t f", t=T)
            at += T * C
            M.xt = carve(at, 128, CK * N).rearrange("p (k n) -> p k n", k=CK)
            M.yg = [[carve(at + (2 * v + k) * C, P, C) for k in range(2)] for v in range(4)]
            at += CK * N
            early = at
            M.rawt = [carve(at + u * C, P, C) for u in range(2)]
            M.xn = [carve(at + (2 + u) * C, P, C) for u in range(2)]
            M.rbias = carve(at + 4 * C, P, C)
            at += 5 * C
            g = [carve(at + j * T * EX, P, T * EX) for j in range(8)]
            at += 8 * T * EX
            M.g = [a.rearrange("p (t e) -> p t e", t=T) for a in g]
            M.gflat = g
            M.col = [carve(at + j * T, P, T) for j in range(4)]
            at += 4 * T
            M.order = carve(at, P, EX)
            M.run = carve(at + EX, P, EX)
            at += 2 * EX
            M.steps = carve(at, P, LIST)
            at += LIST
            M.above = carve(at, P, 2 * T * LIST)
            at += 2 * T * LIST
            M.per = [carve(at + j * EX, P, EX) for j in range(4)]
            at += 4 * EX
            M.slot, M.tile, M.row, M.node = [carve(at + j * 2 * T, P, 2 * T) for j in range(4)]
            M.slot_i = carve(at + 8 * T, P, 2 * T).bitcast(I32)
            M.gate = [carve(at + (11 + k) * T, P, T) for k in range(2)]
            at += 13 * T
            M.span = carve(at, 1, 2 * EX).bitcast(I32)
            at += 2 * EX
            M.list = carve(at, ST, LIST).bitcast(I32)
            M.rows = carve(at + LIST, ST, 1).bitcast(I32)
            at += LIST + 1
            M.wr = carve(at, 128, CK * EX).rearrange("p (k e) -> p k e", k=CK)
            at += CK * EX
            M.b1 = carve(at, 128, EX * M.IC).rearrange("p (e c) -> p e c", e=EX)
            at += EX * M.IC
            M.onesq = carve(at, P, P)
            M.before = carve(at + P, P, P)
            at += 2 * P
            M.lanes = carve(at, P, ST)
            at += ST
            M.in_tile = M.above.rearrange("p (s k) -> p s k", s=2 * T)
            M.in_row = carve(early, P, 2 * T * ST).rearrange("p (s k) -> p s k", s=2 * T)
            M.b2 = carve(at, EX, C)
            at += C
            M.gt = [carve(at + u * P, EX, P) for u in range(2)]

        G0 = S_AT
        iota = carve(G0, P, N // 2).bitcast(I16)
        at = G0 + HALF
        e_nat = [carve(at + j * PER * EP, GROUPS, PER * EP).bitcast(I32) for j in range(2)]
        at += 2 * PER * EP
        e_f = [carve(at + j * PER * EP, GROUPS, PER * EP) for j in range(2)]
        at += 2 * PER * EP
        e_t = carve(at, EP, 2 * PER * GROUPS).rearrange("p (w a j) -> p w a j", w=2, a=PER)
        at += 2 * PER * GROUPS
        lim = carve(at, GROUPS, 2)
        ge = carve(at + 2, GROUPS, T + 1)
        has = carve(at + 14, GROUPS, T)
        rng = carve(at + 24, GROUPS, 2 * T)
        red = carve(at + 44, 2 * T, 1)
        row = carve(at + 46, 1, 2 * T)
        tab_f = carve(at + 70, 1, 4 * T)
        tab = carve(at + 120, 1, 4 * T).bitcast(I32)
        at += 160
        gjunk = carve(at, GROUPS, PER * EP)
        at += PER * EP
        oh_s = [carve(at + u * HALF, EP, N // 2).bitcast(BF16) for u in range(PER)]
        at += PER * HALF
        oh_d = [carve(at + u * 64, EP, 63).bitcast(BF16)[:, 0:P] for u in range(PER)]
        at += PER * 64
        zero = carve(at, EP, 300).bitcast(BF16)
        at += 300
        a_blk = [carve(at + u * N, P, N) for u in range(2)]
        cuts = split(N, 3)
        CUT = (HALF + 1) // 2

        gs = {n: sem("graph_" + n) for n in (
            "in", "float", "et_ready", "et_sb", "rng", "rng_t", "red", "red_t", "tab", "zero",
            "oh", "used", "blk_ready", "blk_sb", "bias", "at_ready", "at_sb", "loops")}
        v_step = sem("vector_step")
        y_clear = sem("y_clear")

        block = ctx.enter_context(nc.Block())

        MAX_STEPS = [0, 1, 3, 4, 6, 7, 9, 10, 12, 13]
        ROWS_AT = 15
        TURN_EARLY, ROWS_EARLY = 11, 12

        def apart(e):
            e.nop(nofuse=True)

        def graph_sync(e):
            e.dma_start(ident[:, :], A["ident"]).then_inc(gs["in"], 16)
            e.dma_start(iota, over(A["nodes"])).then_inc(gs["in"], 16)
            e.dma_start(lim, A["group_limits"]).then_inc(gs["in"], 16)
            e.dma_start(spread[:, :], A["spread"]).then_inc(gs["in"], 16)
            for j, name in enumerate(("dst", "src")):
                e.dma_start(e_nat[j], A[name].rearrange("(j e) -> j e", j=GROUPS)).then_inc(gs["in"], 16)

        def load_projection(e, L, part):
            rows = slice(part * L.KT // 2, (part + 1) * L.KT // 2)
            e.dma_start(L.w_sb[:, rows, :], L.W.rearrange("(k p) f -> p k f", p=128)[:, rows, :]).then_inc(L.w_in[part], 16)

        def gat_sync(e, L):
            for u, r in enumerate((L.al, L.ar)):
                e.dma_start(L.al_b[u].rearrange("p h d -> p (h d)"), over(r.rearrange("h d -> (h d)"))).then_inc(L.v_in, 16)
            if L.src_bias is not None:
                e.dma_start(L.xbias, over(L.src_bias)).then_inc(L.v_in, 16)
            with e.Fori(0, HT) as i:
                for u in range(2):
                    t = 2 * i + u
                    e.wait_ge(L.x_free, L.since["x_free"] + t + 1)
                    e.dma_start(L.xin[u], by_tile(L.src)[:, t, :]).then_inc(L.x_in[u], 16)
            e.wait_ge(L.elt_sb, L.since["elt_sb"] + 3)
            e.dma_start(el_rows[0:2 * L.H, :], L.elt[0:2 * L.H, :]).then_inc(L.el_out, 16)
            e.wait_ge(L.el_out, L.since["el_out"] + 16)

            def load_el(h, u):
                e.dma_start(L.elb[u], over(el_rows[h, :])).then_inc(L.elb_in[u], 16)

            def load_er(h, u):
                e.dma_start(L.erb[u], over(el_rows[h + L.H, :])).then_inc(L.er_in[u], 16)

            def lay_r2(h, u, i, first, more):
                e.wait_ge(L.rt_sb, L.since["rt_sb"] + h + 1)
                apart(e)
                e.dma_start(r_rows[h, T:2 * T, :], L.rt[u][T:2 * T, :]).then_inc(L.r_out[u], 16)
                e.wait_ge(L.r_out[u], L.since["r_out"][u] + 16 * (i + 1))
                apart(e)
                if not isinstance(i, int) or i > 0:
                    e.wait_ge(L.added, L.since["added"] + ADDS * (h - 1))
                    apart(e)
                e.dma_start(L.rb2[u], over(r_rows[h, T:2 * T, :].rearrange("t p -> (t p)"))).then_inc(L.rb2_in[u], 16)
                for half in range(2):
                    if not first:
                        e.wait_ge(L.t_ready, L.since["t_ready"] + TURNS * (h - 1) + TURNS // 2 * (half + 1))
                        apart(e)
                    for v in range(3):
                        e.dma_start(L.r2[half][P:P + 1, v, :],
                                    r_rows[h, T + half * HT:T + (half + 1) * HT, :].rearrange("(o t) p -> o (t p)", o=1)
                                    ).then_inc(L.r2_in[half], 16)
                    if half == 0 and more:
                        load_el(h + 2, u)

            def move_r(h, u, i):
                e.wait_ge(L.rt_sb, L.since["rt_sb"] + h + 1)
                e.dma_start(r_rows[h, :, :], L.rt[u]).then_inc(L.r_out[u], 16)
                e.wait_ge(L.r_out[u], L.since["r_out"][u] + 16 * (i + 1))
                apart(e)
                e.dma_start(L.rb[u], over(r_rows[h, :, :].rearrange("(r t) p -> r (t p)", r=2))).then_inc(L.rb_in[u], 16)

            def load_z(h, u):
                e.dma_start(L.zh[u][:, :, 0:L.D], by_tile(z_heads[h, :, :])).then_inc(L.z_in[u], 16)

            if L.H == 1:
                load_el(0, 0)
                move_r(0, 0, 0)
                return
            load_el(0, 0)
            load_el(1, 1)
            if L.batched:
                load_er(0, 0)
                load_er(1, 1)
                lay_r2(0, 0, 0, True, True)
                lay_r2(1, 1, 0, False, True)

                def rows_of(h, u, i, more):
                    e.wait_ge(L.relued, L.since["relued"] + 2 * T * (h - 1))
                    apart(e)
                    load_er(h, u)
                    lay_r2(h, u, i, False, more)
                with e.Fori(1, L.H // 2 - 1) as i:
                    for u in range(2):
                        rows_of(2 * i + u, u, i, True)
                for u in range(2):
                    rows_of(L.H - 2 + u, u, L.H // 2 - 1, False)
                return
            if L.spill:
                for u in range(2):
                    e.wait_ge(L.spilled[u], L.since["spilled"][u] + 16 * HT)
                e.wait_ge(L.ones, L.since["ones"] + 1)
                load_z(0, 0)
            move_r(0, 0, 0)
            load_z(1, 1)
            move_r(1, 1, 0)
            with e.Fori(1, L.H // 2) as i:
                for u in range(2):
                    h = 2 * i + u
                    e.wait_ge(L.r_ready, L.since["r_ready"] + h - 1)
                    load_el(h, u)
                    e.wait_ge(L.p_free, L.since["p_free"] + 2 * h)
                    load_z(h, u)
                    e.wait_ge(L.e_ready, L.since["e_ready"] + 2 + 2 * T * (h - 1))
                    apart(e)
                    move_r(h, u, i)

        def span(e, M, x):
            return (e.value_load(M.span[0:1, bass.ds(x, 1)], min_val=0, max_val=MAX_TILES),
                    e.value_load(M.span[0:1, bass.ds(x + EX, 1)], min_val=0, max_val=MAX_TILES))

        def all_tiles(e, M):
            return e.value_load(M.span[0:1, 2 * EX - 1:2 * EX], min_val=1, max_val=MAX_TILES)

        def moe_sync(e, M, before, following):
            def load_w(x, u):
                e.dma_start(M.w1s[u], M.w1[x, :, :].rearrange("(k p) i -> p k i", p=128)).then_inc(M.w_in[u], 16)
                e.dma_start(M.w2s[u], M.w2[x, :, :].rearrange("(k p) f -> p k f", p=128)).then_inc(M.w_in[u], 16)

            e.wait_ge(y_clear, 16 * (MAX_TILES - MIN_TILES))
            previous_stored(e, before)
            e.dma_start(M.lanes, over(A["lanes"])).then_inc(M.c_in, 16)
            e.dma_start(M.wr, M.router.rearrange("(k p) e -> p k e", p=128)).then_inc(M.c_in, 16)
            e.dma_start(M.rbias, over(M.raw_bias)).then_inc(M.c_in, 16)
            e.dma_start(M.order, over(A["order"])).then_inc(M.c_in, 16)
            e.dma_start(M.steps, over(A["steps"])).then_inc(M.c_in, 16)
            e.dma_start(M.node, A["node_ids"]).then_inc(M.c_in, 16)
            e.dma_start(M.before, A["before"]).then_inc(M.c_in, 16)
            if M.bias:
                e.dma_start(M.b1, A["L1_b1"]).then_inc(M.c_in, 16)
                e.dma_start(M.b2, A["L1_ffn_b2"]).then_inc(M.c_in, 16)
            with e.Fori(0, HT) as i:
                for u in range(2):
                    t = 2 * i + u
                    e.wait_ge(M.raw_free, t + 1)
                    e.dma_start(M.acc[:, t, :], by_tile(M.res)[:, t, :]).then_inc(M.x_in[u], 16)
                    e.dma_start(M.rawt[u], by_tile(M.raw)[:, t, :]).then_inc(M.x_in[u], 16)

            load_w(0, 0)
            load_w(1, 1)
            e.wait_ge(M.placed, 1)
            def store_outputs(x):
                lo, hi = span(e, M, x)
                with e.Fori(lo, hi) as g:
                    e.wait_ge(M.y_sb, g + 2)
                    apart(e)
                    e.dma_start(y_rows.rearrange("(g p) f -> p g f", p=ST)[:, g, :], M.y).then_inc(M.y_out, 16)

            with e.Fori(0, EX // 2 - 1) as i:
                for u in range(2):
                    store_outputs(2 * i + u)
                    e.wait_ge(M.w_free, 2 * i + u + 1)
                    apart(e)
                    load_w(2 * i + u + 2, u)
            for u in range(2):
                store_outputs(EX - 2 + u)
            if following is not None:
                n = all_tiles(e, M)
                e.wait_ge(M.w_free, EX)
                e.wait_ge(M.y_out, 16 * n + 16)
                apart(e)
                e.wait_ge(M.xg_sb, n + 1)
                apart(e)
                load_projection(e, following, 0)
            with e.Fori(0, T) as t:
                e.wait_ge(M.y_done, t + 1)
                e.dma_start(by_tile(M.dst)[:, t, :], M.acc[:, t, :]).then_inc(M.stored, 16)
            if following is not None:
                load_projection(e, following, 1)
            e.wait_ge(M.stored, 16 * T)

        def previous_stored(e, L):
            for u in range(2):
                e.wait_ge(L.stored[u], L.since["stored"][u] + L.totals["stored"][u])

        def p_is_free(e, L):
            e.wait_ge(L.p_free, L.since["p_free"] + 2 + 2 * L.H)

        def gat_to_gat(e, L, following):
            e.wait_ge(L.p_free, L.since["p_free"] + 2 + 2 * L.H - 1)
            load_projection(e, following, 0)
            if following.KT * following.F > T * HALF:
                p_is_free(e, L)
            load_projection(e, following, 1)
            previous_stored(e, L)
            gat_sync(e, following)

        @block.sync
        def _(e):
            graph_sync(e)
            for part in range(2):
                load_projection(e, layers[0], part)
            e.wait_ge(gs["at_sb"], 3 * T)
            e.wait_ge(gs["bias"], T)
            gat_sync(e, layers[0])
            gat_to_gat(e, layers[0], layers[1])
            gat_to_gat(e, layers[1], layers[2])
            p_is_free(e, layers[2])
            moe_sync(e, moes[0], layers[2], layers[3])
            gat_sync(e, layers[3])
            gat_to_gat(e, layers[3], layers[4])
            p_is_free(e, layers[4])
            moe_sync(e, moes[1], layers[4], None)

        def gat_gpsimd(e, L):
            if L.spill:
                with e.Fori(0, HT) as i:
                    for u in range(2):
                        t = 2 * i + u
                        e.wait_ge(L.z_ready, L.since["z_ready"] + RING + len(L.chunks) * (t + 1))
                        e.dma_start(z_heads[:, :, :].rearrange("h (t p) f -> p t h f", p=P)[:, t, :, :],
                                    L.stage[u]).then_inc(L.spilled[u], 16)

            def store(h):
                for half in range(2):
                    if L.batched:
                        e.wait_ge(L.out_done, L.since["out_done"] + 2 + 2 * h + half + 1)
                        e.dma_start(by_tile(L.dst)[:, half * HT:(half + 1) * HT, bass.ds(h * 64, 64)],
                                    L.og[half][:, 0:HT * 64].rearrange("p (t f) -> p t f", t=HT)).then_inc(L.stored[half], 16)
                        continue
                    for d in range(HT):
                        j = half * HT + d
                        e.wait_ge(L.out_done, L.since["out_done"] + 2 + T * h + j + 1)
                        e.dma_start(by_tile(L.dst)[:, j, bass.ds(h * L.D, L.D)],
                                    L.og[j % 2][:, 0:L.D]).then_inc(L.stored[j % 2], 16)

            if L.H == 1:
                store(0)
            else:
                with e.Fori(0, L.H) as h:
                    store(h)

        def moe_gpsimd(e, M):
            e.wait_ge(y_clear, 16 * (MAX_TILES - MIN_TILES))
            e.wait_ge(M.c_in, 144 if M.bias else 112)
            for u in range(2):
                e.wait_ge(M.xn_out[u], 16 + 16 * HT)
            e.wait_ge(M.listed, 1)
            at = bass.IndirectOffsetOnAxis(ap=M.rows, axis=0)
            e.tensor_copy(M.rows, M.list[:, 0:1]).then_inc(M.rows_ready, 1)
            e.wait_ge(M.rows_ready, 1)
            e.indirect_dma_start(M.xg[:, :], None, xn_rows[:, :], at).then_inc(M.xg_in, 16)
            n = all_tiles(e, M)
            with e.Fori(0, n) as g:
                e.wait_ge(M.xg_in, 16 * g + 16)
                apart(e)
                e.tensor_copy(M.rows, M.list[:, bass.ds(g + 1, 1)]).then_inc(M.rows_ready, 1)
                e.wait_ge(M.rows_ready, g + 2)
                e.wait_ge(M.xg_ready, g + 1)
                apart(e)
                e.indirect_dma_start(M.xg[:, :], None, xn_rows[:, :], at).then_inc(M.xg_in, 16)
            e.wait_ge(M.y_out, 16 * n + 16)
            apart(e)
            for t in range(T):
                if t >= 4:
                    e.wait_ge(M.y_done, t - 3)
                for k in range(2):
                    at = bass.IndirectOffsetOnAxis(ap=M.slot_i[:, k * T + t:k * T + t + 1], axis=0)
                    e.indirect_dma_start(M.yg[t % 4][k], None, y_rows[:, :], at).then_inc(M.yg_in[t % 4], 16)

        @block.gpsimd
        def _(e):
            e.sem_inc(gs["oh"], PER * GROUPS)
            e.sem_inc(gs["used"], PER * GROUPS + PER)
            L = layers[0]
            e.sem_inc(L.x_free, 2)
            e.sem_inc(L.e_free, 2)
            e.sem_inc(L.p_free, 2)
            e.sem_inc(L.p_ready, 4)
            e.sem_inc(L.scored, 2)
            e.sem_inc(L.out_done, 2)
            with e.Fori(MIN_TILES, MAX_TILES) as g:
                e.dma_start(y_rows.rearrange("(g p) f -> p g f", p=ST)[:, g, :], A["no_outputs"]).then_inc(y_clear, 16)
            for M in moes:
                e.sem_inc(M.raw_free, 2)
                e.sem_inc(M.y_sb, 1)
                e.sem_inc(M.h_sb, 1)
                e.sem_inc(M.y_out, 16)
            for L in layers[0:3]:
                gat_gpsimd(e, L)
            moe_gpsimd(e, moes[0])
            for L in layers[3:5]:
                gat_gpsimd(e, L)
            moe_gpsimd(e, moes[1])

        def graph_tensor(e):
            e.wait_ge(gs["float"], 2)
            for w in range(2):
                for a in range(PER):
                    ins = e.transpose(banks[7][0:EP, (PER * w + a) * GROUPS:(PER * w + a + 1) * GROUPS],
                                      e_f[w][:, a * EP:(a + 1) * EP], ident[0:GROUPS, 0:GROUPS])
            ins.then_inc(gs["et_ready"], 1)
            e.wait_ge(gs["rng"], 1)
            e.wait_ge(gs["et_sb"], 1)
            e.transpose(banks[7][0:2 * T, 0:GROUPS], rng, ident[0:GROUPS, 0:GROUPS]).then_inc(gs["rng_t"], 1)
            e.wait_ge(gs["red"], 1)
            e.transpose(banks[6][0:1, 0:2 * T], red, ident[0:2 * T, 0:2 * T]).then_inc(gs["red_t"], 1)
            e.wait_ge(gs["tab"], 1)
            e.wait_ge(gs["zero"], 1)
            for b in range(T):
                lo = e.value_load(tab[0:1, b:b + 1], min_val=0, max_val=GROUPS - 1)
                hi = e.value_load(tab[0:1, T + b:T + b + 1], min_val=1, max_val=GROUPS)
                before = e.value_load(tab[0:1, 2 * T + b:2 * T + b + 1], min_val=0, max_val=T * GROUPS)
                acc = [banks[3 * (b % 2) + c][0:P, 0:w] for c, (_, w) in enumerate(cuts)]
                if b >= 2:
                    e.wait_ge(gs["blk_sb"], b - 1)
                for c, (_, w) in enumerate(cuts):
                    e.matmul(acc[c], zero[:, 0:P], zero[:, P:P + w], start=True, stop=False)
                with e.Fori(lo, hi) as j:
                    for u in range(PER):
                        e.wait_ge(gs["oh"], PER * (before + j) + u + 1)
                        for c, (at, w) in enumerate(cuts):
                            ins = e.matmul(acc[c], oh_d[u], oh_s[u][:, at:at + w], start=False, stop=False)
                        ins.then_inc(gs["used"], 1)
                for c, (_, w) in enumerate(cuts):
                    ins = e.matmul(acc[c], zero[:, 0:P], zero[:, P:P + w], start=False, stop=True)
                ins.then_inc(gs["blk_ready"], 1)
                if b >= 1:
                    graph_turn(e, b - 1)
            graph_turn(e, T - 1)

        def graph_turn(e, b):
            e.wait_ge(gs["blk_sb"], b + 1)
            for g in range(3):
                if 3 * b + g >= 2:
                    e.wait_ge(gs["at_sb"], 3 * b + g - 1)
                bank = banks[6 + (3 * b + g) % 2]
                for s in range(4 * g, min(T, 4 * g + 4)):
                    ins = e.transpose(bank[0:P, (s % 4) * P:(s % 4 + 1) * P], a_blk[b % 2][:, s * P:(s + 1) * P],
                                      ident[0:P, 0:P])
                ins.then_inc(gs["at_ready"], 1)

        def two_ahead(e, body):
            with e.Fori(0, HT - 1) as i:
                for u in range(2):
                    body(2 * i + u, u, False)
            for t in (T - 2, T - 1):
                body(t, t % 2, True)

        def block_exponents(j):
            mid = (5 + 2 * (j % 2)) * 512
            return psum[0:P, mid - CUT:mid - CUT + HALF]

        def gat_tensor(e, L):
            G, NC = len(L.groups), len(L.chunks)

            def transposes(t, u):
                e.wait_ge(L.prepped, L.since["prepped"] + t + 1)
                for g, (k0, n) in enumerate(L.groups):
                    e.wait_ge(L.xt_ready, L.since["xt_ready"] + G * t + g + 1)
                    for k in range(n):
                        ins = e.transpose(banks[g % 2][:, k * P:(k + 1) * P],
                                          L.xin[u][:, (k0 + k) * 128:(k0 + k + 1) * 128], ident[0:P, 0:P])
                    ins.then_inc(L.tp_ready, 1)

            def project(t, u):
                e.wait_ge(L.xt_ready, L.since["xt_ready"] + 2 + G * (t + 1))
                for c, (at, w) in enumerate(L.chunks):
                    bank = banks[2 + (u * NC + c) % L.ring]
                    e.wait_ge(L.z_ready, L.since["z_ready"] + RING - L.ring + NC * t + c + 1)
                    for k in range(L.KT):
                        ins = e.matmul(bank[0:P, 0:w], L.xt[u][:, k, :], L.w_sb[:, k, at:at + w],
                                       start=(k == 0), stop=(k == L.KT - 1))
                        if c == 0 and k == 0:
                            ins.then_inc(L.x_free, 1)
                    ins.then_inc(L.zp_ready, 1)

            transposes(0, 0)
            for c in range(2):
                e.wait_ge(L.w_in[c], L.since["w_in"][c] + 16)

            def both(t, u, last):
                if not (last and u == 1):
                    transposes(t + 1, 1 - u)
                project(t, u)
            two_ahead(e, both)

            for g in range(3):
                if g == 0:
                    e.wait_ge(L.scored, L.since["scored"] + 2 + T)
                    e.wait_ge(L.z_ready, L.since["z_ready"] + RING + NC * T)
                if g == 2:
                    e.wait_ge(L.elt_sb, L.since["elt_sb"] + 1)
                for t in range(4 * g, min(T, 4 * g + 4)):
                    ins = e.transpose(banks[g % 2][0:2 * L.H, (t % 4) * P:(t % 4 + 1) * P], L.elr[:, t, :], ident[0:P, 0:P])
                ins.then_inc(L.elt_ready, 1)

            def turn_r(h, u):
                e.wait_ge(L.r_ready, L.since["r_ready"] + h + 1)
                if not isinstance(h, int) or h > 0:
                    e.wait_ge(L.rt_sb, L.since["rt_sb"] + h)
                e.transpose(banks[0][0:2 * T, 0:P], small[0:P, 64 + u * 2 * T:64 + (u + 1) * 2 * T], ident[0:P, 0:P]).then_inc(L.rt_ready, 1)

            def aggregate(h, u, i, last):
                if L.spill:
                    e.wait_ge(L.z_in[u], L.since["z_in"][u] + 16 * (i + 1))
                for half in range(2):
                    for d in range(HT):
                        j = half * HT + d
                        e.wait_ge(L.out_done, L.since["out_done"] + T * h + j + 1)
                        for c, (at, w) in enumerate(L.cols):
                            for s in range(T):
                                if d == 0 and c == 0:
                                    e.wait_ge(L.p_ready, L.since["p_ready"] + 4 + 2 * T * h + half * T + s + 1)
                                ins = e.matmul(banks[2 + 2 * (j % 2) + c][0:P, 0:w], Ph[half][:, s, d * P:(d + 1) * P],
                                               (L.zh[u] if L.spill else L.z)[:, s, at:at + w], start=(s == 0), stop=(s == T - 1))
                        ins.then_inc(L.ag_ready, 1)
                        if j == 1 and not last:
                            turn_r(h + 1, 1 - u)
                    e.matmul(banks[6][0:1, 0:1], ident[:, 0:1], ident[:, 0:1], start=True, stop=True).then_inc(L.p_free, 1)

            def exponents(h, j):
                half, s = j // T, j % T
                if s == 0:
                    e.wait_ge(L.r2_in[half], L.since["r2_in"][half] + 48 * (h + 1))
                e.wait_ge(L.relued, L.since["relued"] + 2 * T * h + j + 1)
                e.wait_ge(L.e_ready, L.since["e_ready"] + 2 * T * h + j + 1)
                o = block_exponents(j)
                for at, to in ((0, CUT), (CUT, HALF)):
                    ins = e.matmul(o[:, at:to], spread[:, :], L.r2[half][:, s % 3, at:to], start=True, stop=True)
                ins.then_inc(L.t_ready, 1)

            def sum_tile(h, half, d, part):
                if d == 0 and part == 0:
                    e.wait_ge(L.out_done, L.since["out_done"] + 2 * h + half + 1)
                if d == 0:
                    e.wait_ge(L.p_ready, L.since["p_ready"] + 4 + 2 * T * h + half * T + (part + 1) * HT)
                for s in range(part * HT, (part + 1) * HT):
                    ins = e.matmul(banks[2 + half][0:P, d * 65:(d + 1) * 65], Ph[half][:, s, d * P:(d + 1) * P], L.z[:, s, h, :],
                                   start=(s == 0), stop=(s == T - 1))
                if d == HT - 1 and part == 1:
                    ins.then_inc(L.ag_ready, 1)
                    e.matmul(banks[1][0:1, 0:1], ident[:, 0:1], ident[:, 0:1], start=True, stop=True).then_inc(L.p_free, 1)

            def batched_head(h, u, first, last):
                for j in range(2 * T):
                    half, s = j // T, j % T
                    if s not in ADD_AT:
                        exponents(h, j)
                    if not (first and half == 0):
                        sum_tile(h if half else h - 1, 1 - half, s // 2, s % 2)
                    if j == TURN_EARLY and not last:
                        turn_r(h + 1, 1 - u)

            turn_r(0, 0)
            if L.batched:
                batched_head(0, 0, True, False)
                batched_head(1, 1, False, False)
                with e.Fori(1, L.H // 2 - 1) as i:
                    for u in range(2):
                        batched_head(2 * i + u, u, False, False)
                batched_head(L.H - 2, 0, False, False)
                batched_head(L.H - 1, 1, False, True)
                for d in range(HT):
                    for part in range(2):
                        sum_tile(L.H - 1, 1, d, part)
                return
            if L.H == 1:
                aggregate(0, 0, 0, True)
                return
            with e.Fori(0, L.H // 2 - 1) as i:
                aggregate(2 * i, 0, i, False)
                aggregate(2 * i + 1, 1, i, False)
            aggregate(L.H - 2, 0, L.H // 2 - 1, False)
            aggregate(L.H - 1, 1, L.H // 2 - 1, True)

        def moe_tensor(e, M):
            e.wait_ge(M.c_in, 144 if M.bias else 112)

            def transposes(t):
                e.wait_ge(M.prepped, t + 1)
                for g in range(2):
                    e.wait_ge(M.xt_ready, 2 * t + g + 2)
                    for k in range(4 * g, min(CK, 4 * g + 4)):
                        ins = e.transpose(banks[g][:, (k % 4) * P:(k % 4 + 1) * P],
                                          M.xn[t % 2][:, k * 128:(k + 1) * 128], ident[0:P, 0:P])
                    ins.then_inc(M.tp_ready, 1)

            transposes(0)
            for t in range(T):
                if t + 1 < T:
                    transposes(t + 1)
                e.wait_ge(M.xt_ready, 3 + 2 * (t + 1))
                for k in range(CK):
                    ins = e.matmul(banks[2][0:P, t * EX:(t + 1) * EX], M.xt[:, k, t * P:(t + 1) * P], M.wr[:, k, :],
                                   start=(k == 0), stop=(k == CK - 1))
            ins.then_inc(M.lg_ready, 1)

            if M.balanced:
                e.wait_ge(M.probs, 1)
                e.matmul(banks[3][0:P, 0:T * EX], M.onesq, M.gflat[1], start=True, stop=True).then_inc(M.imp_ready, 1)
            e.wait_ge(M.picked, 1)
            e.matmul(banks[4][0:P, 0:T * EX], M.before, M.gflat[7], start=True, stop=True)
            e.matmul(banks[4][0:P, T * EX:2 * T * EX], M.onesq, M.gflat[7], start=True, stop=True).then_inc(M.counts, 1)

            def transposes_of(g):
                e.wait_ge(M.xg_in, 16 * g + 16)
                apart(e)
                for k in range(CK):
                    ins = e.transpose(banks[k // 4][:, (k % 4) * ST:(k % 4 + 1) * ST], M.xg[:, k * 128:(k + 1) * 128], ident[:, :])
                ins.then_inc(M.xg_ready, 1)
            e.wait_ge(M.placed, 1)
            for j in range(2 * T):
                ins = e.matmul(banks[5][:, 0:LIST], M.in_row[:, j, :], M.in_tile[:, j, :], start=(j == 0), stop=(j == 2 * T - 1))
            ins.then_inc(M.list_ready, 1)
            e.wait_ge(M.gates, 1)
            transposes_of(0)

            def expert(x, u, i):
                e.wait_ge(M.w_in[u], 32 * (i + 1))
                lo, hi = span(e, M, x)
                with e.Fori(lo, hi) as g:
                    e.wait_ge(M.xg_sb, g + 1)
                    apart(e)
                    for ci in range(M.IC):
                        for k in range(CK):
                            ins = e.matmul(banks[6][:, ci * ST:(ci + 1) * ST], M.w1s[u][:, k, ci * 128:(ci + 1) * 128], M.xgt[:, k, :],
                                           start=(k == 0), stop=(k == CK - 1))
                    ins.then_inc(M.h_ready, 1)
                    transposes_of(g + 1)
                    e.wait_ge(M.h_sb, g + 2)
                    e.wait_ge(M.y_sb, g + 1)
                    apart(e)
                    for c in range(2):
                        for ci in range(M.IC):
                            ins = e.matmul(banks[2 + c][:, 0:C // 2], M.ht[:, ci, :], M.w2s[u][:, ci, c * (C // 2):(c + 1) * (C // 2)],
                                           start=(ci == 0), stop=(ci == M.IC - 1))
                    ins.then_inc(M.y_ready, 1)
                e.matmul(banks[7][0:1, 0:1], ident[:, 0:1], ident[:, 0:1], start=True, stop=True).then_inc(M.w_free, 1)
            with e.Fori(0, EX // 2) as i:
                for u in range(2):
                    expert(2 * i + u, u, i)
            if M.bias:
                n = all_tiles(e, M)
                e.wait_ge(M.xg_sb, n + 1)
                apart(e)
                def turn_gates(t):
                    if t >= 2:
                        e.wait_ge(M.gt_sb, t - 1)
                    e.transpose(banks[t % 2][0:EX, 0:P], M.g[6][:, t, :], ident[0:P, 0:P]).then_inc(M.gt_ready, 1)
                turn_gates(0)
                for t in range(T):
                    if t + 1 < T:
                        turn_gates(t + 1)
                    e.wait_ge(M.gt_sb, t + 1)
                    if t >= 2:
                        e.wait_ge(M.gb_free, t - 1)
                    for c in range(2):
                        ins = e.matmul(banks[4 + 2 * (t % 2) + c][0:P, 0:C // 2], M.gt[t % 2], M.b2[:, c * (C // 2):(c + 1) * (C // 2)],
                                       start=True, stop=True)
                    ins.then_inc(M.gb_ready, 1)

        @block.tensor
        def _(e):
            graph_tensor(e)
            for n in range(3):
                gat_tensor(e, layers[n])
            moe_tensor(e, moes[0])
            for n in range(3, 5):
                gat_tensor(e, layers[n])
            moe_tensor(e, moes[1])

        def graph_scalar(e):
            e.wait_ge(gs["et_ready"], 1)
            e.activation(e_t.rearrange("p w a j -> p (w a j)"), banks[7][0:EP, 0:2 * PER * GROUPS], ACT.Copy).then_inc(gs["et_sb"], 1)

            def turned(b):
                for g in range(3):
                    e.wait_ge(gs["at_ready"], 3 * b + g + 1)
                    n = min(4, T - 4 * g)
                    e.activation(AT[:, 4 * g:4 * g + n, b * P:(b + 1) * P],
                                 banks[6 + (3 * b + g) % 2][0:P, 0:n * P].rearrange("p (s d) -> p s d", s=n),
                                 ACT.Copy).then_inc(gs["at_sb"], 1)
            for b in range(T):
                e.wait_ge(gs["blk_ready"], b + 1)
                if b >= 2:
                    e.wait_ge(gs["bias"], b - 1)
                for c, (at, w) in enumerate(cuts):
                    ins = e.activation(a_blk[b % 2][:, at:at + w], banks[3 * (b % 2) + c][0:P, 0:w], ACT.Copy)
                ins.then_inc(gs["blk_sb"], 1)
                if b >= 1:
                    turned(b - 1)
            turned(T - 1)

        def gat_scalar(e, L):
            G, NC = len(L.groups), len(L.chunks)
            if L is layers[0]:
                e.sem_inc(L.xt_ready, 2)
                e.sem_inc(L.z_ready, RING)
                e.sem_inc(L.e_ready, 2)

            def mid(t, u):
                e.wait_ge(L.half_prep, L.since["half_prep"] + t + 1)
                if L.prep == "ln":
                    e.activation(small[0:P, 16 + 4 * u + 1:16 + 4 * u + 2], small[0:P, 16 + 4 * u:16 + 4 * u + 1], ACT.Sqrt).then_inc(L.mid, 1)
                else:
                    e.activation(L.low[u], L.low[u], ACT.Exp).then_inc(L.mid, 1)

            def turned(t, u):
                for g, (k0, n) in enumerate(L.groups):
                    e.wait_ge(L.tp_ready, L.since["tp_ready"] + G * t + g + 1)
                    e.activation(L.xt[u][:, k0:k0 + n, :], banks[g % 2][:, 0:n * P].rearrange("p (k n) -> p k n", k=n),
                                 ACT.Copy).then_inc(L.xt_ready, 1)

            def keep(t, u, i):
                for c, (at, w) in enumerate(L.chunks):
                    bank = banks[2 + (u * NC + c) % L.ring]
                    e.wait_ge(L.zp_ready, L.since["zp_ready"] + NC * t + c + 1)
                    if L.spill and c == 0:
                        e.wait_ge(L.scored, L.since["scored"] + t + 1)
                    if L.spill and c == 0 and not (isinstance(i, int) and i == 0):
                        e.wait_ge(L.spilled[u], L.since["spilled"][u] + 16 * i)
                    apart(e)
                    if L.batched:
                        o = L.z[:, t, at // 64:(at + w) // 64, 0:64]
                        s = bank[0:P, 0:w].rearrange("p (h f) -> p h f", f=64)
                    elif L.spill:
                        o, s = L.stage[u][:, c, :], bank[0:P, 0:w]
                    else:
                        o, s = L.z[:, t, at:at + w], bank[0:P, 0:w]
                    ins = e.activation(o, s, ACT.Copy)
                    ins.then_inc(L.z_ready, 1)

            mid(0, 0)
            mid(1, 1)
            turned(0, 0)
            def around(i):
                for u in range(2):
                    t = 2 * i + u
                    turned(t + 1, 1 - u)
                    mid(t + 2, u)
                    keep(t, u, i)
            if L.spill:
                around(0)
            with e.Fori(1 if L.spill else 0, HT - 1) as i:
                around(i)
            turned(T - 1, 1)
            keep(T - 2, 0, HT - 1)
            keep(T - 1, 1, HT - 1)
            for g in range(3):
                n = min(4, T - 4 * g)
                e.wait_ge(L.elt_ready, L.since["elt_ready"] + g + 1)
                e.activation(L.elt[0:2 * L.H, 4 * g * P:(4 * g + n) * P], banks[g % 2][0:2 * L.H, 0:n * P], ACT.Copy).then_inc(L.elt_sb, 1)
            e.wait_ge(L.el_out, L.since["el_out"] + 16)
            e.wait_ge(L.scaled, L.since["scaled"] + 1)

            def rows(h, u):
                e.wait_ge(L.rt_ready, L.since["rt_ready"] + h + 1)
                e.activation(L.rt[u], banks[0][0:2 * T, 0:P], ACT.Copy).then_inc(L.rt_sb, 1)

            def exps(h, u, i, js):
                for j in js:
                    half, s = j // T, j % T
                    if j == 0:
                        e.wait_ge(L.rb_in[u], L.since["rb_in"][u] + 16 * (i + 1))
                    e.wait_ge(L.e_free, L.since["e_free"] + 2 * T * h + j + 1)
                    apart(e)
                    cols = slice(half * HALF, (half + 1) * HALF)
                    e.activation(L.e[j % 2][0], L.rb[u][:, 0, cols], ACT.Exp, bias=L.elr[:, s, bass.ds(h, 1)])
                    e.activation(L.e[j % 2][1], L.rb[u][:, 1, cols], ACT.Exp, bias=L.el2[:, s, bass.ds(h, 1)]).then_inc(L.e_ready, 1)

            def relu(h, u, i, j):
                half, s = j // T, j % T
                if j == 0:
                    e.wait_ge(L.er_in[u], L.since["er_in"][u] + 16 * (i + 1))
                apart(e)
                e.activation(L.r2[half][0:P, s % 3, :], L.erb[u][:, half * HALF:(half + 1) * HALF], ACT.Relu,
                             bias=L.el8[:, s, bass.ds(h, 1)], scale=1.0 - SLOPE).then_inc(L.relued, 1)

            def exponentials(h, j):
                half, s = j // T, j % T
                if s in ADD_AT:
                    e.wait_ge(L.added, L.since["added"] + ADDS * h + of_vector(j) + 1)
                    src = L.ex[j % 4]
                else:
                    e.wait_ge(L.t_ready, L.since["t_ready"] + TURNS * h + j - of_vector(j) + 1)
                    src = block_exponents(j)
                e.wait_ge(L.p_ready, L.since["p_ready"] + 2 * T * h + j + 1)
                apart(e)
                e.activation(L.ex[j % 4], src, ACT.Exp, bias=L.el2[:, s, bass.ds(h, 1)]).then_inc(L.e_ready, 1)

            def batched_head(h, u, i, last):
                for j in range(2 * T):
                    exponentials(h, j)
                    if j == ROWS_EARLY and not last:
                        rows(h + 1, 1 - u)
                    if j + 3 < 2 * T:
                        relu(h, u, i, j + 3)
                    elif not last:
                        relu(h + 1, 1 - u, i + u, j + 3 - 2 * T)

            if L.batched:
                relu(0, 0, 0, 0)
                relu(0, 0, 0, 1)
                relu(0, 0, 0, 2)
            rows(0, 0)
            if L.batched:
                with e.Fori(0, L.H // 2 - 1) as i:
                    for u in range(2):
                        batched_head(2 * i + u, u, i, False)
                batched_head(L.H - 2, 0, L.H // 2 - 1, False)
                batched_head(L.H - 1, 1, L.H // 2 - 1, True)
                return
            if L.H == 1:
                exps(0, 0, 0, range(2 * T))
                return
            with e.Fori(0, L.H // 2 - 1) as i:
                for u in range(2):
                    h = 2 * i + u
                    exps(h, u, i, range(ROWS_AT))
                    rows(h + 1, 1 - u)
                    exps(h, u, i, range(ROWS_AT, 2 * T))
            i = L.H // 2 - 1
            exps(L.H - 2, 0, i, range(ROWS_AT))
            rows(L.H - 1, 1)
            exps(L.H - 2, 0, i, range(ROWS_AT, 2 * T))
            exps(L.H - 1, 1, i, range(2 * T))

        def moe_scalar(e, M):
            e.sem_inc(M.xt_ready, 3)
            for u in range(2):
                e.sem_inc(M.xn_out[u], 16)

            def root(t, u):
                e.wait_ge(M.half_prep, t + 1)
                e.activation(small[0:P, 16 + 4 * u + 1:16 + 4 * u + 2], small[0:P, 16 + 4 * u:16 + 4 * u + 1], ACT.Sqrt).then_inc(M.mid, 1)

            def keep(t, u):
                for g in range(2):
                    n = min(4, CK - 4 * g)
                    e.wait_ge(M.tp_ready, 2 * t + g + 1)
                    apart(e)
                    e.activation(M.xt[:, 4 * g:4 * g + n, bass.ds(t * P, P)],
                                 banks[g][:, 0:n * P].rearrange("p (k n) -> p k n", k=n), ACT.Copy).then_inc(M.xt_ready, 1)
                e.dma_start(by_tile(xn_rows)[:, t, :], M.xn[u]).then_inc(M.xn_out[u], 16)

            def prep(t, u, last):
                if not (last and u == 1):
                    root(t + 1, 1 - u)
                keep(t, u)
            root(0, 0)
            two_ahead(e, prep)
            e.wait_ge(M.exp_in, 1)
            e.activation(M.gflat[0], M.gflat[0], ACT.Exp).then_inc(M.exped, 1)

            def keep_rows(g):
                e.wait_ge(M.xg_ready, g + 1)
                apart(e)
                e.activation(M.xgt[:, 0:4, :], banks[0][:, 0:4 * ST].rearrange("p (k n) -> p k n", k=4), ACT.Copy)
                e.activation(M.xgt[:, 4:CK, :], banks[1][:, 0:(CK - 4) * ST].rearrange("p (k n) -> p k n", k=CK - 4),
                             ACT.Copy).then_inc(M.xg_sb, 1)
            e.wait_ge(M.placed, 1)
            keep_rows(0)

            def expert(x):
                lo, hi = span(e, M, x)
                with e.Fori(lo, hi) as g:
                    if not M.bias:
                        e.wait_ge(M.h_sb, g + 1)
                        apart(e)
                        e.activation(small[0:P, 100:101], M.onesq[:, 0:1], ACT.Silu)
                    e.wait_ge(M.h_ready, g + 1)
                    apart(e)
                    for ci in range(M.IC):
                        src = banks[6][:, ci * ST:(ci + 1) * ST]
                        if M.bias:
                            ins = e.activation(M.ht[:, ci, :], src, ACT.Relu, bias=M.b1[:, bass.ds(x, 1), ci])
                        else:
                            ins = e.activation(M.ht[:, ci, :], src, ACT.Silu)
                    ins.then_inc(M.h_sb, 1)
                    keep_rows(g + 1)
            with e.Fori(0, EX) as x:
                expert(x)
            if M.bias:
                for t in range(T):
                    e.wait_ge(M.gt_ready, t + 1)
                    if t >= 2:
                        e.wait_ge(M.gb_ready, t - 1)
                    e.activation(M.gt[t % 2], banks[t % 2][0:EX, 0:P], ACT.Copy).then_inc(M.gt_sb, 1)

        @block.scalar
        def _(e):
            graph_scalar(e)
            for n in range(3):
                gat_scalar(e, layers[n])
            moe_scalar(e, moes[0])
            for n in range(3, 5):
                gat_scalar(e, layers[n])
            moe_scalar(e, moes[1])

        def graph_vector(e, st):
            e.wait_ge(gs["in"], 16 * 6)
            st.add(e.memset(zero, 0.0))
            for w in range(2):
                e.tensor_copy(e_f[w], e_nat[w]).then_inc(gs["float"], 1)
            e.wait_ge(gs["float"], 2)
            for b in range(T + 1):
                st.wait()
                st.add(e.tensor_scalar(gjunk, e_f[0], b * P - 0.5, None, ALU.is_ge, ALU.add, accum_out=ge[:, b:b + 1]))
            st.wait()
            st.add(e.tensor_tensor(has, ge[:, 0:T], ge[:, 1:T + 1], ALU.not_equal))
            st.wait()
            st.add(e.tensor_scalar(rng[:, 0:T], has, lim[:, 0:1], None, ALU.mult))
            e.tensor_scalar(rng[:, T:2 * T], has, lim[:, 1:2], None, ALU.mult).then_inc(gs["rng"], 1)
            e.wait_ge(gs["rng_t"], 1)
            e.tensor_reduce(red, banks[7][0:2 * T, 0:GROUPS], AX.X, ALU.max).then_inc(gs["red"], 1)
            e.wait_ge(gs["red_t"], 1)
            st.add(e.tensor_scalar(row[:, 0:T], banks[6][0:1, 0:T], -1.0, float(GROUPS), ALU.mult, ALU.add))
            st.wait()
            st.add(e.tensor_scalar(tab_f[:, 0:T], row[:, 0:T], float(GROUPS - 1), None, ALU.min))
            st.wait()
            st.add(e.tensor_scalar(row[:, T:2 * T], tab_f[:, 0:T], 1.0, None, ALU.add))
            st.wait()
            st.add(e.tensor_tensor(tab_f[:, T:2 * T], row[:, T:2 * T], banks[6][0:1, T:2 * T], ALU.max))
            st.wait()
            st.add(e.tensor_tensor(row[:, 0:T], tab_f[:, T:2 * T], tab_f[:, 0:T], ALU.subtract))
            st.add(e.memset(tab_f[:, 3 * T:4 * T], 0.0))
            st.wait()
            for b in range(1, T):
                st.add(e.tensor_tensor(tab_f[:, 3 * T + b:3 * T + b + 1], tab_f[:, 3 * T + b - 1:3 * T + b], row[:, b - 1:b], ALU.add))
                st.wait()
            st.add(e.tensor_tensor(row[:, 0:T], tab_f[:, 3 * T:4 * T], tab_f[:, 0:T], ALU.subtract))
            st.wait()
            st.add(e.tensor_scalar(tab_f[:, 2 * T:3 * T], row[:, 0:T], float(GROUPS), None, ALU.add))
            st.wait()
            e.tensor_copy(tab, tab_f).then_inc(gs["tab"], 1)
            st.add(e.tensor_scalar(noti[:, :], ident[0:P, 0:P], 0.0, None, ALU.is_equal))
            e.wait_ge(gs["et_sb"], 1)
            e.wait_ge(gs["tab"], 1)
            st.wait()
            e.engine_nop().then_inc(gs["zero"], 1)
            for b in range(T):
                lo = e.value_load(tab[0:1, b:b + 1], min_val=0, max_val=GROUPS - 1)
                hi = e.value_load(tab[0:1, T + b:T + b + 1], min_val=1, max_val=GROUPS)
                before = e.value_load(tab[0:1, 2 * T + b:2 * T + b + 1], min_val=0, max_val=T * GROUPS)
                with e.Fori(lo, hi) as j:
                    for u in range(PER):
                        e.wait_ge(gs["used"], PER * (before + j) + u + 1)
                        apart(e)
                        e.tensor_scalar(oh_d[u], iota[:, b * P:(b + 1) * P], e_t[:, 0, u, bass.ds(j, 1)], None, ALU.is_equal)
                        e.tensor_scalar(oh_s[u], iota, e_t[:, 1, u, bass.ds(j, 1)], None, ALU.is_equal).then_inc(gs["oh"], 1)
                if b >= 2:
                    graph_bias(e, b - 2)
            graph_bias(e, T - 2)
            graph_bias(e, T - 1)

        def graph_bias(e, b):
            e.wait_ge(gs["blk_sb"], b + 1)
            e.wait_ge(gs["at_ready"], 3 * (b + 1))
            e.tensor_scalar(MB[:, b, :], a_blk[b % 2], 0.0, NONE, ALU.is_equal, ALU.mult).then_inc(gs["bias"], 1)

        def add_loops(e):
            for t in range(T):
                e.tensor_tensor(AT[:, t, t * P:(t + 1) * P], AT[:, t, t * P:(t + 1) * P], ident[0:P, 0:P], ALU.add)
                e.tensor_tensor(MB[:, t, t * P:(t + 1) * P], MB[:, t, t * P:(t + 1) * P], noti[:, :], ALU.mult).then_inc(gs["loops"], 1)

        def norm_a(e, st, x, u, done):
            apart(e)
            stats = small[0:P, 0:12].rearrange("p (a b) -> p a b", a=2)
            for a in range(2):
                st.add(e.bn_stats(stats[:, a, :], x[:, a * (C // 2):(a + 1) * (C // 2)]))
            st.wait()
            apart(e)
            st.add(e.bn_aggr(small[0:P, 24 + 2 * u:26 + 2 * u], stats))
            st.wait()
            e.tensor_scalar(small[0:P, 16 + 4 * u:16 + 4 * u + 1], small[0:P, 25 + 2 * u:26 + 2 * u], EPS, None, ALU.add).then_inc(done, 1)

        def norm_b(e, st, o, x, u, root, root_at, done):
            e.wait_ge(root, root_at)
            inv = small[0:P, 16 + 4 * u + 2:16 + 4 * u + 3]
            st.add(e.reciprocal(inv, small[0:P, 16 + 4 * u + 1:16 + 4 * u + 2]))
            st.wait()
            e.tensor_scalar(o, x, small[0:P, 24 + 2 * u:25 + 2 * u], inv, ALU.subtract, ALU.mult).then_inc(done, 1)

        def gat_vector(e, st, L):
            e.wait_ge(L.v_in, L.since["v_in"] + L.vectors)
            if not L.spill:
                e.memset(L.z_ones, 1.0).then_inc(L.ones, 1)

            def prep(t, u, i):
                e.wait_ge(L.x_in[u], L.since["x_in"][u] + 16 * (i + 1))
                x = L.xin[u]
                if L.prep == "ln":
                    norm_a(e, st, x, u, L.half_prep)
                    norm_b(e, st, x, x, u, L.mid, L.since["mid"] + t + 1, L.prepped)
                    return
                st.add(e.tensor_tensor(x, x, L.xbias, ALU.add))
                st.wait()
                e.tensor_scalar(L.low[u], x, 0.0, None, ALU.min).then_inc(L.half_prep, 1)
                e.wait_ge(L.mid, L.since["mid"] + t + 1)
                e.scalar_tensor_tensor(out=x, in0=L.low[u], scalar=-1.0, in1=x, op0=ALU.add, op1=ALU.max).then_inc(L.prepped, 1)

            def score(t, u):
                e.wait_ge(L.z_ready, L.since["z_ready"] + RING + len(L.chunks) * (t + 1))
                zt = L.z[:, t, :, 0:64] if L.batched else L.stage[u] if L.spill else L.z[:, t, 0:C].rearrange("p (h d) -> p h d", h=1)
                for r in range(2):
                    st.wait()
                    st.add(e.tensor_tensor(L.prod, zt, L.al_b[r], ALU.mult))
                    st.wait()
                    ins = e.tensor_reduce(L.elr[:, t, r * L.H:(r + 1) * L.H], L.prod, AX.X, ALU.add)
                    if r == 0:
                        st.add(ins)
                ins.then_inc(L.scored, 1)
                e.wait_ge(L.scored, L.since["scored"] + 2 + t + 1)

            prep(0, 0, 0)
            prep(1, 1, 0)
            with e.Fori(0, HT - 1) as i:
                st.enter(i, 6 + (8 if L.prep == "ln" else 2))
                for u in range(2):
                    prep(2 * i + 2 + u, u, i + 1)
                    score(2 * i + u, u)
                st.leave(HT - 1)
            score(T - 2, 0)
            score(T - 1, 1)

            st.add(e.tensor_scalar(L.el2, L.elr[:, :, 0:L.H], SLOPE, None, ALU.mult))
            e.tensor_scalar(L.el8, L.elr[:, :, 0:L.H], 1.0 - SLOPE, None, ALU.mult).then_inc(L.scaled, 1)
            e.wait_ge(L.scaled, L.since["scaled"] + 1)
            mx = small[0:P, 32:32 + T]
            v = [small[0:P, 44:44 + T], small[0:P, 54:54 + T]]

            def max_tile(h, u, i, t):
                if t == 0:
                    e.wait_ge(L.elb_in[u], L.since["elb_in"][u] + 16 * (i + 1))
                st.wait()
                apart(e)
                st.add(e.tensor_tensor_reduce(L.junk, L.elb[u], MB[:, t, :], 1.0, -3.0e38, ALU.add, ALU.max, mx[:, t:t + 1]))

            def max_end(h, u):
                er = L.elr[:, :, bass.ds(L.H + h, 1)].rearrange("p t o -> p (t o)")
                r = small[0:P, 64 + u * 2 * T:64 + (u + 1) * 2 * T]
                st.wait()
                st.add(e.scalar_tensor_tensor(out=mx, in0=mx, scalar=0.5 * NONE, in1=mx, op0=ALU.is_ge, op1=ALU.mult))
                st.wait()
                st.add(e.tensor_tensor(v[0], mx, er, ALU.add))
                st.wait()
                st.add(e.scalar_tensor_tensor(out=v[1], in0=v[0], scalar=SLOPE, in1=v[0], op0=ALU.mult, op1=ALU.max))
                st.wait()
                st.add(e.tensor_tensor(r[:, 0:T], er, v[1], ALU.subtract))
                e.scalar_tensor_tensor(out=r[:, T:2 * T], in0=er, scalar=SLOPE, in1=v[1], op0=ALU.mult, op1=ALU.subtract).then_inc(L.r_ready, 1)

            def weights(h, j):
                half, s = j // T, j % T
                if s == 0:
                    e.wait_ge(L.p_free, L.since["p_free"] + 2 * h + half + 1)
                e.wait_ge(L.e_ready, L.since["e_ready"] + 2 + 2 * T * h + j + 1)
                counts = AT[:, s, half * HALF:(half + 1) * HALF]
                if L.batched:
                    e.scalar_tensor_tensor(out=Ph[half][:, s, :], in0=L.ex[j % 4], scalar=2.0, in1=counts,
                                           op0=ALU.min, op1=ALU.mult).then_inc(L.p_ready, 1)
                    return
                e.tensor_tensor(L.m[j % 2], L.e[j % 2][0], L.e[j % 2][1], ALU.max).then_inc(L.e_free, 1)
                e.wait_ge(L.e_free, L.since["e_free"] + 2 + 2 * T * h + j + 1)
                e.scalar_tensor_tensor(out=Ph[half][:, s, :], in0=L.m[j % 2], scalar=2.0,
                                       in1=counts, op0=ALU.min, op1=ALU.mult).then_inc(L.p_ready, 1)

            rd = small[0:P, 110:110 + HT]

            def finish(h, half, tiles=range(HT)):
                if L.batched:
                    e.wait_ge(L.ag_ready, L.since["ag_ready"] + 2 * h + half + 1)
                    sums = banks[2 + half][0:P, 0:HT * 65].rearrange("p (t f) -> p t f", t=HT)
                    o = L.og[half][:, 0:HT * 64].rearrange("p (t f) -> p t f", t=HT)
                    st.add(e.tensor_scalar(rd.rearrange("p (t o) -> p t o", o=1), sums[:, :, 64:65], TINY, None, ALU.max))
                    st.wait()
                    st.add(e.reciprocal(rd, rd))
                    st.wait()
                    e.wait_ge(L.stored[half], L.since["stored"][half] + 16 * h)
                    st.add(e.tensor_tensor(o, sums[:, :, 0:64], rd.rearrange("p (t o) -> p t o", o=1).to_broadcast([P, HT, 64]), ALU.mult))
                    st.wait()
                    e.tensor_tensor(o, o, L.z[:, half * HT:(half + 1) * HT, h, 0:64], ALU.add).then_inc(L.out_done, 1)
                    return
                for d in tiles:
                    j = half * HT + d
                    e.wait_ge(L.ag_ready, L.since["ag_ready"] + T * h + j + 1)
                    last = banks[2 + 2 * (j % 2) + 1][0:P, 0:L.cols[1][1]]
                    den = last[:, L.cols[1][1] - 1:L.cols[1][1]]
                    st.add(e.tensor_scalar(rd[:, 0:1], den, TINY if L.add_z else 1e-16, None, ALU.max if L.add_z else ALU.add))
                    st.wait()
                    st.add(e.reciprocal(rd[:, 1:2], rd[:, 0:1]))
                    st.wait()
                    e.wait_ge(L.stored[j % 2], L.since["stored"][j % 2] + 16 * (HT * h + j // 2))
                    for c, (at, w) in enumerate(L.cols):
                        w -= c
                        src = banks[2 + 2 * (j % 2) + c][0:P, 0:w]
                        o = L.og[j % 2][:, at:at + w]
                        if L.add_z:
                            ins = e.scalar_tensor_tensor(out=o, in0=src, scalar=rd[:, 1:2], in1=L.z[:, j, at:at + w], op0=ALU.mult, op1=ALU.add)
                        else:
                            ins = e.tensor_scalar(o, src, rd[:, 1:2], None, ALU.mult)
                    ins.then_inc(L.out_done, 1)

            def add_r2(h, u, i, j):
                half, s = j // T, j % T
                if j == ADD_AT[0]:
                    e.wait_ge(L.rb2_in[u], L.since["rb2_in"][u] + 16 * (i + 1))
                e.wait_ge(L.relued, L.since["relued"] + 2 * T * h + j + 1)
                e.wait_ge(L.p_ready, L.since["p_ready"] + 2 * T * h + j + 1)
                apart(e)
                e.tensor_tensor(L.ex[j % 4], L.r2[half][0:P, s % 3, :], L.rb2[u][:, half * HALF:(half + 1) * HALF], ALU.add).then_inc(L.added, 1)

            def batched_head(h, u, i, first, more):
                for j in range(2 * T):
                    if first:
                        if j < T:
                            max_tile(1, 1, 0, j)
                            if j == T - 1:
                                max_end(1, 1)
                        else:
                            max_tile(2, 0, 1, j - T)
                    elif more and j % 2 == 0:
                        max_tile(h + 2, u, i + 1, j // 2)
                    if more and j == 2 * T - 1:
                        max_end(h + 2, u)
                    weights(h, j)
                    if j + 3 < 2 * T and (j + 3) % T in ADD_AT:
                        add_r2(h, u, i, j + 3)
                    if not first and j in (1, T + 1):
                        finish(h - 1, j // T)

            FIN = 3 if L.batched else 2 * HT
            for t in range(T):
                if L.spill and t == HT:
                    for u in range(2):
                        e.wait_ge(L.spilled[u], L.since["spilled"][u] + 16 * HT)
                    for u in range(2):
                        st.add(e.memset(L.zh[u][:, :, L.D:L.D + 1], 1.0))
                    st.wait()
                    e.engine_nop().then_inc(L.ones, 1)
                max_tile(0, 0, 0, t)
            max_end(0, 0)

            FINISH_AT = {3: [0], 7: [1], T - 1: range(2, HT)}

            def head(h, u, first, last, i):
                at = 0
                for j in range(2 * T):
                    if not last and j in MAX_STEPS:
                        max_tile(h + 1, 1 - u, i + u, at)
                        at += 1
                        if at == T:
                            max_end(h + 1, 1 - u)
                    weights(h, j)
                    before, half = (h, 0) if j >= T else (None if first else h - 1, 1)
                    if before is not None and j % T in FINISH_AT:
                        finish(before, half, FINISH_AT[j % T])

            if L.batched:
                batched_head(0, 0, 0, True, True)
                batched_head(1, 1, 0, False, True)
                with e.Fori(1, L.H // 2 - 1) as i:
                    st.enter(i - 1, 2 * (T + 4 + 2 * FIN))
                    for u in range(2):
                        batched_head(2 * i + u, u, i, False, True)
                    st.leave(L.H // 2 - 2)
                for u in range(2):
                    batched_head(L.H - 2 + u, u, L.H // 2 - 1, False, False)
                finish(L.H - 1, 0)
                finish(L.H - 1, 1)
                return
            if L.H == 1:
                head(0, 0, True, True, 0)
                finish(0, 1)
                return
            head(0, 0, True, False, 0)
            head(1, 1, False, L.H == 2, 0)
            i = L.H // 2 - 1
            head(L.H - 2, 0, False, False, i)
            head(L.H - 1, 1, False, True, i)
            finish(L.H - 1, 1)

        def moe_vector(e, st, M):
            e.wait_ge(M.c_in, 144 if M.bias else 112)

            def prep(t, u, i):
                e.wait_ge(M.x_in[u], 32 * (i + 1))
                x = M.acc[:, t, :]
                st.add(e.tensor_tensor(x, x, M.rbias, ALU.add))
                st.wait()
                e.tensor_tensor(x, x, M.rawt[u], ALU.add).then_inc(M.raw_free, 1)
                e.wait_ge(M.raw_free, 2 + t + 1)
                norm_a(e, st, x, u, M.half_prep)

            def norm(t, u, i):
                e.wait_ge(M.xt_ready, 2 * t + 1)
                e.wait_ge(M.xn_out[u], 16 * (i + 1))
                norm_b(e, st, M.xn[u], M.acc[:, t, :], u, M.mid, t + 1, M.prepped)

            prep(0, 0, 0)
            with e.Fori(0, HT - 1) as i:
                st.enter(i, 10)
                prep(2 * i + 1, 1, i)
                norm(2 * i, 0, i)
                prep(2 * i + 2, 0, i + 1)
                norm(2 * i + 1, 1, i)
                st.leave(HT - 1)
            prep(T - 1, 1, HT - 1)
            norm(T - 2, 0, HT - 1)
            norm(T - 1, 1, HT - 1)
            g, flat, col = M.g, M.gflat, M.col
            wide = lambda c: c.rearrange("p (t o) -> p t o", o=1).to_broadcast([P, T, EX])
            order = M.order.rearrange("p (o e) -> p o e", o=1).to_broadcast([P, T, EX])

            def step(ins):
                st.add(ins)
                st.wait()
            step(e.memset(M.onesq, 1.0))
            e.wait_ge(M.lg_ready, 1)
            lg = banks[2][0:P, 0:T * EX].rearrange("p (t e) -> p t e", t=T)
            step(e.tensor_reduce(col[0], lg, AX.X, ALU.max))
            e.tensor_tensor(g[0], lg, wide(col[0]), ALU.subtract).then_inc(M.exp_in, 1)
            e.wait_ge(M.exped, 1)
            step(e.tensor_reduce(col[1], g[0], AX.X, ALU.add))
            step(e.reciprocal(col[2], col[1]))
            e.tensor_tensor(g[1], g[0], wide(col[2]), ALU.mult).then_inc(M.probs, 1)
            e.wait_ge(M.probs, 1)

            def pick(p, taken):
                step(e.tensor_reduce(col[0], p, AX.X, ALU.max))
                step(e.tensor_tensor(g[2], p, wide(col[0]), ALU.is_equal))
                step(e.tensor_tensor(g[2], g[2], order, ALU.mult))
                step(e.tensor_reduce(col[1], g[2], AX.X, ALU.max))
                step(e.tensor_tensor(taken, order, wide(col[1]), ALU.is_equal))
            pick(g[1], g[3])
            step(e.scalar_tensor_tensor(out=flat[4], in0=flat[3], scalar=-2.0, in1=flat[1], op0=ALU.mult, op1=ALU.add))
            pick(g[4], g[5])
            e.tensor_tensor(g[7], g[3], g[5], ALU.add).then_inc(M.picked, 1)

            e.wait_ge(M.counts, 1)
            inside, tiles = [banks[4][0:P, j * T * EX:(j + 1) * T * EX].rearrange("p (t e) -> p t e", t=T) for j in range(2)]
            n, tile_n, end, first = M.per
            step(e.memset(g[2][:, 0, :], 0.0))
            for t in range(1, T):
                step(e.tensor_tensor(g[2][:, t, :], g[2][:, t - 1, :], tiles[:, t - 1, :], ALU.add))
            step(e.tensor_tensor(n, g[2][:, T - 1, :], tiles[:, T - 1, :], ALU.add))
            step(e.tensor_tensor(g[2], g[2], inside, ALU.add))
            most = -(-N // ST)
            above = M.above[:, 0:EX * most].rearrange("p (e k) -> p e k", e=EX)
            step(e.tensor_tensor(above, n.rearrange("p (e o) -> p e o", o=1).to_broadcast([P, EX, most]),
                                 M.steps[:, 0:most].rearrange("p (o k) -> p o k", o=1).to_broadcast([P, EX, most]), ALU.is_gt))
            step(e.tensor_reduce(tile_n, above, AX.X, ALU.add))
            step(e.tensor_scalar(tile_n, tile_n, 1.0, None, ALU.max))
            step(e.tensor_copy(end[:, 0:1], tile_n[:, 0:1]))
            for x in range(1, EX):
                step(e.tensor_tensor(end[:, x:x + 1], end[:, x - 1:x], tile_n[:, x:x + 1], ALU.add))
            step(e.tensor_tensor(first, end, tile_n, ALU.subtract))
            step(e.tensor_copy(M.span[0:1, 0:EX], first[0:1, :]))
            step(e.tensor_copy(M.span[0:1, EX:2 * EX], end[0:1, :]))
            step(e.tensor_scalar(first, first, float(ST), None, ALU.mult))
            step(e.tensor_tensor(g[2], g[2], first.rearrange("p (o e) -> p o e", o=1).to_broadcast([P, T, EX]), ALU.add))
            for k, taken in enumerate((g[3], g[5])):
                step(e.tensor_tensor(g[4], g[2], taken, ALU.mult))
                step(e.tensor_reduce(M.slot[:, k * T:(k + 1) * T], g[4], AX.X, ALU.add))
            wide_s = lambda a, n: a.rearrange("p (s o) -> p s o", o=1).to_broadcast([P, 2 * T, n])
            wide_k = lambda a, n: a.rearrange("p (o k) -> p o k", o=1).to_broadcast([P, 2 * T, n])
            above = M.above[:, 0:2 * T * MAX_TILES].rearrange("p (s k) -> p s k", s=2 * T)
            step(e.tensor_tensor(above, wide_s(M.slot, MAX_TILES), wide_k(M.steps[:, 1:1 + MAX_TILES], MAX_TILES), ALU.is_ge))
            step(e.tensor_reduce(M.tile, above, AX.X, ALU.add))
            step(e.tensor_scalar(M.tile, M.tile, float(ST), None, ALU.mult))
            step(e.tensor_tensor(M.row, M.slot, M.tile, ALU.subtract))
            step(e.tensor_tensor(M.in_tile, wide_s(M.tile, LIST), wide_k(M.steps, LIST), ALU.is_equal))
            step(e.tensor_tensor(M.in_tile, M.in_tile, wide_s(M.node, LIST), ALU.mult))
            for u in range(2):
                e.wait_ge(M.xn_out[u], 16 + 16 * HT)
            e.tensor_tensor(M.in_row, wide_s(M.row, ST), wide_k(M.lanes, ST), ALU.is_equal).then_inc(M.placed, 1)
            step(e.tensor_copy(M.slot_i, M.slot))
            e.wait_ge(M.list_ready, 1)
            e.tensor_copy(M.list, banks[5][:, 0:LIST]).then_inc(M.listed, 1)

            if M.balanced:
                step(e.tensor_tensor(g[4], g[7], g[1], ALU.mult))
                e.wait_ge(M.imp_ready, 1)
                step(e.tensor_reduce(M.run, banks[3][0:P, 0:T * EX].rearrange("p (t e) -> p e t", t=T), AX.X, ALU.add))
                step(e.tensor_scalar(M.run, M.run, -1.0, DECAY_STEP, ALU.add, ALU.mult))
                step(e.tensor_scalar(M.run, M.run, 1.0, BAL_EPS, ALU.add, ALU.add))
                step(e.reciprocal(M.run, M.run))
                step(e.tensor_tensor(g[0], g[4], M.run.rearrange("p (o e) -> p o e", o=1).to_broadcast([P, T, EX]), ALU.mult))
                step(e.tensor_reduce(col[0], g[0], AX.X, ALU.add))
                step(e.reciprocal(col[1], col[0]))
                e.tensor_tensor(g[6], g[0], wide(col[1]), ALU.mult).then_inc(M.gates, 1)
            else:
                e.tensor_tensor(g[6], g[7], g[1], ALU.mult).then_inc(M.gates, 1)
            e.wait_ge(M.gates, 1)
            for k, taken in enumerate((g[3], g[5])):
                step(e.tensor_tensor(g[4], g[6], taken, ALU.mult))
                step(e.tensor_reduce(M.gate[k], g[4], AX.X, ALU.add))

            e.wait_ge(M.placed, 1)
            with e.Fori(0, all_tiles(e, M)) as i:
                e.wait_ge(M.y_ready, i + 1)
                e.wait_ge(M.y_out, 16 * i + 16)
                apart(e)
                e.tensor_copy(M.y[:, 0:C // 2], banks[2][:, 0:C // 2])
                e.tensor_copy(M.y[:, C // 2:C], banks[3][:, 0:C // 2]).then_inc(M.y_sb, 1)
            for t in range(T):
                if M.bias:
                    e.wait_ge(M.gb_ready, t + 1)
                    for c in range(2):
                        a = M.acc[:, t, c * (C // 2):(c + 1) * (C // 2)]
                        ins = e.tensor_tensor(a, a, banks[4 + 2 * (t % 2) + c][0:P, 0:C // 2], ALU.add)
                    ins.then_inc(M.gb_free, 1)
                    e.wait_ge(M.gb_free, t + 1)
                e.wait_ge(M.yg_in[t % 4], 32 * (t // 4 + 1))
                a = M.acc[:, t, :]
                for k in range(2):
                    ins = e.scalar_tensor_tensor(out=a, in0=M.yg[t % 4][k], scalar=M.gate[k][:, t:t + 1], in1=a, op0=ALU.mult, op1=ALU.add)
                    if k == 0:
                        step(ins)
                ins.then_inc(M.y_done, 1)

        @block.vector
        def _(e):
            st = Step(e, v_step)
            graph_vector(e, st)
            e.wait_ge(gs["at_sb"], 3 * T)
            e.wait_ge(gs["bias"], T)
            for n in range(3):
                gat_vector(e, st, layers[n])
            add_loops(e)
            moe_vector(e, st, moes[0])
            e.wait_ge(gs["loops"], T)
            for n in range(3, 5):
                gat_vector(e, st, layers[n])
            moe_vector(e, st, moes[1])


_KEEP = ["x", "src", "dst", "L0_gnn_W0", "L0_gnn_al0", "L0_gnn_ar0", "L0_gnn_b0", "L0_gnn_W1", "L0_gnn_al1",
         "L0_gnn_ar1", "L0_gnn_b1", "L0_gnn_W2", "L0_gnn_al2", "L0_gnn_ar2", "L0_gnn_b2", "L1_gnn_W1",
         "L1_gnn_a1_src", "L1_gnn_a1_dst", "L1_gnn_b1", "L1_gnn_W2", "L1_gnn_a2_src", "L1_gnn_a2_dst",
         "L1_gnn_b2", "L1_ffn_Wg", "L1_ffn_W1", "L1_ffn_W2", "L1_ffn_b2"]


def kernel(**inputs):
    import concourse.bacc as bacc
    from concourse.bass_utils import run_bass_kernel_spmd as run

    a = {n: np.ascontiguousarray(inputs[n]) for n in _KEEP}
    a["L0_router"] = np.ascontiguousarray(np.asarray(inputs["L0_ffn_router_w"]).T)
    a["L0_w1"] = np.ascontiguousarray(np.asarray(inputs["L0_ffn_w1"]).transpose(0, 2, 1))
    a["L0_w2"] = np.ascontiguousarray(np.asarray(inputs["L0_ffn_w2"]).transpose(0, 2, 1))
    a["L1_b1"] = np.ascontiguousarray(np.asarray(inputs["L1_ffn_b1"]).reshape(EX, -1, 128).transpose(2, 0, 1))
    a["ident"] = np.eye(128, dtype=np.float32)
    a["spread"] = np.concatenate([np.eye(P), np.ones((1, P))]).astype(np.float32)
    a["nodes"] = np.arange(N, dtype=np.int16)
    a["order"] = np.arange(EX, 0, -1).astype(np.float32)
    a["lanes"] = np.arange(ST).astype(np.float32)
    a["no_outputs"] = np.zeros((ST, C), np.float32)
    a["steps"] = (ST * np.arange(LIST)).astype(np.float32)
    a["node_ids"] = np.ascontiguousarray(np.tile(np.arange(N).reshape(T, P).T, (1, 2))).astype(np.float32)
    a["before"] = np.triu(np.ones((P, P), np.float32), 1)
    a["group_limits"] = np.stack([GROUPS - np.arange(GROUPS), 1 + np.arange(GROUPS)], 1).astype(np.float32)

    nc = bacc.Bacc("TRN2", target_bir_lowering=False, num_devices=1)
    aps = {n: nc.dram_tensor(f"in_{n}", v.shape, mybir.dt.from_np(v.dtype), kind="ExternalInput").ap() for n, v in a.items()}
    out = nc.dram_tensor("out_x", (N, C), F32, kind="ExternalOutput").ap()
    graph_transformer(nc, aps, out)
    r = run(nc, [{f"in_{n}": v for n, v in a.items()}], core_ids=[0])
    return r.results[0]["out_x"]
```
